# Optimizing a Trainium2 kernel written in Bass

```python
import numpy as np
import jax
import jax.numpy as jnp

def _softmax(x, axis=-1):
    return jax.nn.softmax(x, axis=axis)

def _gelu(x):
    return jax.nn.gelu(x, approximate=True)

def _silu(x):
    return jax.nn.silu(x)

def _sigmoid(x):
    return jax.nn.sigmoid(x)

def _layernorm(x, axis=-1, eps=1e-05):
    m = jnp.mean(x, axis=axis, keepdims=True)
    v = jnp.var(x, axis=axis, keepdims=True)
    return (x - m) / jnp.sqrt(v + eps)

def _scatter_add(tgt, idx, src, axis=0):
    return tgt.at[idx].add(src)

def _segment_sum(src, seg, n):
    return jax.ops.segment_sum(src, seg, n)
kernel_name = 'mk_gnn_resnorm_d4_gnn_r64_dab72f'

def setup_inputs(seed: int=0):
    np.random.seed(seed)
    _w = jnp.asarray

    def _rec_inputs():
        import jax
        import jax.numpy as jnp
        _gk = jax.random.key(seed)
        x = -0.0001006 + 1 * jax.random.normal(jax.random.fold_in(_gk, 1), (100000, 96), jnp.float32)
        src = jax.random.randint(jax.random.fold_in(_gk, 2), (50000,), 0, 100000, jnp.int32)
        dst = jax.random.randint(jax.random.fold_in(_gk, 3), (50000,), 0, 100000, jnp.int32)
        _o = jnp.argsort(dst, stable=True)
        src = src[_o]
        dst = dst[_o]
        edge_attr_4 = 0.000714719 + 1.00021 * jax.random.normal(jax.random.fold_in(_gk, 12), (50000, 4), jnp.float32)
        return (x, src, dst, edge_attr_4)
    x, src, dst, edge_attr_4 = _rec_inputs()

    def _L0_gnn_setup():
        import jax, jax.numpy as jnp
        import numpy as np
        N_NODES = 50000
        N_EDGES = 12500
        IN_DIM = 96
        HID = 96

        def _gcn_conv(x, src, dst, norm, W, b, n_nodes):
            xw = x @ W
            msg = xw[src] * norm[:, None]
            agg = jax.ops.segment_sum(msg, dst, num_segments=n_nodes)
            return agg + b
        key = jax.random.key(seed)
        k1, k2, k3, k4 = jax.random.split(key, 4)
        x = jax.random.normal(k1, (N_NODES, IN_DIM), dtype=jnp.float32)
        edge_index = jax.random.randint(k2, (2, N_EDGES), 0, N_NODES, dtype=jnp.int64)
        s1 = 1.0 / np.sqrt(IN_DIM)
        s2 = 1.0 / np.sqrt(HID)
        W1 = jax.random.normal(k3, (IN_DIM, HID), dtype=jnp.float32) * s1
        b1 = jnp.zeros((HID,), dtype=jnp.float32)
        W2 = jax.random.normal(k4, (HID, HID), dtype=jnp.float32) * s2
        b2 = jnp.zeros((HID,), dtype=jnp.float32)
        return {'x': x, 'edge_index': edge_index, 'W1': W1, 'b1': b1, 'W2': W2, 'b2': b2}
    _L0_gnn_all = _L0_gnn_setup()
    _L0_gnn_in = {k: v for k, v in _L0_gnn_all.items() if k in ('W1', 'b1', 'W2', 'b2')}
    del _L0_gnn_all

    def _L1_gnn_setup():
        import jax, jax.numpy as jnp
        import numpy as np
        N_NODES = 50000
        N_EDGES = 12500
        D = 96
        DEPTH = 2
        key = jax.random.key(seed)
        ks = jax.random.split(key, 8)
        scale = 1.0 / np.sqrt(D)
        x = jax.random.normal(ks[0], (N_NODES, D), dtype=jnp.float32)
        W0 = jax.random.normal(ks[1], (DEPTH, D, D), dtype=jnp.float32) * scale
        b0 = jnp.zeros((DEPTH, D), dtype=jnp.float32)
        W1 = jax.random.normal(ks[2], (DEPTH, D, D), dtype=jnp.float32) * scale
        b1 = jnp.zeros((DEPTH, D), dtype=jnp.float32)
        W2 = jax.random.normal(ks[3], (DEPTH, 2 * D, D), dtype=jnp.float32) * (1.0 / np.sqrt(2 * D))
        b2 = jnp.zeros((DEPTH, D), dtype=jnp.float32)
        edge_src = jax.random.randint(ks[4], (N_EDGES,), 0, N_NODES, dtype=jnp.int64 if jax.config.jax_enable_x64 else jnp.int32)
        edge_dst = jnp.sort(jax.random.randint(ks[5], (N_EDGES,), 0, N_NODES, dtype=jnp.int64 if jax.config.jax_enable_x64 else jnp.int32))
        return {'x': x, 'W0': W0, 'b0': b0, 'W1': W1, 'b1': b1, 'W2': W2, 'b2': b2, 'edge_src': edge_src, 'edge_dst': edge_dst}
    _L1_gnn_all = _L1_gnn_setup()
    _L1_gnn_in = {k: v for k, v in _L1_gnn_all.items() if k in ('W0', 'b0', 'W1', 'b1', 'W2', 'b2')}
    del _L1_gnn_all

    def _L2_gnn_setup():
        import jax, jax.numpy as jnp
        import numpy as np
        N_NODES = 50000
        N_EDGES = 12500
        DIM = 96
        HEADS = 4
        LAYERS = 3
        NEG_SLOPE = 0.2

        def _gat_layer(x, src, dst, W, a_src, a_dst, b):
            N = x.shape[0]
            H, C = a_src.shape
            h = (x @ W).reshape(N, H, C)
            alpha_s = jnp.einsum('nhc,hc->nh', h, a_src)
            alpha_d = jnp.einsum('nhc,hc->nh', h, a_dst)
            e = jax.nn.leaky_relu(alpha_s[src] + alpha_d[dst], NEG_SLOPE)
            m = jax.ops.segment_max(e, dst, num_segments=N)
            m = jnp.where(jnp.isfinite(m), m, 0.0)
            ex = jnp.exp(e - m[dst])
            den = jax.ops.segment_sum(ex, dst, num_segments=N)
            alpha = ex / (den[dst] + 1e-16)
            msg = h[src] * alpha[:, :, None]
            out = jax.ops.segment_sum(msg, dst, num_segments=N)
            return out.reshape(N, H * C) + b
        key = jax.random.key(seed)
        ks = jax.random.split(key, 6)
        C = DIM // HEADS
        x = jax.random.normal(ks[0], (N_NODES, DIM), dtype=jnp.float32)
        edge_index = jax.random.randint(ks[1], (2, N_EDGES), 0, N_NODES, dtype=jnp.int32)
        W = jax.random.normal(ks[2], (LAYERS, DIM, DIM), dtype=jnp.float32) * (1.0 / np.sqrt(DIM))
        att_src = jax.random.normal(ks[3], (LAYERS, HEADS, C), dtype=jnp.float32) * (1.0 / np.sqrt(C))
        att_dst = jax.random.normal(ks[4], (LAYERS, HEADS, C), dtype=jnp.float32) * (1.0 / np.sqrt(C))
        bias = jnp.zeros((LAYERS, DIM), dtype=jnp.float32)
        return {'x': x, 'edge_index': edge_index, 'W': W, 'att_src': att_src, 'att_dst': att_dst, 'bias': bias}
    _L2_gnn_all = _L2_gnn_setup()
    _L2_gnn_in = {k: v for k, v in _L2_gnn_all.items() if k in ('W', 'att_src', 'att_dst', 'bias')}
    del _L2_gnn_all

    def _L3_gnn_setup():
        import jax, jax.numpy as jnp
        import numpy as np
        EPS = 1e-05

        def _mlp(h, W, b, gamma, beta):
            h = jax.nn.relu(h @ W + b)
            mu = jnp.mean(h, axis=0)
            var = jnp.mean(jnp.square(h - mu), axis=0)
            return gamma * (h - mu) * jax.lax.rsqrt(var + EPS) + beta
        key = jax.random.key(seed)
        ks = jax.random.split(key, 10)
        N, E, C_in, C_out, E_dim = (50000, 12500, 96, 96, 4)
        x = jax.random.normal(ks[0], (N, C_in), dtype=jnp.float32)
        edge_index = jax.random.randint(ks[1], (2, E), 0, N, dtype=jnp.int64)
        edge_attr = jax.random.normal(ks[2], (E, E_dim), dtype=jnp.float32)
        s = lambda fan_in: 1.0 / np.sqrt(fan_in)
        W_node = jax.random.uniform(ks[3], (C_in, C_out), jnp.float32, -s(C_in), s(C_in))
        b_node = jnp.zeros((C_out,), jnp.float32)
        g_node = jnp.ones((C_out,), jnp.float32)
        beta_node = jnp.zeros((C_out,), jnp.float32)
        W_edge = jax.random.uniform(ks[4], (E_dim, C_out), jnp.float32, -s(E_dim), s(E_dim))
        b_edge = jnp.zeros((C_out,), jnp.float32)
        g_edge = jnp.ones((C_out,), jnp.float32)
        beta_edge = jnp.zeros((C_out,), jnp.float32)
        M_in = 2 * C_in + C_out
        W_msg = jax.random.uniform(ks[5], (M_in, C_out), jnp.float32, -s(M_in), s(M_in))
        b_msg = jnp.zeros((C_out,), jnp.float32)
        g_msg = jnp.ones((C_out,), jnp.float32)
        beta_msg = jnp.zeros((C_out,), jnp.float32)
        return dict(x=x, edge_index=edge_index, edge_attr=edge_attr, W_node=W_node, b_node=b_node, g_node=g_node, beta_node=beta_node, W_edge=W_edge, b_edge=b_edge, g_edge=g_edge, beta_edge=beta_edge, W_msg=W_msg, b_msg=b_msg, g_msg=g_msg, beta_msg=beta_msg)
    _L3_gnn_all = _L3_gnn_setup()
    _L3_gnn_in = {k: v for k, v in _L3_gnn_all.items() if k in ('W_node', 'b_node', 'g_node', 'beta_node', 'W_edge', 'b_edge', 'g_edge', 'beta_edge', 'W_msg', 'b_msg', 'g_msg', 'beta_msg')}
    del _L3_gnn_all
    return {'x': x, 'src': src, 'dst': dst, 'edge_attr_4': edge_attr_4, 'L0_gnn_W1': _L0_gnn_in['W1'], 'L0_gnn_b1': _L0_gnn_in['b1'], 'L0_gnn_W2': _L0_gnn_in['W2'], 'L0_gnn_b2': _L0_gnn_in['b2'], 'L1_gnn_W0': _L1_gnn_in['W0'], 'L1_gnn_b0': _L1_gnn_in['b0'], 'L1_gnn_W1': _L1_gnn_in['W1'], 'L1_gnn_b1': _L1_gnn_in['b1'], 'L1_gnn_W2': _L1_gnn_in['W2'], 'L1_gnn_b2': _L1_gnn_in['b2'], 'L2_gnn_W': _L2_gnn_in['W'], 'L2_gnn_att_src': _L2_gnn_in['att_src'], 'L2_gnn_att_dst': _L2_gnn_in['att_dst'], 'L2_gnn_bias': _L2_gnn_in['bias'], 'L3_gnn_W_node': _L3_gnn_in['W_node'], 'L3_gnn_b_node': _L3_gnn_in['b_node'], 'L3_gnn_g_node': _L3_gnn_in['g_node'], 'L3_gnn_beta_node': _L3_gnn_in['beta_node'], 'L3_gnn_W_edge': _L3_gnn_in['W_edge'], 'L3_gnn_b_edge': _L3_gnn_in['b_edge'], 'L3_gnn_g_edge': _L3_gnn_in['g_edge'], 'L3_gnn_beta_edge': _L3_gnn_in['beta_edge'], 'L3_gnn_W_msg': _L3_gnn_in['W_msg'], 'L3_gnn_b_msg': _L3_gnn_in['b_msg'], 'L3_gnn_g_msg': _L3_gnn_in['g_msg'], 'L3_gnn_beta_msg': _L3_gnn_in['beta_msg']}

def reference(x, src, dst, edge_attr_4, L0_gnn_W1, L0_gnn_b1, L0_gnn_W2, L0_gnn_b2, L1_gnn_W0, L1_gnn_b0, L1_gnn_W1, L1_gnn_b1, L1_gnn_W2, L1_gnn_b2, L2_gnn_W, L2_gnn_att_src, L2_gnn_att_dst, L2_gnn_bias, L3_gnn_W_node, L3_gnn_b_node, L3_gnn_g_node, L3_gnn_beta_node, L3_gnn_W_edge, L3_gnn_b_edge, L3_gnn_g_edge, L3_gnn_beta_edge, L3_gnn_W_msg, L3_gnn_b_msg, L3_gnn_g_msg, L3_gnn_beta_msg):
    import jax
    import jax.numpy as jnp

    def _L0_gnn_ref(x, edge_index, W1, b1, W2, b2):
        import jax, jax.numpy as jnp
        import numpy as np
        N_NODES = 50000
        N_EDGES = 12500
        IN_DIM = 96
        HID = 96

        def _gcn_conv(x, src, dst, norm, W, b, n_nodes):
            xw = x @ W
            msg = xw[src] * norm[:, None]
            agg = jax.ops.segment_sum(msg, dst, num_segments=n_nodes)
            return agg + b
        n_nodes = x.shape[0]
        loops = jnp.arange(n_nodes, dtype=edge_index.dtype)
        src = jnp.concatenate([edge_index[0], loops])
        dst = jnp.concatenate([edge_index[1], loops])
        deg = jax.ops.segment_sum(jnp.ones(dst.shape, dtype=x.dtype), dst, num_segments=n_nodes)
        dinv = jnp.where(deg > 0, jax.lax.rsqrt(deg), 0.0)
        norm = dinv[src] * dinv[dst]
        h = jax.nn.relu(_gcn_conv(x, src, dst, norm, W1, b1, n_nodes))
        h = jax.nn.relu(_gcn_conv(h, src, dst, norm, W2, b2, n_nodes))
        return h

    def _L1_gnn_ref(x, W0, b0, W1, b1, W2, b2, edge_src, edge_dst):
        import jax, jax.numpy as jnp
        import numpy as np
        N_NODES = 50000
        N_EDGES = 12500
        D = 96
        DEPTH = 2
        n = x.shape[0]
        depth = W0.shape[0]
        for i in range(depth):
            h_self = x @ W1[i] + b1[i]
            h_nb = x @ W0[i] + b0[i]
            agg = jax.ops.segment_sum(h_nb[edge_src], edge_dst, num_segments=n)
            x = jnp.concatenate([h_self, agg], axis=-1) @ W2[i] + b2[i]
            x = x / jnp.std(x, axis=-1, ddof=1, keepdims=True)
        return x

    def _L2_gnn_ref(x, edge_index, W, att_src, att_dst, bias):
        import jax, jax.numpy as jnp
        import numpy as np
        N_NODES = 50000
        N_EDGES = 12500
        DIM = 96
        HEADS = 4
        LAYERS = 3
        NEG_SLOPE = 0.2

        def _gat_layer(x, src, dst, W, a_src, a_dst, b):
            N = x.shape[0]
            H, C = a_src.shape
            h = (x @ W).reshape(N, H, C)
            alpha_s = jnp.einsum('nhc,hc->nh', h, a_src)
            alpha_d = jnp.einsum('nhc,hc->nh', h, a_dst)
            e = jax.nn.leaky_relu(alpha_s[src] + alpha_d[dst], NEG_SLOPE)
            m = jax.ops.segment_max(e, dst, num_segments=N)
            m = jnp.where(jnp.isfinite(m), m, 0.0)
            ex = jnp.exp(e - m[dst])
            den = jax.ops.segment_sum(ex, dst, num_segments=N)
            alpha = ex / (den[dst] + 1e-16)
            msg = h[src] * alpha[:, :, None]
            out = jax.ops.segment_sum(msg, dst, num_segments=N)
            return out.reshape(N, H * C) + b
        src = edge_index[0]
        dst = edge_index[1]
        for l in range(W.shape[0]):
            x = jax.nn.relu(_gat_layer(x, src, dst, W[l], att_src[l], att_dst[l], bias[l]))
        return x

    def _L3_gnn_ref(x, edge_index, edge_attr, W_node, b_node, g_node, beta_node, W_edge, b_edge, g_edge, beta_edge, W_msg, b_msg, g_msg, beta_msg):
        import jax, jax.numpy as jnp
        import numpy as np
        EPS = 1e-05

        def _mlp(h, W, b, gamma, beta):
            h = jax.nn.relu(h @ W + b)
            mu = jnp.mean(h, axis=0)
            var = jnp.mean(jnp.square(h - mu), axis=0)
            return gamma * (h - mu) * jax.lax.rsqrt(var + EPS) + beta
        node_feat = _mlp(x, W_node, b_node, g_node, beta_node)
        edge_feat = _mlp(edge_attr, W_edge, b_edge, g_edge, beta_edge)
        row, col = (edge_index[0], edge_index[1])
        message = jnp.concatenate([x[row], x[col], edge_feat], axis=1)
        message = _mlp(message, W_msg, b_msg, g_msg, beta_msg)
        agg = jax.ops.segment_sum(message, col, num_segments=node_feat.shape[0])
        return agg + node_feat
    edge_index = jnp.stack([src, dst])
    x = _layernorm(x + _L0_gnn_ref(x, edge_index, L0_gnn_W1, L0_gnn_b1, L0_gnn_W2, L0_gnn_b2), axis=-1)
    x = _layernorm(x + _L1_gnn_ref(x, L1_gnn_W0, L1_gnn_b0, L1_gnn_W1, L1_gnn_b1, L1_gnn_W2, L1_gnn_b2, src, dst), axis=-1)
    x = _layernorm(x + _L2_gnn_ref(x, edge_index, L2_gnn_W, L2_gnn_att_src, L2_gnn_att_dst, L2_gnn_bias), axis=-1)
    x = _layernorm(x + _L3_gnn_ref(x, edge_index, edge_attr_4, L3_gnn_W_node, L3_gnn_b_node, L3_gnn_g_node, L3_gnn_beta_node, L3_gnn_W_edge, L3_gnn_b_edge, L3_gnn_g_edge, L3_gnn_beta_edge, L3_gnn_W_msg, L3_gnn_b_msg, L3_gnn_g_msg, L3_gnn_beta_msg), axis=-1)
    return x

_drawn_inputs = setup_inputs


def setup_inputs(seed=0):
    import zlib

    import numpy as np

    out = dict(_drawn_inputs(seed))
    spreads = {'L0_gnn_b1': (0.0, 0.1),
     'L0_gnn_b2': (0.0, 0.1),
     'L1_gnn_b0': (0.0, 0.1),
     'L1_gnn_b1': (0.0, 0.1),
     'L1_gnn_b2': (0.0, 0.1),
     'L2_gnn_bias': (0.0, 0.1),
     'L3_gnn_b_node': (0.0, 0.1),
     'L3_gnn_g_node': (1.0, 0.2),
     'L3_gnn_beta_node': (0.0, 0.1),
     'L3_gnn_b_edge': (0.0, 0.1),
     'L3_gnn_g_edge': (1.0, 0.2),
     'L3_gnn_beta_edge': (0.0, 0.645),
     'L3_gnn_b_msg': (0.0, 0.1),
     'L3_gnn_g_msg': (1.0, 0.2),
     'L3_gnn_beta_msg': (0.0, 0.1)}
    factors = {'L2_gnn_att_src': 5.597, 'L2_gnn_att_dst': 8.0}
    for name, (base, spread) in spreads.items():
        noise = np.random.default_rng([zlib.crc32(name.encode()), seed]).standard_normal(out[name].shape)
        drawn = base * np.exp(spread * noise) if base else spread * noise
        out[name] = jnp.asarray(drawn.astype(out[name].dtype))
    for name, factor in factors.items():
        out[name] = (out[name] * factor).astype(out[name].dtype)
    return out
```

```python
import numpy as np
import concourse.bass as bass
from concourse import mybir
from contextlib import ExitStack

F32, I32 = mybir.dt.float32, mybir.dt.int32
ALU, ACT, AX = mybir.AluOpType, mybir.ActivationFunctionType, mybir.AxisListType

P = 128
N, E, D = 100000, 50000, 96
HEADS, CH = 4, 24
ATT = D + HEADS
ATT_ALL = ATT + HEADS
T = -(-E // P)
TH = T + 1
LAST = E - (P - 1) * T
J = 4
SLOTS = 2
STEPS = TH // (J * SLOTS)
assert STEPS * J * SLOTS == TH
FAR = 1 << 20
GROUP = P * J
DENSE_FULL = N // GROUP
REST = (N - DENSE_FULL * GROUP) // J
DENSE_STEPS = (DENSE_FULL + 1) // SLOTS
assert DENSE_STEPS * SLOTS == DENSE_FULL + 1 and REST * J + DENSE_FULL * GROUP == N
EPS = 1e-5
HUGE = 1.0e30


def steps(eng, count, body):
    body(0)
    body(1)
    with eng.Fori(2, count - 1) as step:
        body(step)
    body(count - 1)


def counter(eng, step):
    known = {}

    def through(n, back=0):
        if isinstance(step, int):
            return n * (step + 1 - back)
        if (n, back) not in known:
            known[n, back] = eng.to_reg(step * n + n * (1 - back))
        return known[n, back]
    return through


def wait(eng, sem, value):
    if not (isinstance(value, int) and value <= 0):
        eng.wait_ge(sem, value)


def wait_apart(eng, entered, *waits):
    eng.wait_ge(entered, 1)
    for sem, value in waits:
        wait(eng, sem, value)


def cols(step, slot, count=J, skip=0):
    return bass.ds(step * (J * SLOTS) + (J * slot + skip), count)


def over_rows(column_tile, width):
    return column_tile.unsqueeze(2).to_broadcast([column_tile.shape[0], column_tile.shape[1], width])


def turns(eng, front, back):
    def body(step):
        first = isinstance(step, int) and step == 0
        front(step, 0)
        if not first:
            back(step - 1, 1)
        front(step, 1)
        back(step, 0)
    steps(eng, STEPS, body)
    back(STEPS - 1, 1)



class Phase:

    def __init__(self, nc, name):
        self.nc, self.name, self.stack, self.sems = nc, name, ExitStack(), []
        self.entered = self.sem("entered")

    def sb(self, name, shape, dt=F32):
        return self.stack.enter_context(self.nc.sbuf_tensor(f"{self.name}_{name}", shape, dt))

    def ps(self, name, shape=(P, 512)):
        return self.stack.enter_context(self.nc.psum_tensor(f"{self.name}_{name}", list(shape), F32))

    def sem(self, name):
        s = self.nc.alloc_semaphore(f"{self.name}_{name}")
        self.sems.append(s)
        return s

    def pair(self, make, name, *args):
        return [make(f"{name}{u}", *args) for u in range(SLOTS)]

    def close(self):
        self.stack.close()
        self.nc.clear_and_free_semaphores(self.sems)
        self.nc.all_engine_barrier()


def prepare(nc, a, k):
    ph = Phase(nc, "prep")
    dst_i = ph.sb("dst_i", [P, T], I32)
    prev_i, next_i = ph.sb("prev_i", [P, 1], I32), ph.sb("next_i", [P, 1], I32)
    blank = ph.sb("blank", [P, ATT])
    dst, attr = ph.sb("dst", [P, T]), ph.sb("attr", [P, T, 4])
    prev_tail, next_head = ph.sb("prev_tail", [P, 1]), ph.sb("next_head", [P, 1])
    is_end, valid, tmp = ph.sb("is_end", [P, T]), ph.sb("valid", [P, T]), ph.sb("tmp", [P, T])
    linked, head_ends, head_len = ph.sb("linked", [P, 1]), ph.sb("head_ends", [P, 1]), ph.sb("head_len", [P, 1])
    ones = ph.sb("ones", [P, T])
    row_base = ph.sb("row_base", [P, 1])
    wide = ph.sb("wide", [P, 2, P])
    head_of, tail_of = ph.sb("head_of", [P, P]), ph.sb("tail_of", [P, P])
    later, earlier = ph.sb("later", [P, P]), ph.sb("earlier", [P, P])
    head_out = ph.sb("head_out", [P, 1])
    w1b = ph.sb("w1b", [D + 1, 2, D])
    w0b = ph.sb("w0b", [D + 1, 2, D])
    w2 = ph.sb("w2", [D, 2, 2, D])
    b2 = ph.sb("b2", [1, 2, D])
    bias_at = ph.sb("bias_at", [1, D + 1])
    w_gat = ph.sb("w_gat", [D, 3, D])
    att = ph.sb("att", [D, 3, 2 * HEADS])
    turned = ph.sb("turned", [D, 7, D + 1])
    ps_a, ps_b, ps_c, ps_d = (ph.ps(f"ps{n}") for n in range(4))
    ps_w = [ph.ps("psw0"), ph.ps("psw1")]

    cleared, loaded, masks = ph.sem("cleared"), ph.sem("loaded"), ph.sem("masks")
    link, broad, spread, counted, carried = (ph.sem(n) for n in ("link", "broad", "spread", "counted", "carried"))
    root_in, root_out = ph.sem("root_in"), ph.sem("root_out")
    w_turn, w_copied, w_made, w_kept = (ph.sem(n) for n in ("w_turn", "w_copied", "w_made", "w_kept"))
    loads = [0]

    with nc.Block() as block:
        @block.sync
        def _(sp):
            def load(out, in_):
                with nc.allow_non_contiguous_dma(reason="a few columns of weights and indices"):
                    sp.dma_start(out, in_).then_inc(loaded, 16)
                loads[0] += 16

            sp.wait_ge(cleared, 1)
            load(k.l_acc[:, T, :], blank[:, 0:D])
            load(k.l_acc100[:, T, :], blank[:, :])
            d = a["dst"]
            load(dst_i[0:P - 1, :], d[0:(P - 1) * T].rearrange("(p t) -> p t", t=T))
            load(dst_i[P - 1:P, 0:LAST], d[(P - 1) * T:E].unsqueeze(0))
            load(k.src_idx[0:P - 1, 0:T], a["src"][0:(P - 1) * T].rearrange("(p t) -> p t", t=T))
            load(k.src_idx[P - 1:P, 0:LAST], a["src"][(P - 1) * T:E].unsqueeze(0))
            load(prev_i[1:P, :], d[0:(P - 1) * T].rearrange("(p t) -> p t", t=T)[:, T - 1:T])
            load(next_i[0:P - 2, :], d[T:(P - 1) * T].rearrange("(p t) -> p t", t=T)[:, 0:1])
            load(next_i[P - 2:P - 1, :], d[(P - 1) * T:(P - 1) * T + 1].unsqueeze(0))
            e = a["edge_attr_4"]
            load(attr[0:P - 1, :, :], e[0:(P - 1) * T, :].rearrange("(p t) c -> p t c", t=T))
            load(attr[P - 1:P, 0:LAST, :], e[(P - 1) * T:E, :].unsqueeze(0))
            for n, name in enumerate(("1", "2")):
                load(k.w_gcn[n][0:D, :], a[f"L0_gnn_W{name}"])
                load(k.w_gcn[n][D:D + 1, :], a[f"L0_gnn_b{name}"].unsqueeze(0))
            for i in range(2):
                load(w1b[0:D, i, :], a["L1_gnn_W1"][i])
                load(w1b[D:D + 1, i, :], a["L1_gnn_b1"][i:i + 1, :])
                load(w0b[0:D, i, :], a["L1_gnn_W0"][i])
                load(w0b[D:D + 1, i, :], a["L1_gnn_b0"][i:i + 1, :])
                load(w2[:, i, :, :], a["L1_gnn_W2"][i].rearrange("(s c) n -> c s n", c=D))
                load(b2[0:1, i, :], a["L1_gnn_b2"][i:i + 1, :])
            for i in range(3):
                load(w_gat[:, i, :], a["L2_gnn_W"][i])
                for s, name in enumerate(("L2_gnn_att_src", "L2_gnn_att_dst")):
                    for h in range(HEADS):
                        load(att[h * CH:(h + 1) * CH, i, HEADS * s + h:HEADS * s + h + 1],
                             a[name][i, h:h + 1, :].rearrange("a c -> c a"))
                load(k.gat_bias[:, i:i + 1], a["L2_gnn_bias"][i:i + 1, :].rearrange("a c -> c a"))
            load(k.gat_bias_row[:, :], a["L2_gnn_bias"][2:3, :].to_broadcast([P, D]))
            load(k.w_node[0:D, :], a["L3_gnn_W_node"])
            load(k.w_node[D:D + 1, :], a["L3_gnn_b_node"].unsqueeze(0))
            load(k.w_edge[0:4, :], a["L3_gnn_W_edge"])
            load(k.w_edge[4:5, :], a["L3_gnn_b_edge"].unsqueeze(0))
            load(k.w_msg[:, :, :], a["L3_gnn_W_msg"].rearrange("(s c) n -> c s n", c=D))
            for n, name in enumerate(("L3_gnn_g_node", "L3_gnn_beta_node", "L3_gnn_g_edge", "L3_gnn_beta_edge",
                                      "L3_gnn_g_msg", "L3_gnn_beta_msg")):
                load(k.l3_cols[:, n:n + 1], a[name].unsqueeze(1))
            load(k.msg_bias[0:1, :], a["L3_gnn_b_msg"].unsqueeze(0))

        @block.gpsimd
        def _(pool):
            pool.memset(dst_i[:, :], FAR)
            pool.memset(k.src_idx[:, :], 0)
            pool.memset(prev_i[:, :], -1)
            pool.memset(next_i[:, :], -2)
            pool.memset(att[:, :, :], 0.0)
            pool.memset(blank[:, :], 0.0)
            pool.memset(attr[:, :, :], 0.0)
            pool.memset(k.edge_in[:, :, 4:5], 1.0).then_inc(cleared, 1)
            pool.memset(ones[:, :], 1.0)
            pool.memset(k.cont[:, :], 0.0)
            pool.memset(k.cnt[:, :], 0.0)
            pool.memset(k.ident[:, :], 0.0)
            pool.memset(later[:, :], 1.0)
            pool.memset(earlier[:, :], 1.0)
            pool.memset(bias_at[:, 0:D], 0.0)
            pool.memset(bias_at[:, D:D + 1], 1.0)
            pool.memset(k.eps[:, :], EPS)
            pool.iota(row_base[:, :], pattern=[[0, 1]], base=-1, channel_multiplier=TH,
                      allow_small_or_imprecise_dtypes=True).then_inc(masks, 1)
            pool.wait_ge(masks, 1)
            pool.affine_select(out=k.ident[:, :], in_=k.ident[:, :], compare_op=ALU.not_equal, fill=1.0,
                               base=0, pattern=[[-1, P]], channel_multiplier=1)
            pool.affine_select(out=later[:, :], in_=later[:, :], compare_op=ALU.is_gt, fill=0.0,
                               base=0, pattern=[[1, P]], channel_multiplier=-1)
            pool.affine_select(out=earlier[:, :], in_=earlier[:, :], compare_op=ALU.is_gt, fill=0.0,
                               base=0, pattern=[[-1, P]], channel_multiplier=1).then_inc(masks, 1)

        @block.vector
        def _(dve):
            done = [0]

            def then(ins):
                done[0] += 1
                ins.then_inc(link, 1)
                dve.wait_ge(link, done[0])

            dve.wait_ge(loaded, loads[0])
            dve.wait_ge(masks, 2)
            then(dve.tensor_copy(dst[:, :], dst_i[:, :]))
            dve.tensor_copy(k.edge_in[:, 0:T, 0:4], attr[:, :, :])
            then(dve.tensor_copy(prev_tail[:, :], prev_i[:, :]))
            then(dve.tensor_copy(next_head[:, :], next_i[:, :]))
            head, tail = dst[:, 0:1], dst[:, T - 1:T]
            then(dve.tensor_tensor(k.cont[:, 1:T], dst[:, 1:T], dst[:, 0:T - 1], ALU.is_equal))
            then(dve.tensor_scalar(is_end[:, 0:T - 1], k.cont[:, 1:T], -1.0, 1.0, ALU.mult, ALU.add))
            then(dve.tensor_tensor(is_end[:, T - 1:T], tail, next_head[:, :], ALU.not_equal))
            then(dve.tensor_copy(k.tail_ended[:, :], is_end[:, T - 1:T]))
            then(dve.tensor_scalar(k.in_head[:, :], dst[:, :], head, None, ALU.is_equal))
            then(dve.tensor_tensor(linked[:, :], prev_tail[:, :], head, ALU.is_equal))
            then(dve.tensor_tensor(tmp[:, :], is_end[:, :], k.in_head[:, :], ALU.mult))
            then(dve.tensor_reduce(head_ends[:, :], tmp[:, :], AX.X, ALU.max))
            then(dve.tensor_tensor(head_out[:, :], head_ends[:, :], linked[:, :], ALU.mult))
            then(dve.tensor_scalar(tmp[:, :], k.in_head[:, :], linked[:, :], -1.0, ALU.mult, ALU.mult))
            then(dve.tensor_scalar(tmp[:, :], tmp[:, :], 1.0, None, ALU.add))
            then(dve.tensor_tensor(valid[:, :], is_end[:, :], tmp[:, :], ALU.mult))
            then(dve.scalar_tensor_tensor(out=tmp[:, :], in0=dst[:, :], scalar=float(-FAR), in1=valid[:, :],
                                          op0=ALU.add, op1=ALU.mult))
            then(dve.tensor_scalar(k.out_idx[:, 0:T], tmp[:, :], float(FAR), None, ALU.add))
            then(dve.scalar_tensor_tensor(out=tmp[:, 0:1], in0=head, scalar=float(-FAR), in1=head_out[:, :],
                                          op0=ALU.add, op1=ALU.mult))
            then(dve.tensor_scalar(k.out_idx[:, T:TH], tmp[:, 0:1], float(FAR), None, ALU.add))
            then(dve.tensor_scalar(k.own_idx[:, 0:T], dst[:, :], float(N - 1), None, ALU.min))
            then(dve.tensor_copy(k.own_idx[:, T:TH], head))
            then(dve.tensor_reduce(head_len[:, :], k.in_head[:, :], AX.X, ALU.add))
            then(dve.tensor_tensor(k.head_row[:, :], head_len[:, :], row_base[:, :], ALU.add))
            then(dve.tensor_tensor_scan(k.cnt[:, 0:T], k.cont[:, 0:T], ones[:, :], 0.0, ALU.mult, ALU.add))
            then(dve.tensor_copy(wide[:, 0, :], head.to_broadcast([P, P])))
            dve.tensor_copy(wide[:, 1, :], tail.to_broadcast([P, P])).then_inc(broad, 1)
            dve.wait_ge(spread, 1)
            then(dve.tensor_copy(head_of[:, :], ps_a[:, 0:P]))
            then(dve.tensor_copy(tail_of[:, :], ps_a[:, P:2 * P]))
            then(dve.tensor_scalar(k.carry_sel[:, :], head_of[:, :], tail, None, ALU.is_equal))
            dve.tensor_tensor(k.carry_sel[:, :], k.carry_sel[:, :], later[:, :], ALU.mult).then_inc(counted, 1)
            dve.wait_ge(counted, 1)
            then(dve.tensor_scalar(k.tail_sel[:, :], tail_of[:, :], head, head_out[:, :], ALU.is_equal, ALU.mult))
            then(dve.tensor_tensor(k.tail_sel[:, :], k.tail_sel[:, :], earlier[:, :], ALU.mult))
            for n, (of, mine) in enumerate(((tail_of, tail), (head_of, tail), (tail_of, head), (head_of, head))):
                then(dve.tensor_scalar(k.apart[:, n, :], of[:, :], mine, None, ALU.is_equal))
                then(dve.tensor_scalar(k.apart[:, n, :], k.apart[:, n, :], -1.0, HUGE, ALU.add, ALU.mult))
            then(dve.tensor_copy(k.seg_end[:, :], is_end[:, :]))
            then(dve.memset(k.seg_end[:, T - 1:T], 1.0))
            then(dve.tensor_scalar(k.not_end[:, :], k.seg_end[:, :], -1.0, 1.0, ALU.mult, ALU.add))
            then(dve.tensor_scalar(k.head_closed[:, :], k.in_head[:, :], head_out[:, :], None, ALU.mult))
            then(dve.tensor_scalar(k.not_head_closed[:, :], k.head_closed[:, :], -1.0, 1.0, ALU.mult, ALU.add))
            dve.wait_ge(carried, 1)
            then(dve.tensor_tensor(k.cnt[:, T:TH], ps_b[:, 0:1], head_len[:, :], ALU.add))
            dve.tensor_copy(k.dinv[:, :], k.cnt[:, :]).then_inc(root_in, 1)
            dve.wait_ge(root_out, 1)
            then(dve.reciprocal(k.dinv[:, :], k.dinv[:, :]))
            for n in range(7):
                dve.wait_ge(w_turn, n + 1)
                dve.tensor_copy(turned[:, n, :], ps_w[n % 2][0:D, 0:D + 1]).then_inc(w_copied, 1)
            outs = [k.w_self[0], k.w_agg[0], k.w_self[1], k.w_agg[1]]
            for n in range(4):
                dve.wait_ge(w_made, n + 1)
                dve.tensor_copy(outs[n][:, :], (ps_c, ps_d)[n % 2][0:D + 1, 0:D]).then_inc(w_kept, 1)
            for n in range(3):
                dve.wait_ge(w_made, 5 + n)
                then(dve.tensor_copy(k.w_att[n][:, 0:D], w_gat[:, n, :]))
                dve.tensor_copy(k.w_att[n][:, D:ATT_ALL], (ps_c, ps_d)[n % 2][0:D, 0:2 * HEADS]).then_inc(w_kept, 1)
            dve.wait_ge(w_kept, 7)
            for n in range(2):
                dve.tensor_scalar(turned[:, n, 0:1], k.gat_bias[:, n:n + 1], 0.0, None, ALU.max)
            then(dve.tensor_scalar(k.gat_rest_row[:, :], k.gat_bias_row[:, :], 0.0, None, ALU.max))
            for n in range(2):
                dve.tensor_copy(k.wide_bias[:, n, :], turned[:, n, 0:1].to_broadcast([D, P])).then_inc(broad, 1)
            dve.wait_ge(spread, 3)
            for n in range(2):
                for j in range(J):
                    then(dve.tensor_copy(k.att_rest[n][:, j, :], ps_w[n][:, 0:ATT]))

        @block.scalar
        def _(act):
            act.wait_ge(root_in, 1)
            act.activation(k.dinv[:, :], k.dinv[:, :], ACT.Sqrt, bias=1.0).then_inc(root_out, 1)

        @block.tensor
        def _(pe):
            pe.wait_ge(loaded, loads[0])
            pe.wait_ge(masks, 2)
            ident = k.ident
            pe.wait_ge(broad, 1)
            pe.transpose(ps_a[:, 0:P], wide[:, 0, :], ident[:, :])
            pe.transpose(ps_a[:, P:2 * P], wide[:, 1, :], ident[:, :]).then_inc(spread, 1)
            pe.wait_ge(counted, 1)
            pe.matmul(ps_b[:, 0:1], k.carry_sel[:, :], k.cnt[:, T - 1:T], start=True, stop=True).then_inc(carried, 1)
            takes = [w1b[:, 0, :], w0b[:, 0, :], w1b[:, 1, :], w0b[:, 1, :]] + [w_gat[:, i, :] for i in range(3)]
            for n, w in enumerate(takes):
                if n >= 2:
                    pe.wait_ge(w_copied, n - 1)
                rows = w.shape[0]
                pe.transpose(ps_w[n % 2][0:D, 0:rows], w, ident[0:rows, 0:rows]).then_inc(w_turn, 1)
            for n in range(7):
                ps = (ps_c, ps_d)[n % 2]
                pe.wait_ge(w_copied, min(n + 1, 7))
                if n >= 2:
                    pe.wait_ge(w_kept, n - 1)
                if n < 4:
                    i, part = n // 2, n % 2
                    ins = pe.matmul(ps[0:D + 1, 0:D], turned[:, n, :], w2[:, i, part, :], start=True, stop=part == 1)
                    if part == 0:
                        ins = pe.matmul(ps[0:D + 1, 0:D], bias_at[:, :], b2[0:1, i, :], start=False, stop=True)
                else:
                    ins = pe.matmul(ps[0:D, 0:2 * HEADS], turned[:, n, 0:D], att[:, n - 4, :], start=True, stop=True)
                ins.then_inc(w_made, 1)
            pe.wait_ge(broad, 3)
            for n in range(2):
                pe.matmul(ps_w[n][:, 0:ATT], k.wide_bias[:, n, :], k.w_att[n + 1][:, 0:ATT],
                          start=True, stop=True).then_inc(spread, 1)
    ph.close()


class Norm:

    def __init__(self, ph, name, slots=SLOTS):
        self.entered = ph.entered
        self.stat = [ph.sb(f"{name}_stat{u}", [P, J, 6]) for u in range(slots)]
        self.mv = [ph.sb(f"{name}_mv{u}", [P, J, 2]) for u in range(slots)]
        self.root = [ph.sb(f"{name}_root{u}", [P, J]) for u in range(slots)]
        self.stats_in = [ph.sem(f"{name}_stats{u}") for u in range(slots)]
        self.var_in = [ph.sem(f"{name}_var{u}") for u in range(slots)]
        self.rooted = [ph.sem(f"{name}_rooted{u}") for u in range(slots)]
        self.inverted = [ph.sem(f"{name}_inverted{u}") for u in range(slots)]

    def spread(self, dve, u, rows, through, parts=P):
        for j in range(J):
            ins = dve.bn_stats(self.stat[u][0:parts, j, :], rows[:, j, :])
        ins.then_inc(self.stats_in[u], 1)
        wait_apart(dve, self.entered, (self.stats_in[u], through(1)))
        for j in range(J):
            ins = dve.bn_aggr(self.mv[u][0:parts, j, :], self.stat[u][0:parts, j, :])
        ins.then_inc(self.var_in[u], 1)

    def take_root(self, act, u, through, scale, bias, parts=P):
        act.wait_ge(self.var_in[u], through(1))
        act.activation(self.root[u][0:parts, :], self.mv[u][0:parts, :, 1], ACT.Sqrt, scale=scale,
                       bias=bias).then_inc(self.rooted[u], 1)

    def invert(self, dve, u, through, parts=P):
        dve.wait_ge(self.rooted[u], through(1))
        dve.reciprocal(self.root[u][0:parts, :], self.root[u][0:parts, :]).then_inc(self.inverted[u], 1)
        dve.wait_ge(self.inverted[u], through(1))

    def mean(self, u, parts=P):
        return self.mv[u][0:parts, :, 0:1].to_broadcast([parts, J, D])

    def inverse(self, u, parts=P):
        return over_rows(self.root[u][0:parts, :], D)


def dense_rows(table, step, u, parts=P):
    if parts != P:
        return table[DENSE_FULL * GROUP:N, :].rearrange("(p j) c -> p j c", j=J)
    groups = table[0:DENSE_FULL * GROUP, :].rearrange("(g p j) c -> p g j c", p=P, j=J)
    return groups[:, bass.ds(step * SLOTS + u, 1), :, :].rearrange("p g j c -> p (g j) c")


def dense_chain(nc, a, k):
    ph = Phase(nc, "dense")
    x = ph.pair(ph.sb, "x", [P, J, D])
    h1, x1, y1, x2, x3, z, c = (ph.pair(ph.sb, n, [P, J, D]) for n in ("h1", "x1", "y1", "x2", "x3", "z", "c"))
    att = ph.pair(ph.sb, "att", [P, J, ATT])
    xt = ph.pair(ph.sb, "xt", [D + 1, GROUP])
    ps_t = ph.pair(ph.ps, "ps_t", [P, 512])
    ps_y = ph.pair(ph.ps, "ps_y", [P, 512])
    loaded, stored = ph.pair(ph.sem, "loaded"), ph.pair(ph.sem, "stored")
    const_stored = ph.sem("const_stored")
    ones_set = ph.sem("ones_set")
    MM = 5
    turned = [ph.pair(ph.sem, f"turned{m}_") for m in range(MM)]
    copied = [ph.pair(ph.sem, f"copied{m}_") for m in range(MM)]
    made = [ph.pair(ph.sem, f"made{m}_") for m in range(MM)]
    ready = {n: ph.pair(ph.sem, f"{n}_ready") for n in ("h1", "x1", "y1", "x2", "x3", "att")}
    sub = {n: ph.pair(ph.sem, f"{n}_sub") for n in ("a", "b", "c", "d", "e", "f", "g", "h")}
    norms = [Norm(ph, f"n{n}") for n in range(5)]
    weights = [k.w_gcn[0], k.w_gcn[1], k.w_self[0], k.w_self[1], k.w_att[0]]

    def parts_of(step, u):
        return REST if isinstance(step, int) and step == DENSE_STEPS - 1 and u == SLOTS - 1 else P

    with nc.Block() as block:
        @block.sync
        def _(sp):
            sp.sem_inc(ph.entered, 1)

            def body(step):
                through = counter(sp, step)
                for u in range(SLOTS):
                    n = parts_of(step, u)
                    wait(sp, ready["x1"][u], through(1, 1))
                    sp.dma_start(x[u][0:n], dense_rows(a["x"], step, u, n)).then_inc(loaded[u], 16)
                for name, table, tile in (("h1", k.t_h1, h1), ("x1", k.t_x1, x1), ("y1", k.t_y1, y1),
                                          ("att", k.t_att[0], att), ("x3", k.t_x3, x3)):
                    for u in range(SLOTS):
                        n = parts_of(step, u)
                        sp.wait_ge(ready[name][u], through(1))
                        sp.dma_start(dense_rows(table, step, u, n), tile[u][0:n]).then_inc(stored[u], 16)
            steps(sp, DENSE_STEPS, body)
            for u in range(SLOTS):
                sp.wait_ge(stored[u], 16 * 5 * DENSE_STEPS)

        @block.tensor
        def _(pe):
            pe.wait_ge(ones_set, 1)

            def body(step):
                through = counter(pe, step)
                for m, (src, is_ready) in enumerate(((x, loaded), (h1, ready["h1"]), (x1, ready["x1"]),
                                                     (y1, ready["y1"]), (x2, ready["x2"]))):
                    for u in range(SLOTS):
                        n = parts_of(step, u)
                        pe.wait_ge(is_ready[u], through(16 if m == 0 else 1))
                        if m == 0:
                            wait(pe, copied[MM - 1][u], through(1, 1))
                        for j in range(J):
                            ins = pe.transpose(ps_t[u][0:D, j * P:j * P + n], src[u][0:n, j, :], k.ident[0:n, 0:n])
                        ins.then_inc(turned[m][u], 1)
                    for u in range(SLOTS):
                        n = parts_of(step, u)
                        rows = D if m == 4 else D + 1
                        width = ATT if m == 4 else D
                        pe.wait_ge(copied[m][u], through(1))
                        if m == 0:
                            wait(pe, ready["att"][u], through(1, 1))
                        for j in range(J):
                            ins = pe.matmul(ps_y[u][0:n, j * width:(j + 1) * width], xt[u][0:rows, j * P:j * P + n],
                                            weights[m][0:rows, 0:width], start=True, stop=True)
                        ins.then_inc(made[m][u], 1)
            steps(pe, DENSE_STEPS, body)

        @block.scalar
        def _(act):
            for n in range(2):
                t = k.t_att[n + 1][0:DENSE_FULL * GROUP, :].rearrange("(g p j) c -> p g (j c)", p=P, j=J)
                flat = k.att_rest[n][:, :, :].rearrange("p j c -> p (j c)")
                for g in range(0, DENSE_FULL, 15):
                    act.dma_start(t[:, g:g + 15, :], flat.unsqueeze(1).to_broadcast([P, 15, J * ATT]))\
                       .then_inc(const_stored, 16)
                act.dma_start(dense_rows(k.t_att[n + 1], 0, 0, REST), k.att_rest[n][0:REST]).then_inc(const_stored, 16)
            act.dma_start(k.t_x[:, :].rearrange("(p n) c -> p (n c)", p=80),
                          a["x"].rearrange("(p n) c -> p (n c)", p=80)).then_inc(const_stored, 16)

            def copy_turned(m, u, n, through):
                act.wait_ge(turned[m][u], through(1))
                if n == P:
                    act.activation(xt[u][0:D, :], ps_t[u][0:D, :], ACT.Copy).then_inc(copied[m][u], 1)
                else:
                    for j in range(J):
                        ins = act.activation(xt[u][0:D, j * P:j * P + n], ps_t[u][0:D, j * P:j * P + n], ACT.Copy)
                    ins.then_inc(copied[m][u], 1)

            def body(step):
                through = counter(act, step)
                us = [(u, parts_of(step, u)) for u in range(SLOTS)]
                for u, n in us:
                    copy_turned(0, u, n, through)
                for u, n in us:
                    act.wait_ge(made[0][u], through(1))
                    wait(act, stored[u], through(80, 1))
                    act.activation(h1[u][0:n].rearrange("p j c -> p (j c)"), ps_y[u][0:n, 0:J * D],
                                   ACT.Relu).then_inc(ready["h1"][u], 1)
                for u, n in us:
                    copy_turned(1, u, n, through)
                for u, n in us:
                    norms[0].take_root(act, u, through, 1.0, k.eps[0:n, :], n)
                for u, n in us:
                    copy_turned(2, u, n, through)
                for u, n in us:
                    norms[1].take_root(act, u, through, D / (D - 1), 0.0, n)
                for u, n in us:
                    copy_turned(3, u, n, through)
                for u, n in us:
                    norms[2].take_root(act, u, through, D / (D - 1), 0.0, n)
                for u, n in us:
                    norms[3].take_root(act, u, through, 1.0, k.eps[0:n, :], n)
                for u, n in us:
                    copy_turned(4, u, n, through)
                for u, n in us:
                    norms[4].take_root(act, u, through, 1.0, k.eps[0:n, :], n)
                for u, n in us:
                    act.wait_ge(made[4][u], through(1))
                    wait(act, stored[u], through(80, 1))
                    act.activation(att[u][0:n].rearrange("p j c -> p (j c)"), ps_y[u][0:n, 0:J * ATT],
                                   ACT.Copy).then_inc(ready["att"][u], 1)
            steps(act, DENSE_STEPS, body)
            act.wait_ge(const_stored, 16 * (2 * (DENSE_FULL // 15 + 1) + 1))

        @block.vector
        def _(dve):
            for u in range(SLOTS):
                ins = dve.memset(xt[u][D:D + 1, :], 1.0)
            ins.then_inc(ones_set, 1)
            def body(step):
                through = counter(dve, step)
                us = [(u, parts_of(step, u)) for u in range(SLOTS)]

                def made_rows(u, n):
                    return ps_y[u][0:n, 0:J * D].rearrange("p (j c) -> p j c", c=D)

                def center(norm, src, out, u, n, sem):
                    dve.wait_ge(norm.var_in[u], through(1))
                    dve.tensor_tensor(out[u][0:n], src[u][0:n], norm.mean(u, n), ALU.subtract).then_inc(sub[sem][u], 1)

                for u, n in us:
                    dve.wait_ge(made[1][u], through(1))
                    dve.scalar_tensor_tensor(out=z[u][0:n], in0=made_rows(u, n), scalar=0.0, in1=x[u][0:n],
                                             op0=ALU.max, op1=ALU.add).then_inc(sub["a"][u], 1)
                for u, n in us:
                    dve.wait_ge(sub["a"][u], through(1))
                    norms[0].spread(dve, u, z[u][0:n], through, n)
                for u, n in us:
                    center(norms[0], z, c, u, n, "b")
                for u, n in us:
                    norms[0].invert(dve, u, through, n)
                    dve.wait_ge(sub["b"][u], through(1))
                    wait(dve, stored[u], through(80, 1))
                    dve.tensor_tensor(x1[u][0:n], c[u][0:n], norms[0].inverse(u, n),
                                      ALU.mult).then_inc(ready["x1"][u], 1)
                for u, n in us:
                    dve.wait_ge(made[2][u], through(1))
                    norms[1].spread(dve, u, made_rows(u, n), through, n)
                for u, n in us:
                    norms[1].invert(dve, u, through, n)
                    dve.tensor_tensor(y1[u][0:n], made_rows(u, n), norms[1].inverse(u, n),
                                      ALU.mult).then_inc(ready["y1"][u], 1)
                for u, n in us:
                    dve.wait_ge(made[3][u], through(1))
                    norms[2].spread(dve, u, made_rows(u, n), through, n)
                for u, n in us:
                    norms[2].invert(dve, u, through, n)
                    dve.tensor_tensor(c[u][0:n], made_rows(u, n), norms[2].inverse(u, n),
                                      ALU.mult).then_inc(sub["c"][u], 1)
                for u, n in us:
                    dve.wait_ge(sub["c"][u], through(1))
                    dve.tensor_tensor(z[u][0:n], c[u][0:n], x1[u][0:n], ALU.add).then_inc(sub["d"][u], 1)
                for u, n in us:
                    dve.wait_ge(sub["d"][u], through(1))
                    norms[3].spread(dve, u, z[u][0:n], through, n)
                for u, n in us:
                    center(norms[3], z, c, u, n, "e")
                for u, n in us:
                    norms[3].invert(dve, u, through, n)
                    dve.wait_ge(sub["e"][u], through(1))
                    dve.tensor_tensor(x2[u][0:n], c[u][0:n], norms[3].inverse(u, n),
                                      ALU.mult).then_inc(ready["x2"][u], 1)
                for u, n in us:
                    dve.wait_ge(ready["x2"][u], through(1))
                    dve.tensor_tensor(z[u][0:n], x2[u][0:n],
                                      k.gat_rest_row[0:n, :].unsqueeze(1).to_broadcast([n, J, D]),
                                      ALU.add).then_inc(sub["f"][u], 1)
                for u, n in us:
                    dve.wait_ge(sub["f"][u], through(1))
                    norms[4].spread(dve, u, z[u][0:n], through, n)
                for u, n in us:
                    center(norms[4], z, c, u, n, "g")
                for u, n in us:
                    norms[4].invert(dve, u, through, n)
                    dve.wait_ge(sub["g"][u], through(1))
                    dve.tensor_tensor(x3[u][0:n], c[u][0:n], norms[4].inverse(u, n),
                                      ALU.mult).then_inc(ready["x3"][u], 1)
            steps(dve, DENSE_STEPS, body)
    ph.close()


def rows_of(tile):
    return tile.rearrange("p j c -> p (j c)")


def by_head(rows):
    return rows[:, :, 0:D].rearrange("p j (h c) -> p j h c", h=HEADS)


def per_head(weights):
    return weights.unsqueeze(3).to_broadcast([P, J, HEADS, CH])


class Rows:

    def __init__(self, ph, gather=None, gather_idx=None, scatter=None, scatter_idx=None, width=D, head_too=False):
        self.ph, self.table, self.idx, self.out, self.out_idx = ph, gather, gather_idx, scatter, scatter_idx
        self.head_too = head_too
        if gather is not None:
            self.rows = ph.pair(ph.sb, "gathered", [P, J, width])
            self.window = ph.pair(ph.sb, "take_window", [P, J], I32)
            self.window_in, self.here = ph.pair(ph.sem, "take_window_in"), ph.pair(ph.sem, "gathered_in")
        if scatter is not None:
            self.out_window = ph.pair(ph.sb, "put_window", [P, J], I32)
            self.out_window_in, self.gone = ph.pair(ph.sem, "put_window_in"), ph.pair(ph.sem, "scattered")

    def count(self, step, u):
        return J - 1 if not self.head_too and is_last(step) and u == SLOTS - 1 else J

    def all_here(self, step, u, through):
        return through(16 * J) - 16 * (J - self.count(step, u)) if is_last(step) else through(16 * J)

    def gather(self, pool, step, u, through, *free):
        wait_apart(pool, self.ph.entered, (self.window_in[u], through(1)), *free)
        for j in range(self.count(step, u)):
            pool.indirect_dma_start(
                out=self.rows[u][:, j, :], out_offset=None, in_=self.table,
                in_offset=bass.IndirectOffsetOnAxis(ap=self.window[u][:, j:j + 1], axis=0)).then_inc(self.here[u], 16)

    def scatter(self, pool, tile, u, through, ready, bound):
        wait_apart(pool, self.ph.entered, (self.out_window_in[u], through(1)), (ready, through(1)))
        for j in range(J):
            pool.indirect_dma_start(
                out=self.out, out_offset=bass.IndirectOffsetOnAxis(ap=self.out_window[u][:, j:j + 1], axis=0),
                in_=tile[:, j, :], in_offset=None, bounds_check=bound, oob_is_err=False).then_inc(self.gone[u], 16)

    def first_windows(self, act):
        for u in range(SLOTS):
            act.activation(self.window[u][:, :], self.idx[:, cols(0, u)], ACT.Copy).then_inc(self.window_in[u], 1)

    def next_window(self, act, step, u, through):
        if not is_last(step):
            wait_apart(act, self.ph.entered, (self.here[u], self.all_here(step, u, through)))
            act.activation(self.window[u][:, :], self.idx[:, cols(step, u, skip=J * SLOTS)],
                           ACT.Copy).then_inc(self.window_in[u], 1)

    def put_window(self, act, step, u, through, back=0):
        wait_apart(act, self.ph.entered, (self.gone[u], through(16 * J, 1)))
        act.activation(self.out_window[u][:, :], self.out_idx[:, cols(step, u, skip=-J * SLOTS * back)],
                       ACT.Copy).then_inc(self.out_window_in[u], 1)


def is_last(step):
    return isinstance(step, int) and step == STEPS - 1


class EdgeFeatures:

    def __init__(self, ph, k, slots):
        self.k, self.slots = k, slots
        self.attr_t = [ph.sb(f"attr_t{u}", [5, GROUP]) for u in range(slots)]
        self.ps_attr = [ph.ps(f"ps_attr{u}") for u in range(slots)]
        self.ps_feat = [ph.ps(f"ps_feat{u}") for u in range(slots)]
        self.turned, self.copied, self.made, self.kept, self.here = (
            [ph.sem(f"{n}{u}") for u in range(SLOTS)]
            for n in ("attr_turned", "attr_copied", "feat_made", "feat_kept", "attr_here"))
        self.window = ph.pair(ph.sb, "attr_window", [P, J, 5])
        self.entered = ph.entered

    def take(self, act, step, u, through):
        n = edge_places(step, u)
        wait_apart(act, self.entered, (self.turned[u], through(1, 1)))
        act.activation(self.window[u][:, 0:n, :], self.k.edge_in[:, cols(step, u, n), :],
                       ACT.Copy).then_inc(self.here[u], 1)

    def turn(self, pe, step, u, through):
        pe.wait_ge(self.here[u], through(1))
        ps = self.ps_attr[u % self.slots]
        for j in range(edge_places(step, u)):
            ins = pe.transpose(ps[0:5, j * P:(j + 1) * P], self.window[u][:, j, :], self.k.ident[:, :])
        ins.then_inc(self.turned[u], 1)


def edge_places(step, u):
    return J - 1 if is_last(step) and u == SLOTS - 1 else J


def column_stats(dve, ph, stat, lone, values, step, u):
    n = edge_places(step, u)
    v = values[:, 0:n * P].rearrange("c (j p) -> c j p", p=P)
    dve.bn_stats(stat[:, bass.ds(step * SLOTS + u, 1), :].rearrange("c a s -> c (a s)"), v[:, :, 0:P - 1])
    return dve.tensor_copy(lone[:, cols(step, u, n)], v[:, :, P - 1])


def column_scale(dve, act, gamma, beta, mv, root, scale, shift, sems, k, act_side):
    var_in, rooted, link = sems
    if act_side:
        act.wait_ge(var_in, 1)
        act.activation(root, mv[:, 1:2], ACT.Sqrt, bias=k.eps[0:D, :]).then_inc(rooted, 1)
        return
    dve.wait_ge(rooted, 1)
    dve.reciprocal(root, root).then_inc(link, 1)
    dve.wait_ge(link, 1)
    dve.tensor_tensor(scale, gamma, root, ALU.mult).then_inc(link, 1)
    dve.wait_ge(link, 2)
    dve.tensor_tensor(root, mv[:, 0:1], scale, ALU.mult).then_inc(link, 1)
    dve.wait_ge(link, 3)
    dve.tensor_tensor(shift, beta, root, ALU.subtract).then_inc(link, 1)
    dve.wait_ge(link, 4)


def own_rows(nc, a, k):
    ph = Phase(nc, "own")
    take = Rows(ph, a["x"], k.own_idx, k.t_x, k.out_idx, head_too=True)
    x = take.rows
    scaled = ph.pair(ph.sb, "scaled", [P, J, D])
    scaled_in, x_stored, scaled_stored = (ph.pair(ph.sem, n) for n in ("scaled_in", "x_stored", "scaled_stored"))
    ef = EdgeFeatures(ph, k, SLOTS)
    feat = ph.pair(ph.sb, "feat", [D, GROUP])
    feat_read = ph.pair(ph.sem, "feat_read")
    stat, lone = ph.sb("stat", [D, 2 * STEPS + 1, 6]), ph.sb("lone", [D, TH])
    mv, root = ph.sb("mv", [D, 2]), ph.sb("root", [D, 1])
    shift_wide = ph.sb("shift_wide", [1, D + 1])
    ps_w = ph.ps("ps_w")
    stat_in, var_in, rooted, link, folded, bias_in = (
        ph.sem(n) for n in ("stat_in", "var_in", "rooted", "link", "folded", "bias_in"))

    with nc.Block() as block:
        @block.sync
        def _(sp):
            sp.sem_inc(ph.entered, 1)

            def body(step):
                through = counter(sp, step)
                for u in range(SLOTS):
                    sp.wait_ge(take.here[u], take.all_here(step, u, through))
                    sp.dma_start(k.l_x[:, cols(step, u), :], x[u][:, :, :]).then_inc(x_stored[u], 16)
                    sp.wait_ge(scaled_in[u], through(1))
                    sp.dma_start(k.l_s[:, cols(step, u), :], scaled[u][:, :, :]).then_inc(scaled_stored[u], 16)
            steps(sp, STEPS, body)
            for u in range(SLOTS):
                sp.wait_ge(x_stored[u], 16 * STEPS)
                sp.wait_ge(scaled_stored[u], 16 * STEPS)

        @block.gpsimd
        def _(pool):
            bound = pool.to_reg(N - 1)

            def body(step):
                through = counter(pool, step)
                before = None if isinstance(step, int) and step == 0 else counter(pool, step - 1)
                for u in range(SLOTS):
                    take.gather(pool, step, u, through, (x_stored[u], through(16, 1)), (scaled_in[u], through(1, 1)))
                    if before is not None:
                        take.scatter(pool, scaled[u], u, before, scaled_in[u], bound)
            steps(pool, STEPS, body)
            for u in range(SLOTS):
                take.scatter(pool, scaled[u], u, counter(pool, STEPS - 1), scaled_in[u], bound)
            for u in range(SLOTS):
                pool.wait_ge(take.gone[u], 16 * J * STEPS)

        @block.scalar
        def _(act):
            take.first_windows(act)

            def body(step):
                through = counter(act, step)
                for u in range(SLOTS):
                    take.next_window(act, step, u, through)
                    take.put_window(act, step, u, through)
                    ef.take(act, step, u, through)
                    n = edge_places(step, u) * P
                    act.wait_ge(ef.turned[u], through(1))
                    act.activation(ef.attr_t[u][:, 0:n], ef.ps_attr[u][0:5, 0:n], ACT.Copy).then_inc(ef.copied[u], 1)
                    act.wait_ge(ef.made[u], through(1))
                    wait(act, feat_read[u], through(1, 1))
                    act.activation(feat[u][:, 0:n], ef.ps_feat[u][0:D, 0:n], ACT.Relu).then_inc(ef.kept[u], 1)
            steps(act, STEPS, body)
            column_scale(None, act, None, None, mv, root[:, :], None, None, (var_in, rooted, link), k, True)

        @block.tensor
        def _(pe):
            def body(step):
                through = counter(pe, step)
                for u in range(SLOTS):
                    wait(pe, ef.copied[u], through(1, 1))
                    ef.turn(pe, step, u, through)
                    n = edge_places(step, u) * P
                    pe.wait_ge(ef.copied[u], through(1))
                    wait(pe, ef.kept[u], through(1, 1))
                    pe.matmul(ef.ps_feat[u][0:D, 0:n], k.w_edge[:, :], ef.attr_t[u][:, 0:n],
                              start=True, stop=True).then_inc(ef.made[u], 1)
            steps(pe, STEPS, body)
            pe.wait_ge(folded, 1)
            pe.matmul(ps_w[0:1, 0:D], k.l3_cols[:, 7:8], k.w_msg[:, 2, :], start=True, stop=True).then_inc(bias_in, 1)

        @block.vector
        def _(dve):
            def body(step):
                through = counter(dve, step)
                for u in range(SLOTS):
                    dve.wait_ge(take.here[u], take.all_here(step, u, through))
                    wait(dve, take.gone[u], through(16 * J, 1))
                    wait(dve, scaled_stored[u], through(16, 1))
                    dve.tensor_tensor(scaled[u][:, :, :], x[u][:, :, :], over_rows(k.dinv[:, cols(step, u)], D),
                                      ALU.mult).then_inc(scaled_in[u], 1)
                    wait_apart(dve, ph.entered, (ef.kept[u], through(1)))
                    column_stats(dve, ph, stat, lone, feat[u], step, u).then_inc(feat_read[u], 1)
            steps(dve, STEPS, body)
            dve.wait_ge(feat_read[0], STEPS)
            dve.wait_ge(feat_read[1], STEPS)
            dve.bn_stats(stat[:, 2 * STEPS, :], lone[:, 0:LAST]).then_inc(stat_in, 1)
            dve.wait_ge(stat_in, 1)
            dve.bn_aggr(mv[:, :], stat[:, :, :].rearrange("c a s -> c (a s)")).then_inc(var_in, 1)
            column_scale(dve, None, k.l3_cols[:, 2:3], k.l3_cols[:, 3:4], mv, root[:, :], k.edge_scale[:, :],
                         k.l3_cols[:, 7:8], (var_in, rooted, link), k, False)
            dve.tensor_scalar(k.w_feat[0:D, :], k.w_msg[:, 2, :], k.edge_scale[:, :], None, ALU.mult).then_inc(folded, 1)
            dve.wait_ge(bias_in, 1)
            dve.tensor_tensor(k.msg_bias[:, :], ps_w[0:1, 0:D], k.msg_bias[:, :], ALU.add)
    ph.close()


GCN1, GCN2, SAGE1, SAGE2, GAT1, GAT2, GAT3 = "gcn1", "gcn2", "sage1", "sage2", "gat1", "gat2", "gat3"


def node_round(nc, a, k, kind, table=None, out=None, own=None, rest=None, keep=None, layer=0):
    assert SLOTS == 2
    gat, sage, gcn = kind in (GAT1, GAT2, GAT3), kind in (SAGE1, SAGE2), kind in (GCN1, GCN2)
    C = ATT if gat else D
    A_WIDTH = D + 1 if sage else C
    OUT = ATT if kind in (SAGE2, GAT1, GAT2) else D
    normed = kind in (GCN2, SAGE2, GAT3)
    over_std = sage
    multiplied = kind != GAT3
    ph = Phase(nc, kind)
    put = Rows(ph, table, k.src_idx, out, k.out_idx)
    acc = ph.pair(ph.sb, "acc", [P, J, A_WIDTH])
    cont = ph.pair(ph.sb, "cont", [P, J])
    new = ph.pair(ph.sb, "new", [P, J, OUT])
    head_part = ph.sb("head_part", [P, C])
    xt = ph.pair(ph.sb, "xt", [D + 1, GROUP])
    ps_x, ps_y = ph.pair(ph.ps, "ps_x"), ph.pair(ph.ps, "ps_y")
    ps_carry = ph.ps("ps_carry")
    link = [ph.pair(ph.sem, f"summed{j}_") for j in range(J)]
    windows, acc_stored = ph.pair(ph.sem, "windows"), ph.pair(ph.sem, "acc_stored")
    carried, head_here, ones_set, started = (ph.sem(n) for n in ("carried", "head_here", "ones_set", "started"))
    input_in, turned, copied, made = (ph.pair(ph.sem, n) for n in ("input_in", "turned", "copied", "made"))
    new_in, new_stored, step_a, step_b, step_c = (
        ph.pair(ph.sem, n) for n in ("new_in", "new_stored", "step_a", "step_b", "step_c"))
    if gcn or gat:
        mixed = ph.pair(ph.sb, "mixed", [P, J, D])
        mix_a, mix_b = ph.pair(ph.sem, "mix_a"), ph.pair(ph.sem, "mix_b")
    if own is not None:
        mine, own_in = ph.pair(ph.sb, "mine", [P, J, D]), ph.pair(ph.sem, "own_in")
    if rest is not None:
        resid, rest_in = ph.pair(ph.sb, "resid", [P, J, D]), ph.pair(ph.sem, "rest_in")
    if sage:
        own_t, ps_o = ph.pair(ph.sb, "own_t", [D + 1, GROUP]), ph.pair(ph.ps, "ps_o")
        unit = Norm(ph, "unit")
    if gat:
        msg, weighted = ph.pair(ph.sb, "msg", [P, J, ATT]), ph.pair(ph.sb, "weighted", [P, J, ATT])
        den = ph.pair(ph.sb, "den", [P, J, HEADS])
        msg_in, weighed, ex_in = (ph.pair(ph.sem, n) for n in ("msg_in", "weighed", "ex_in"))
    if normed:
        norm = Norm(ph, "norm")
        z, c = ph.pair(ph.sb, "z", [P, J, D]), ph.pair(ph.sb, "c", [P, J, D])
        z_in, c_in = ph.pair(ph.sem, "z_in"), ph.pair(ph.sem, "c_in")
    if kind == SAGE2:
        x2, x2t = ph.pair(ph.sb, "x2", [P, J, D]), ph.sb("x2t", [D, GROUP])
        ps_u = ph.ps("ps_u")
        x2_in, x2_turned, x2_copied, x2_made = (
            ph.pair(ph.sem, n) for n in ("x2_in", "x2_turned", "x2_copied", "x2_made"))
    l_acc = k.l_acc100 if gat else k.l_acc
    kept = None if keep is None else (x2 if kind == SAGE2 else new)
    kept_in = None if keep is None else (x2_in if kind == SAGE2 else new_in)

    def msgs(step, u):
        return edge_places(step, u)

    with nc.Block() as block:
        @block.sync
        def _(sp):
            sp.sem_inc(ph.entered, 1)

            def load_rows(step, u, through):
                if gat:
                    wait(sp, link[J - 1][u], through(1, 1))
                    n = msgs(step, u)
                    sp.dma_start(msg[u][:, 0:n, :], k.l_msg[:, cols(step, u, n), :]).then_inc(msg_in[u], 16)
                if own is not None:
                    wait(sp, (mix_b if gcn else turned)[u], through(1, 1))
                    sp.dma_start(mine[u][:, :, :], own[:, cols(step, u), :]).then_inc(own_in[u], 16)

            def load_rest(step, u, through):
                if rest is not None:
                    wait(sp, z_in[u], through(1, 1))
                    sp.dma_start(resid[u][:, :, :], rest[:, cols(step, u), :]).then_inc(rest_in[u], 16)

            def store_sums(step, u, through):
                n = msgs(step, u)
                sp.wait_ge(link[n - 1][u], through(1))
                sp.dma_start(l_acc[:, cols(step, u, n), :], acc[u][:, 0:n, 0:C]).then_inc(acc_stored[u], 16)

            def store_new(step, u):
                if keep is not None:
                    sp.wait_ge(kept_in[u], counter(sp, step)(1))
                    sp.dma_start(keep[:, cols(step, u), :], kept[u][:, :, :]).then_inc(new_stored[u], 16)

            def body(step):
                through = counter(sp, step)
                load_rows(step, 0, through)
                load_rows(step, 1, through)
                load_rest(step, 0, through)
                store_sums(step, 0, through)
                if not (isinstance(step, int) and step == 0):
                    store_new(step - 1, 1)
                load_rest(step, 1, through)
                store_sums(step, 1, through)
                store_new(step, 0)
            steps(sp, STEPS, body)
            store_new(STEPS - 1, 1)
            for u in range(SLOTS):
                if keep is not None:
                    sp.wait_ge(new_stored[u], 16 * STEPS)

        @block.gpsimd
        def _(pool):
            bound = pool.to_reg(N - 1)

            def body(step):
                through = counter(pool, step)
                before = None if isinstance(step, int) and step == 0 else counter(pool, step - 1)
                for u in range(SLOTS):
                    if not gat:
                        put.gather(pool, step, u, through, (link[J - 1][u], through(1, 1)))
                    if before is not None:
                        put.scatter(pool, new[u], u, before, new_in[u], bound)
            steps(pool, STEPS, body)
            for u in range(SLOTS):
                pool.wait_ge(acc_stored[u], 16 * STEPS)
            pool.indirect_dma_start(
                out=head_part[:, :], out_offset=None, in_=l_acc.rearrange("p t c -> (p t) c"),
                in_offset=bass.IndirectOffsetOnAxis(ap=k.head_row[:, 0:1], axis=0)).then_inc(head_here, 16)
            for u in range(SLOTS):
                put.scatter(pool, new[u], u, counter(pool, STEPS - 1), new_in[u], bound)
            for u in range(SLOTS):
                pool.wait_ge(put.gone[u], 16 * J * STEPS)

        @block.scalar
        def _(act):
            if not gat:
                put.first_windows(act)

            def front(step, u):
                through = counter(act, step)
                wait_apart(act, ph.entered, (link[J - 1][u], through(1, 1)))
                if sage:
                    wait_apart(act, ph.entered, (turned[u], through(1, 1)))
                    act.activation(acc[u][:, :, D], k.cnt[:, cols(step, u)], ACT.Copy)
                if gat:
                    n = msgs(step, u)
                    act.activation(weighted[u][:, 0:n, D:ATT], k.att_e[:, cols(step, u, n), :], ACT.Copy)
                act.activation(cont[u][:, :], k.cont[:, cols(step, u)], ACT.Copy).then_inc(windows[u], 1)
                if not gat:
                    put.next_window(act, step, u, through)
                if multiplied:
                    rows = D + 1 if sage else D
                    act.wait_ge(turned[u], through(1))
                    wait(act, made[u], through(1, 1))
                    if kind in (GAT1, GAT2):
                        act.activation(xt[u][0:D, :], ps_x[u][0:D, :], ACT.Relu,
                                       bias=k.gat_bias[:, layer:layer + 1]).then_inc(copied[u], 1)
                    elif sage:
                        act.activation(own_t[u][0:D, :], ps_o[u][0:D, :], ACT.Copy)
                        act.activation(xt[u][0:rows, :], ps_x[u][0:rows, :], ACT.Copy).then_inc(copied[u], 1)
                    else:
                        act.activation(xt[u][0:D, :], ps_x[u][0:D, :], ACT.Copy).then_inc(copied[u], 1)

            def back(step, u):
                through = counter(act, step)
                put.put_window(act, step, u, through)
                if over_std:
                    unit.take_root(act, u, through, D / (D - 1), 0.0)
                if normed:
                    norm.take_root(act, u, through, 1.0, k.eps[:, :])
                if kind == SAGE2:
                    act.wait_ge(x2_turned[u], through(1))
                    act.activation(x2t[:, :], ps_u[0:D, :], ACT.Copy).then_inc(x2_copied[u], 1)
            turns(act, front, back)

        @block.tensor
        def _(pe):
            pe.wait_ge(ones_set, 1)

            def carry(step, u):
                if is_last(step) and u == SLOTS - 1:
                    pe.wait_ge(link[J - 2][u], STEPS)
                    pe.matmul(ps_carry[:, 0:C], k.carry_sel[:, :], acc[u][:, J - 2, 0:C],
                              start=True, stop=True).then_inc(carried, 1)

            def front(step, u):
                through = counter(pe, step)
                carry(step, u)
                if not multiplied:
                    return
                if sage:
                    pe.wait_ge(own_in[u], through(16))
                    wait(pe, copied[u], through(1, 1))
                    for j in range(J):
                        pe.transpose(ps_o[u][0:D, j * P:(j + 1) * P], mine[u][:, j, :], k.ident[:, :])
                    pe.wait_ge(link[J - 1][u], through(1))
                    for j in range(J):
                        ins = pe.transpose(ps_x[u][0:D + 1, j * P:(j + 1) * P], acc[u][:, j, :], k.ident[:, :])
                else:
                    pe.wait_ge(mix_b[u], through(1))
                    wait(pe, copied[u], through(1, 1))
                    for j in range(J):
                        ins = pe.transpose(ps_x[u][0:D, j * P:(j + 1) * P], mixed[u][:, j, :], k.ident[:, :])
                ins.then_inc(turned[u], 1)

            def back(step, u):
                if not multiplied:
                    return
                through = counter(pe, step)
                pe.wait_ge(copied[u], through(1))
                wait(pe, (z_in if normed else new_in)[u], through(1, 1))
                for j in range(J):
                    at = slice(j * P, (j + 1) * P)
                    if gcn:
                        ins = pe.matmul(ps_y[u][:, j * D:(j + 1) * D], xt[u][:, at], k.w_gcn[layer][:, :],
                                        start=True, stop=True)
                    elif sage:
                        pe.matmul(ps_y[u][:, j * D:(j + 1) * D], own_t[u][:, at], k.w_self[layer][:, :],
                                  start=True, stop=False)
                        ins = pe.matmul(ps_y[u][:, j * D:(j + 1) * D], xt[u][:, at], k.w_agg[layer][:, :],
                                        start=False, stop=True)
                    else:
                        ins = pe.matmul(ps_y[u][:, j * ATT_ALL:(j + 1) * ATT_ALL], xt[u][0:D, at],
                                        k.w_att[layer + 1][:, :], start=True, stop=True)
                ins.then_inc(made[u], 1)
                if kind == SAGE2:
                    pe.wait_ge(x2_in[u], through(1))
                    wait(pe, new_in[1 - u], through(1, 1) if u == 0 else through(1))
                    for j in range(J):
                        ins = pe.transpose(ps_u[0:D, j * P:(j + 1) * P], x2[u][:, j, :], k.ident[:, :])
                    ins.then_inc(x2_turned[u], 1)
                    pe.wait_ge(x2_copied[u], through(1))
                    for j in range(J):
                        ins = pe.matmul(ps_u[:, j * ATT_ALL:(j + 1) * ATT_ALL], x2t[:, j * P:(j + 1) * P],
                                        k.w_att[0][:, :], start=True, stop=True)
                    ins.then_inc(x2_made[u], 1)
            turns(pe, front, back)

        @block.vector
        def _(dve):
            for u in range(SLOTS):
                dve.memset(xt[u][D:D + 1, :], 1.0)
                if sage:
                    dve.memset(own_t[u][D:D + 1, :], 1.0)
            dve.memset(acc[1][:, J - 1, 0:C], 0.0).then_inc(ones_set, 1)
            dve.wait_ge(ones_set, 1)

            def front(step, u):
                through = counter(dve, step)
                n = msgs(step, u)
                if gat:
                    dve.wait_ge(msg_in[u], through(16))
                    dve.tensor_tensor(by_head(weighted[u][:, 0:n, :]), by_head(msg[u][:, 0:n, :]),
                                      k.att_e[:, cols(step, u, n), :].unsqueeze(3).to_broadcast([P, n, HEADS, CH]),
                                      ALU.mult).then_inc(weighed[u], 1)
                    dve.wait_ge(weighed[u], through(1))
                else:
                    dve.wait_ge(put.here[u], put.all_here(step, u, through))
                rows = weighted[u] if gat else put.rows[u]
                dve.wait_ge(windows[u], through(1))
                wait(dve, acc_stored[u], through(16, 1))
                if sage:
                    wait(dve, turned[u], through(1, 1))
                for j in range(n):
                    if j:
                        dve.wait_ge(link[j - 1][u], through(1))
                        before = acc[u][:, j - 1, 0:C]
                    else:
                        wait(dve, link[J - 1][1 - u], through(1, 1) if u == 0 else through(1))
                        before = acc[1 - u][:, J - 1, 0:C]
                    dve.scalar_tensor_tensor(out=acc[u][:, j, 0:C], in0=before, scalar=cont[u][:, j:j + 1],
                                             in1=rows[:, j, :], op0=ALU.mult, op1=ALU.add).then_inc(link[j][u], 1)
                if n < J:
                    dve.wait_ge(carried, 1)
                    dve.wait_ge(head_here, 16)
                    dve.tensor_tensor(acc[u][:, J - 1, 0:C], ps_carry[:, 0:C], head_part[:, :],
                                      ALU.add).then_inc(link[J - 1][u], 1)
                if gcn:
                    dve.wait_ge(link[J - 1][u], through(1))
                    dve.wait_ge(own_in[u], through(16))
                    wait(dve, turned[u], through(1, 1))
                    dve.tensor_tensor(mine[u][:, :, :], acc[u][:, :, :], mine[u][:, :, :], ALU.add).then_inc(step_a[u], 1)
                    dve.wait_ge(step_a[u], through(1))
                    dve.tensor_tensor(mixed[u][:, :, :], mine[u][:, :, :], over_rows(k.dinv[:, cols(step, u)], D),
                                      ALU.mult).then_inc(mix_b[u], 1)
                if gat:
                    dve.wait_ge(link[J - 1][u], through(1))
                    dve.tensor_scalar(den[u][:, :, :], acc[u][:, :, D:ATT], 1e-16, None, ALU.add).then_inc(step_a[u], 1)
                    dve.wait_ge(step_a[u], through(1))
                    dve.reciprocal(den[u][:, :, :], den[u][:, :, :]).then_inc(mix_a[u], 1)
                    dve.wait_ge(mix_a[u], through(1))
                    if multiplied:
                        wait(dve, turned[u], through(1, 1))
                    dve.tensor_tensor(by_head(mixed[u]), by_head(acc[u]), per_head(den[u][:, :, :]),
                                      ALU.mult).then_inc(mix_b[u], 1)

            def back(step, u):
                through = counter(dve, step)
                y = ps_y[u][:, 0:J * D].rearrange("p (j c) -> p j c", c=D)

                def new_free():
                    wait(dve, put.gone[u], through(16 * J, 1))
                    if keep is not None:
                        wait(dve, new_stored[u], through(16, 1))

                if kind == GCN1:
                    dve.wait_ge(made[u], through(1))
                    new_free()
                    dve.scalar_tensor_tensor(out=new[u][:, :, :], in0=y, scalar=0.0,
                                             in1=over_rows(k.dinv[:, cols(step, u)], D),
                                             op0=ALU.max, op1=ALU.mult).then_inc(new_in[u], 1)
                elif kind == GCN2:
                    dve.wait_ge(made[u], through(1))
                    dve.wait_ge(rest_in[u], through(16))
                    dve.scalar_tensor_tensor(out=z[u][:, :, :], in0=y, scalar=0.0, in1=resid[u][:, :, :],
                                             op0=ALU.max, op1=ALU.add).then_inc(z_in[u], 1)
                elif sage:
                    dve.wait_ge(made[u], through(1))
                    unit.spread(dve, u, y, through)
                    unit.invert(dve, u, through)
                    if kind == SAGE1:
                        new_free()
                        dve.tensor_tensor(new[u][:, :, :], y, unit.inverse(u), ALU.mult).then_inc(new_in[u], 1)
                    else:
                        dve.wait_ge(rest_in[u], through(16))
                        dve.tensor_tensor(c[u][:, :, :], y, unit.inverse(u), ALU.mult).then_inc(step_a[u], 1)
                        dve.wait_ge(step_a[u], through(1))
                        dve.tensor_tensor(z[u][:, :, :], c[u][:, :, :], resid[u][:, :, :], ALU.add).then_inc(z_in[u], 1)
                elif kind in (GAT1, GAT2):
                    dve.wait_ge(made[u], through(1))
                    new_free()
                    y = ps_y[u][:, 0:J * ATT_ALL].rearrange("p (j c) -> p j c", c=ATT_ALL)
                    dve.tensor_scalar(k.att_dst[:, cols(step, u), :], y[:, :, ATT:ATT_ALL], 1.0, None, ALU.mult)
                    dve.tensor_copy(new[u][:, :, :], y[:, :, 0:ATT]).then_inc(new_in[u], 1)
                else:
                    dve.wait_ge(mix_b[u], through(1))
                    dve.tensor_tensor(c[u][:, :, :], mixed[u][:, :, :],
                                      k.gat_bias_row[:, :].unsqueeze(1).to_broadcast([P, J, D]),
                                      ALU.add).then_inc(step_b[u], 1)
                    dve.wait_ge(step_b[u], through(1))
                    dve.wait_ge(rest_in[u], through(16))
                    dve.scalar_tensor_tensor(out=z[u][:, :, :], in0=c[u][:, :, :], scalar=0.0, in1=resid[u][:, :, :],
                                             op0=ALU.max, op1=ALU.add).then_inc(z_in[u], 1)
                if normed:
                    dve.wait_ge(z_in[u], through(1))
                    norm.spread(dve, u, z[u], through)
                    dve.wait_ge(norm.var_in[u], through(1))
                    dve.tensor_tensor(c[u][:, :, :], z[u][:, :, :], norm.mean(u), ALU.subtract).then_inc(c_in[u], 1)
                    norm.invert(dve, u, through)
                    dve.wait_ge(c_in[u], through(1))
                    if kind == SAGE2:
                        wait(dve, new_stored[u], through(16, 1))
                        wait(dve, x2_turned[u], through(1, 1))
                        dve.tensor_tensor(x2[u][:, :, :], c[u][:, :, :], norm.inverse(u), ALU.mult).then_inc(x2_in[u], 1)
                        dve.wait_ge(x2_made[u], through(1))
                        wait(dve, put.gone[u], through(16 * J, 1))
                        y = ps_u[:, 0:J * ATT_ALL].rearrange("p (j c) -> p j c", c=ATT_ALL)
                        dve.tensor_scalar(k.att_dst[:, cols(step, u), :], y[:, :, ATT:ATT_ALL], 1.0, None, ALU.mult)
                        dve.tensor_copy(new[u][:, :, :], y[:, :, 0:ATT]).then_inc(new_in[u], 1)
                    else:
                        new_free()
                        dve.tensor_tensor(new[u][:, :, :], c[u][:, :, :], norm.inverse(u), ALU.mult)\
                            .then_inc(new_in[u], 1)
            turns(dve, front, back)
    ph.close()


def attention_weights(nc, k, table, layer):
    ph = Phase(nc, f"logits{layer}")
    take = Rows(ph, table, k.src_idx, width=ATT)
    row_stored, logit_in = ph.pair(ph.sem, "row_stored"), ph.pair(ph.sem, "logit_in")
    e, run = k.att_e, ph.sb("run", [P, TH, HEADS])
    peak = ph.sb("peak", [P, 2, HEADS])
    whole = ph.sb("whole", [P, 2, HEADS])
    lone = ph.sb("lone", [P, HEADS])
    reset = ph.sb("reset", [P, T])
    values = ph.sb("values", [P, T])
    wide = ph.sb("wide", [P, 2 * HEADS, P])
    seen = ph.sb("seen", [P, HEADS, P])
    ps_tail, ps_head, ps_sel = ph.ps("ps_tail"), ph.ps("ps_head"), ph.ps("ps_sel")
    link, opened, wide_in, turned, ready, exp_in = (
        ph.sem(n) for n in ("link", "opened", "wide_in", "turned", "ready", "exp_in"))

    with nc.Block() as block:
        @block.sync
        def _(sp):
            sp.sem_inc(ph.entered, 1)

            def body(step):
                through = counter(sp, step)
                for u in range(SLOTS):
                    n = edge_places(step, u)
                    sp.wait_ge(take.here[u], take.all_here(step, u, through))
                    sp.dma_start(k.l_msg[:, cols(step, u, n), :], take.rows[u][:, 0:n, :]).then_inc(row_stored[u], 16)
            steps(sp, STEPS, body)
            for u in range(SLOTS):
                sp.wait_ge(row_stored[u], 16 * STEPS)

        @block.gpsimd
        def _(pool):
            def body(step):
                through = counter(pool, step)
                for u in range(SLOTS):
                    take.gather(pool, step, u, through, (row_stored[u], through(16, 1)), (logit_in[u], through(1, 1)))
            steps(pool, STEPS, body)

        @block.scalar
        def _(act):
            take.first_windows(act)

            def body(step):
                through = counter(act, step)
                for u in range(SLOTS):
                    n = edge_places(step, u)
                    wait_apart(act, ph.entered, (take.here[u], take.all_here(step, u, through)))
                    act.activation(e[:, cols(step, u, n), :], take.rows[u][:, 0:n, D:ATT], ACT.Copy)\
                        .then_inc(logit_in[u], 1)
                    take.next_window(act, step, u, through)
            steps(act, STEPS, body)
            act.wait_ge(ready, 1)
            act.activation(e[:, 0:T, :], e[:, 0:T, :], ACT.Exp).then_inc(exp_in, 1)

        @block.tensor
        def _(pe):
            pe.wait_ge(opened, 1)
            pe.matmul(ps_sel[:, 0:HEADS], k.tail_sel[:, :], k.att_dst[:, T, :], start=True, stop=True)\
                .then_inc(turned, 1)
            pe.wait_ge(wide_in, 1)
            for n in range(2 * HEADS):
                ps = (ps_tail, ps_head)[n // HEADS]
                ins = pe.transpose(ps[:, (n % HEADS) * P:(n % HEADS + 1) * P], wide[:, n, :], k.ident[:, :])
            ins.then_inc(turned, 1)

        @block.vector
        def _(dve):
            done = [0]

            def then(ins):
                done[0] += 1
                ins.then_inc(link, 1)
                dve.wait_ge(link, done[0])

            d = k.att_dst
            then(dve.tensor_copy(reset[:, :], k.cont[:, 0:T]))
            dve.tensor_scalar(reset[:, :], reset[:, :], -1.0, HUGE, ALU.add, ALU.mult).then_inc(opened, 1)
            dve.wait_ge(opened, 1)
            dve.wait_ge(turned, 1)
            then(dve.scalar_tensor_tensor(out=d[:, T - 1, :], in0=d[:, T - 1, :], scalar=k.tail_ended[:, :],
                                          in1=ps_sel[:, 0:HEADS], op0=ALU.mult, op1=ALU.add))
            for h in range(HEADS):
                then(dve.tensor_tensor(values[:, :], d[:, 0:T, h], k.seg_end[:, :], ALU.mult))
                then(dve.tensor_tensor_scan(run[:, 0:T, h][:, ::-1], k.not_end[:, ::-1], values[:, ::-1], 0.0,
                                            ALU.mult, ALU.add))
                then(dve.tensor_tensor(run[:, 0:T, h], run[:, 0:T, h], k.not_head_closed[:, :], ALU.mult))
                then(dve.scalar_tensor_tensor(out=run[:, 0:T, h], in0=k.head_closed[:, :], scalar=d[:, T, h:h + 1],
                                              in1=run[:, 0:T, h], op0=ALU.mult, op1=ALU.add))
            for u in range(SLOTS):
                dve.wait_ge(logit_in[u], STEPS)
            then(dve.tensor_tensor(run[:, 0:T, :], run[:, 0:T, :], e[:, 0:T, :], ALU.add))
            then(dve.scalar_tensor_tensor(out=e[:, 0:T, :], in0=run[:, 0:T, :], scalar=0.2, in1=run[:, 0:T, :],
                                          op0=ALU.mult, op1=ALU.max))
            for h in range(HEADS):
                then(dve.tensor_tensor_scan(run[:, 0:T, h], reset[:, :], e[:, 0:T, h], 0.0, ALU.add, ALU.max))
                then(dve.tensor_copy(peak[:, 0, h:h + 1], run[:, T - 1, h:h + 1]))
                then(dve.tensor_scalar(values[:, :], k.in_head[:, :], -1.0, HUGE, ALU.add, ALU.mult))
                then(dve.tensor_tensor(values[:, :], values[:, :], e[:, 0:T, h], ALU.add))
                then(dve.tensor_reduce(peak[:, 1, h:h + 1], values[:, :], AX.X, ALU.max))
            flat = peak[:, :, :].rearrange("p s h -> p (s h)")
            dve.tensor_copy(wide[:, :, :], flat.unsqueeze(2).to_broadcast([P, 2 * HEADS, P])).then_inc(wide_in, 1)
            dve.wait_ge(turned, 2)
            for mine in range(2):
                for part, ps in enumerate((ps_tail, ps_head)):
                    then(dve.tensor_tensor(seen[:, :, :], ps[:, :].rearrange("p (h q) -> p h q", q=P),
                                           k.apart[:, 2 * mine + part, :].unsqueeze(1).to_broadcast([P, HEADS, P]),
                                           ALU.add))
                    out = whole[:, mine, :] if part == 0 else lone[:, :]
                    then(dve.tensor_reduce(out, seen[:, :, :], AX.X, ALU.max))
                then(dve.tensor_tensor(whole[:, mine, :], whole[:, mine, :], lone[:, :], ALU.max))
            then(dve.tensor_copy(run[:, T - 1, :], whole[:, 0, :]))
            for h in range(HEADS):
                then(dve.tensor_tensor(values[:, :], run[:, 0:T, h], k.seg_end[:, :], ALU.mult))
                then(dve.tensor_tensor_scan(run[:, 0:T, h][:, ::-1], k.not_end[:, ::-1], values[:, ::-1], 0.0,
                                            ALU.mult, ALU.add))
                then(dve.tensor_scalar(values[:, :], k.in_head[:, :], -1.0, -1.0, ALU.add, ALU.mult))
                then(dve.tensor_tensor(run[:, 0:T, h], run[:, 0:T, h], values[:, :], ALU.mult))
                then(dve.scalar_tensor_tensor(out=run[:, 0:T, h], in0=k.in_head[:, :], scalar=whole[:, 1, h:h + 1],
                                              in1=run[:, 0:T, h], op0=ALU.mult, op1=ALU.add))
            dve.tensor_tensor(e[:, 0:T, :], e[:, 0:T, :], run[:, 0:T, :], ALU.subtract).then_inc(ready, 1)
    ph.close()


def rows_from_columns(dve, pe, k, columns, rows, wide, ps, wide_in, turned):
    if dve is not None:
        for n, column in enumerate(columns):
            ins = dve.tensor_copy(wide[:, n, :], column.to_broadcast([D, P]))
        ins.then_inc(wide_in, 1)
        dve.wait_ge(turned, 1)
        for n, row in enumerate(rows):
            dve.tensor_copy(row, ps[:, n * P:n * P + D])
    else:
        pe.wait_ge(wide_in, 1)
        for n in range(len(columns)):
            ins = pe.transpose(ps[:, n * P:n * P + D], wide[:, n, :], k.ident[0:D, 0:D])
        ins.then_inc(turned, 1)


def message_round(nc, a, k):
    ph = Phase(nc, "msg")
    src = Rows(ph, k.t_x3, k.src_idx)
    ph.name = "msg_dst"
    dst = Rows(ph, k.t_x3, k.own_idx, head_too=True)
    ph.name = "msg"
    ef = EdgeFeatures(ph, k, 1)
    src_t, dst_t = ph.pair(ph.sb, "src_t", [D, GROUP]), ph.pair(ph.sb, "dst_t", [D, GROUP])
    feat_t = ph.pair(ph.sb, "feat_t", [D + 1, GROUP])
    rows, across = ph.pair(ph.sb, "rows", [P, J, D]), ph.pair(ph.sb, "across", [D, GROUP])
    acc, cont = ph.pair(ph.sb, "acc", [P, J, D]), ph.pair(ph.sb, "cont", [P, J])
    head_part = ph.sb("head_part", [P, D])
    stat, lone = ph.sb("stat", [D, 2 * STEPS + 1, 6]), ph.sb("lone", [D, TH])
    mv, root, both = ph.sb("mv", [D, 2]), ph.sb("root", [D, 1]), ph.sb("both", [D, 2])
    wide = ph.sb("wide", [D, 2, P])
    ps_s, ps_d, ps_m, ps_z, ps_c = (ph.ps(n) for n in ("ps_s", "ps_d", "ps_m", "ps_z", "ps_c"))
    link = [ph.pair(ph.sem, f"summed{j}_") for j in range(J)]
    (src_turned, dst_turned, src_copied, dst_copied, rows_made, across_made, rows_in, across_in, across_read,
     acc_stored, dst_stored, windows) = (
        ph.pair(ph.sem, n) for n in ("src_turned", "dst_turned", "src_copied", "dst_copied", "rows_made",
                                     "across_made", "rows_in", "across_in", "across_read", "acc_stored",
                                     "dst_stored", "windows"))
    carried, head_here, ones_set, bias_in, stat_in, var_in, rooted, chain, wide_in, wide_turned = (
        ph.sem(n) for n in ("carried", "head_here", "ones_set", "bias_in", "stat_in", "var_in", "rooted", "chain",
                            "wide_in", "wide_turned"))

    def group_before(sems, u, through, n=1):
        return sems[1 - u], through(n, 1) if u == 0 else through(n)

    with nc.Block() as block:
        @block.sync
        def _(sp):
            sp.sem_inc(ph.entered, 1)
            sp.dma_start(k.w_feat[D:D + 1, :], k.msg_bias[0:1, :]).then_inc(bias_in, 16)

            def body(step):
                through = counter(sp, step)
                for u in range(SLOTS):
                    n = edge_places(step, u)
                    sp.wait_ge(dst.here[u], through(16 * J))
                    sp.dma_start(k.l_xd[:, cols(step, u), :], dst.rows[u][:, :, :]).then_inc(dst_stored[u], 16)
                    if u == 0:
                        if not (isinstance(step, int) and step == 0):
                            store(step - 1, 1)
                    else:
                        store(step, 0)

            def store(step, u):
                n = edge_places(step, u)
                sp.wait_ge(link[n - 1][u], counter(sp, step)(1))
                sp.dma_start(k.l_acc[:, cols(step, u, n), :], acc[u][:, 0:n, :]).then_inc(acc_stored[u], 16)
            steps(sp, STEPS, body)
            store(STEPS - 1, 1)
            sp.wait_ge(link[J - 1][1], STEPS)
            sp.dma_start(k.l_acc[:, T:TH, :], acc[1][:, J - 1:J, :]).then_inc(acc_stored[1], 16)
            sp.wait_ge(acc_stored[0], 16 * STEPS)
            sp.wait_ge(acc_stored[1], 16 * STEPS + 16)
            for u in range(SLOTS):
                sp.wait_ge(dst_stored[u], 16 * STEPS)

        @block.gpsimd
        def _(pool):
            def body(step):
                through = counter(pool, step)
                for u in range(SLOTS):
                    src.gather(pool, step, u, through, (src_turned[u], through(1, 1)))
                    dst.gather(pool, step, u, through, (dst_turned[u], through(1, 1)), (dst_stored[u], through(16, 1)))
            steps(pool, STEPS, body)
            pool.wait_ge(acc_stored[0], 16 * STEPS)
            pool.wait_ge(acc_stored[1], 16 * STEPS)
            pool.indirect_dma_start(
                out=head_part[:, :], out_offset=None, in_=k.l_acc.rearrange("p t c -> (p t) c"),
                in_offset=bass.IndirectOffsetOnAxis(ap=k.head_row[:, 0:1], axis=0)).then_inc(head_here, 16)

        @block.scalar
        def _(act):
            src.first_windows(act)
            dst.first_windows(act)

            def front(step, u):
                through = counter(act, step)
                n = edge_places(step, u) * P
                wait_apart(act, ph.entered, (link[J - 1][u], through(1, 1)))
                act.activation(cont[u][:, :], k.cont[:, cols(step, u)], ACT.Copy).then_inc(windows[u], 1)
                ef.take(act, step, u, through)
                act.wait_ge(src_turned[u], through(1))
                wait(act, across_made[u], through(1, 1))
                act.activation(src_t[u][:, 0:n], ps_s[0:D, 0:n], ACT.Copy).then_inc(src_copied[u], 1)
                act.wait_ge(ef.turned[u], through(1))
                wait(act, *group_before(ef.made, u, through))
                act.activation(ef.attr_t[0][:, 0:n], ef.ps_attr[0][0:5, 0:n], ACT.Copy).then_inc(ef.copied[u], 1)
                src.next_window(act, step, u, through)
                dst.next_window(act, step, u, through)

            def back(step, u):
                through = counter(act, step)
                n = edge_places(step, u) * P
                act.wait_ge(ef.made[u], through(1))
                act.activation(feat_t[u][0:D, 0:n], ef.ps_feat[0][0:D, 0:n], ACT.Relu).then_inc(ef.kept[u], 1)
                act.wait_ge(rows_made[u], through(1))
                wait(act, link[J - 1][u], through(1, 1))
                act.activation(rows_of(rows[u][:, :, :])[:, 0:n // P * D], ps_m[:, 0:n // P * D],
                               ACT.Relu).then_inc(rows_in[u], 1)
                act.wait_ge(across_made[u], through(1))
                wait(act, across_read[u], through(1, 1))
                act.activation(across[u][:, 0:n], ps_z[0:D, 0:n], ACT.Relu).then_inc(across_in[u], 1)
            turns(act, front, back)
            column_scale(None, act, None, None, mv, root[:, :], None, None, (var_in, rooted, chain), k, True)

        @block.tensor
        def _(pe):
            pe.wait_ge(ones_set, 1)
            pe.wait_ge(bias_in, 16)

            def front(step, u):
                through = counter(pe, step)
                n = edge_places(step, u)
                pe.wait_ge(src.here[u], src.all_here(step, u, through))
                wait(pe, *group_before(src_copied, u, through))
                for j in range(n):
                    ins = pe.transpose(ps_s[0:D, j * P:(j + 1) * P], src.rows[u][:, j, :], k.ident[:, :])
                ins.then_inc(src_turned[u], 1)
                pe.wait_ge(dst.here[u], through(16 * J))
                wait(pe, *group_before(dst_copied, u, through))
                for j in range(n):
                    ins = pe.transpose(ps_d[0:D, j * P:(j + 1) * P], dst.rows[u][:, j, :], k.ident[:, :])
                ins.then_inc(dst_turned[u], 1)
                wait(pe, *group_before(ef.copied, u, through))
                ef.turn(pe, step, u, through)

            def back(step, u):
                through = counter(pe, step)
                n = edge_places(step, u)
                pe.wait_ge(ef.copied[u], through(1))
                wait(pe, *group_before(ef.kept, u, through))
                pe.matmul(ef.ps_feat[0][0:D, 0:n * P], k.w_edge[:, :], ef.attr_t[0][:, 0:n * P],
                          start=True, stop=True).then_inc(ef.made[u], 1)
                pe.wait_ge(src_copied[u], through(1))
                pe.wait_ge(dst_copied[u], through(1))
                pe.wait_ge(ef.kept[u], through(1))
                wait(pe, *group_before(rows_in, u, through))
                for j in range(n):
                    at = slice(j * P, (j + 1) * P)
                    out = ps_m[:, j * D:(j + 1) * D]
                    pe.matmul(out, src_t[u][:, at], k.w_msg[:, 0, :], start=True, stop=False)
                    pe.matmul(out, dst_t[u][:, at], k.w_msg[:, 1, :], start=False, stop=False)
                    ins = pe.matmul(out, feat_t[u][:, at], k.w_feat[:, :], start=False, stop=True)
                ins.then_inc(rows_made[u], 1)
                wait(pe, *group_before(across_in, u, through))
                pe.matmul(ps_z[0:D, 0:n * P], k.w_msg[:, 0, :], src_t[u][:, 0:n * P], start=True, stop=False)
                pe.matmul(ps_z[0:D, 0:n * P], k.w_msg[:, 1, :], dst_t[u][:, 0:n * P], start=False, stop=False)
                pe.matmul(ps_z[0:D, 0:n * P], k.w_feat[:, :], feat_t[u][:, 0:n * P],
                          start=False, stop=True).then_inc(across_made[u], 1)
                if is_last(step) and u == SLOTS - 1:
                    pe.wait_ge(link[J - 2][u], STEPS)
                    pe.matmul(ps_c[:, 0:D], k.carry_sel[:, :], acc[u][:, J - 2, :], start=True, stop=True)\
                        .then_inc(carried, 1)
            turns(pe, front, back)
            rows_from_columns(None, pe, k, [None] * 2, None, wide, ps_c, wide_in, wide_turned)

        @block.vector
        def _(dve):
            for u in range(SLOTS):
                dve.memset(feat_t[u][D:D + 1, :], 1.0)
            dve.memset(acc[1][:, J - 1, :], 0.0).then_inc(ones_set, 1)
            dve.wait_ge(ones_set, 1)

            def front(step, u):
                through = counter(dve, step)
                n = edge_places(step, u) * P
                dve.wait_ge(dst_turned[u], through(1))
                wait(dve, across_made[u], through(1, 1))
                dve.tensor_copy(dst_t[u][:, 0:n], ps_d[0:D, 0:n]).then_inc(dst_copied[u], 1)

            def back(step, u):
                through = counter(dve, step)
                n = edge_places(step, u)
                dve.wait_ge(rows_in[u], through(1))
                dve.wait_ge(windows[u], through(1))
                wait(dve, acc_stored[u], through(16, 1))
                for j in range(n):
                    if j:
                        dve.wait_ge(link[j - 1][u], through(1))
                        before = acc[u][:, j - 1, :]
                    else:
                        wait(dve, link[J - 1][1 - u], through(1, 1) if u == 0 else through(1))
                        before = acc[1 - u][:, J - 1, :]
                    dve.scalar_tensor_tensor(out=acc[u][:, j, :], in0=before, scalar=cont[u][:, j:j + 1],
                                             in1=rows[u][:, j, :], op0=ALU.mult, op1=ALU.add).then_inc(link[j][u], 1)
                if n < J:
                    dve.wait_ge(carried, 1)
                    dve.wait_ge(head_here, 16)
                    dve.tensor_tensor(acc[u][:, J - 1, :], ps_c[:, 0:D], head_part[:, :],
                                      ALU.add).then_inc(link[J - 1][u], 1)
                wait_apart(dve, ph.entered, (across_in[u], through(1)))
                column_stats(dve, ph, stat, lone, across[u], step, u).then_inc(across_read[u], 1)
            turns(dve, front, back)
            dve.wait_ge(across_read[0], STEPS)
            dve.wait_ge(across_read[1], STEPS)
            dve.bn_stats(stat[:, 2 * STEPS, :], lone[:, 0:LAST]).then_inc(stat_in, 1)
            dve.wait_ge(stat_in, 1)
            dve.bn_aggr(mv[:, :], stat[:, :, :].rearrange("c a s -> c (a s)")).then_inc(var_in, 1)
            column_scale(dve, None, k.l3_cols[:, 4:5], k.l3_cols[:, 5:6], mv, root[:, :], both[:, 0:1],
                         both[:, 1:2], (var_in, rooted, chain), k, False)
            rows_from_columns(dve, None, k, [both[:, 0:1], both[:, 1:2]], [k.msg_scale[:, :], k.msg_shift[:, :]],
                              wide, ps_c, wide_in, wide_turned)
    ph.close()


def node_stats(nc, k):
    ph = Phase(nc, "stats")
    x = ph.pair(ph.sb, "x", [P, J, D])
    xt, across = ph.pair(ph.sb, "xt", [D + 1, GROUP]), ph.pair(ph.sb, "across", [D, GROUP])
    ps_x, ps_z = ph.pair(ph.ps, "ps_x"), ph.pair(ph.ps, "ps_z")
    ps_w = ph.ps("ps_w")
    stat = ph.sb("stat", [D, DENSE_FULL + 1, 6])
    mv, root, both, wide = ph.sb("mv", [D, 2]), ph.sb("root", [D, 1]), ph.sb("both", [D, 2]), ph.sb("wide", [D, 2, P])
    loaded, turned, copied, made, kept, read = (
        ph.pair(ph.sem, n) for n in ("loaded", "turned", "copied", "made", "kept", "read"))
    ones_set, var_in, rooted, chain, wide_in, wide_turned = (
        ph.sem(n) for n in ("ones_set", "var_in", "rooted", "chain", "wide_in", "wide_turned"))

    def width(step, u):
        last = isinstance(step, int) and step == DENSE_STEPS - 1 and u == SLOTS - 1
        return REST if last else P

    with nc.Block() as block:
        @block.sync
        def _(sp):
            sp.sem_inc(ph.entered, 1)

            def body(step):
                through = counter(sp, step)
                for u in range(SLOTS):
                    n = width(step, u)
                    wait(sp, turned[u], through(1, 1))
                    sp.dma_start(x[u][0:n], dense_rows(k.t_x3, step, u, n)).then_inc(loaded[u], 16)
            steps(sp, DENSE_STEPS, body)

        @block.tensor
        def _(pe):
            pe.wait_ge(ones_set, 1)

            def body(step):
                through = counter(pe, step)
                for u in range(SLOTS):
                    n = width(step, u)
                    pe.wait_ge(loaded[u], through(16))
                    wait(pe, copied[u], through(1, 1))
                    for j in range(J):
                        ins = pe.transpose(ps_x[u][0:D, j * n:(j + 1) * n], x[u][0:n, j, :], k.ident[0:n, 0:n])
                    ins.then_inc(turned[u], 1)
                for u in range(SLOTS):
                    n = width(step, u) * J
                    pe.wait_ge(copied[u], through(1))
                    wait(pe, kept[u], through(1, 1))
                    pe.matmul(ps_z[u][0:D, 0:n], k.w_node[:, :], xt[u][:, 0:n], start=True, stop=True)\
                        .then_inc(made[u], 1)
            steps(pe, DENSE_STEPS, body)
            rows_from_columns(None, pe, k, [None] * 2, None, wide, ps_w, wide_in, wide_turned)

        @block.scalar
        def _(act):
            def body(step):
                through = counter(act, step)
                for u in range(SLOTS):
                    n = width(step, u) * J
                    act.wait_ge(turned[u], through(1))
                    wait(act, made[u], through(1, 1))
                    act.activation(xt[u][0:D, 0:n], ps_x[u][0:D, 0:n], ACT.Copy).then_inc(copied[u], 1)
                for u in range(SLOTS):
                    n = width(step, u) * J
                    act.wait_ge(made[u], through(1))
                    wait(act, read[u], through(1, 1))
                    act.activation(across[u][:, 0:n], ps_z[u][0:D, 0:n], ACT.Relu).then_inc(kept[u], 1)
            steps(act, DENSE_STEPS, body)
            column_scale(None, act, None, None, mv, root[:, :], None, None, (var_in, rooted, chain), k, True)

        @block.vector
        def _(dve):
            for u in range(SLOTS):
                ins = dve.memset(xt[u][D:D + 1, :], 1.0)
            ins.then_inc(ones_set, 1)
            def body(step):
                through = counter(dve, step)
                for u in range(SLOTS):
                    n = width(step, u) * J
                    wait_apart(dve, ph.entered, (kept[u], through(1)))
                    dve.bn_stats(stat[:, bass.ds(step * SLOTS + u, 1), :].rearrange("c a s -> c (a s)"),
                                 across[u][:, 0:n]).then_inc(read[u], 1)
            steps(dve, DENSE_STEPS, body)
            dve.wait_ge(read[0], DENSE_STEPS)
            dve.wait_ge(read[1], DENSE_STEPS)
            dve.bn_aggr(mv[:, :], stat[:, :, :].rearrange("c a s -> c (a s)")).then_inc(var_in, 1)
            column_scale(dve, None, k.l3_cols[:, 0:1], k.l3_cols[:, 1:2], mv, root[:, :], both[:, 0:1],
                         both[:, 1:2], (var_in, rooted, chain), k, False)
            rows_from_columns(dve, None, k, [both[:, 0:1], both[:, 1:2]], [k.node_scale[:, :], k.node_shift[:, :]],
                              wide, ps_w, wide_in, wide_turned)
    ph.close()


def output_pass(nc, k, out, edges):
    ph = Phase(nc, "out_edges" if edges else "out_dense")
    count = STEPS if edges else DENSE_STEPS
    put = Rows(ph, None, None, out, k.out_idx) if edges else None
    x, y_scaled, z, c, new = (ph.pair(ph.sb, n, [P, J, D]) for n in ("x", "y_scaled", "z", "c", "new"))
    xt = ph.pair(ph.sb, "xt", [D + 1, GROUP])
    ps_x, ps_y = ph.pair(ph.ps, "ps_x"), ph.pair(ph.ps, "ps_y")
    norm = Norm(ph, "norm")
    loaded, turned, copied, made, scaled_in, shifted, z_in, c_in, new_in, stored = (
        ph.pair(ph.sem, n) for n in ("loaded", "turned", "copied", "made", "scaled_in", "shifted", "z_in", "c_in",
                                     "new_in", "stored"))
    ones_set = ph.sem("ones_set")
    if edges:
        sums, sums_in = ph.pair(ph.sb, "sums", [P, J, D]), ph.pair(ph.sem, "sums_in")
        parts = ph.pair(ph.sb, "parts", [P, J, D])
        part_a, part_b, part_c, placed = (ph.pair(ph.sem, n) for n in ("part_a", "part_b", "part_c", "placed"))

    def rows_in(step, u):
        last = not edges and isinstance(step, int) and step == DENSE_STEPS - 1 and u == SLOTS - 1
        return REST if last else P

    def every_place(row, n):
        return row[0:n, :].unsqueeze(1).to_broadcast([n, J, D])

    with nc.Block() as block:
        @block.sync
        def _(sp):
            sp.sem_inc(ph.entered, 1)

            def body(step):
                through = counter(sp, step)
                for u in range(SLOTS):
                    n = rows_in(step, u)
                    wait(sp, z_in[u], through(1, 1))
                    if edges:
                        sp.dma_start(sums[u][:, :, :], k.l_acc[:, cols(step, u), :]).then_inc(sums_in[u], 16)
                        sp.dma_start(x[u][:, :, :], k.l_xd[:, cols(step, u), :]).then_inc(loaded[u], 16)
                    else:
                        sp.dma_start(x[u][0:n], dense_rows(k.t_x3, step, u, n)).then_inc(loaded[u], 16)
                if not edges:
                    for u in range(SLOTS):
                        n = rows_in(step, u)
                        sp.wait_ge(new_in[u], through(1))
                        sp.dma_start(dense_rows(out, step, u, n), new[u][0:n]).then_inc(stored[u], 16)
            steps(sp, count, body)
            if not edges:
                for u in range(SLOTS):
                    sp.wait_ge(stored[u], 16 * count)

        @block.gpsimd
        def _(pool):
            if edges:
                bound = pool.to_reg(N - 1)

                def body(step):
                    through = counter(pool, step)
                    for u in range(SLOTS):
                        put.scatter(pool, new[u], u, through, new_in[u], bound)
                steps(pool, count, body)
                for u in range(SLOTS):
                    pool.wait_ge(put.gone[u], 16 * J * count)

        @block.tensor
        def _(pe):
            pe.wait_ge(ones_set, 1)

            def body(step):
                through = counter(pe, step)
                for u in range(SLOTS):
                    n = rows_in(step, u)
                    pe.wait_ge(loaded[u], through(16))
                    wait(pe, copied[u], through(1, 1))
                    for j in range(J):
                        ins = pe.transpose(ps_x[u][0:D, j * P:j * P + n], x[u][0:n, j, :], k.ident[0:n, 0:n])
                    ins.then_inc(turned[u], 1)
                for u in range(SLOTS):
                    n = rows_in(step, u)
                    pe.wait_ge(copied[u], through(1))
                    wait(pe, scaled_in[u], through(1, 1))
                    for j in range(J):
                        ins = pe.matmul(ps_y[u][0:n, j * D:(j + 1) * D], xt[u][:, j * P:j * P + n], k.w_node[:, :],
                                        start=True, stop=True)
                    ins.then_inc(made[u], 1)
            steps(pe, count, body)

        @block.scalar
        def _(act):
            def body(step):
                through = counter(act, step)
                for u in range(SLOTS):
                    n = rows_in(step, u)
                    act.wait_ge(turned[u], through(1))
                    wait(act, made[u], through(1, 1))
                    if n == P:
                        act.activation(xt[u][0:D, :], ps_x[u][0:D, :], ACT.Copy).then_inc(copied[u], 1)
                    else:
                        for j in range(J):
                            ins = act.activation(xt[u][0:D, j * P:j * P + n], ps_x[u][0:D, j * P:j * P + n], ACT.Copy)
                        ins.then_inc(copied[u], 1)
                for u in range(SLOTS):
                    if edges:
                        put.put_window(act, step, u, through)
                    norm.take_root(act, u, through, 1.0, k.eps[0:rows_in(step, u), :], rows_in(step, u))
            steps(act, count, body)

        @block.vector
        def _(dve):
            for u in range(SLOTS):
                ins = dve.memset(xt[u][D:D + 1, :], 1.0)
            ins.then_inc(ones_set, 1)
            def body(step):
                through = counter(dve, step)
                us = [(u, rows_in(step, u)) for u in range(SLOTS)]
                for u, n in us:
                    if edges:
                        dve.tensor_tensor(parts[u][:, :, :], over_rows(k.cnt[:, cols(step, u)], D),
                                          every_place(k.msg_shift, P), ALU.mult).then_inc(part_a[u], 1)
                        dve.wait_ge(sums_in[u], through(16))
                        dve.tensor_tensor(sums[u][:, :, :], sums[u][:, :, :], every_place(k.msg_scale, P),
                                          ALU.mult).then_inc(part_b[u], 1)
                        dve.wait_ge(part_a[u], through(1))
                        dve.wait_ge(part_b[u], through(1))
                        dve.tensor_tensor(parts[u][:, :, :], parts[u][:, :, :], sums[u][:, :, :],
                                          ALU.add).then_inc(part_c[u], 1)
                    dve.wait_ge(loaded[u], through(16))
                    wait(dve, c_in[u], through(1, 1))
                    dve.tensor_tensor(c[u][0:n], x[u][0:n], every_place(k.node_shift, n), ALU.add)\
                        .then_inc((placed if edges else shifted)[u], 1)
                    dve.wait_ge(made[u], through(1))
                    dve.scalar_tensor_tensor(
                        out=y_scaled[u][0:n], in0=ps_y[u][0:n, 0:J * D].rearrange("p (j c) -> p j c", c=D), scalar=0.0,
                        in1=every_place(k.node_scale, n), op0=ALU.max, op1=ALU.mult).then_inc(scaled_in[u], 1)
                    if edges:
                        dve.wait_ge(placed[u], through(1))
                        dve.wait_ge(part_c[u], through(1))
                        dve.tensor_tensor(c[u][:, :, :], c[u][:, :, :], parts[u][:, :, :], ALU.add)\
                            .then_inc(shifted[u], 1)
                for u, n in us:
                    dve.wait_ge(shifted[u], through(1))
                    dve.wait_ge(scaled_in[u], through(1))
                    dve.tensor_tensor(z[u][0:n], c[u][0:n], y_scaled[u][0:n], ALU.add).then_inc(z_in[u], 1)
                for u, n in us:
                    dve.wait_ge(z_in[u], through(1))
                    norm.spread(dve, u, z[u][0:n], through, n)
                for u, n in us:
                    dve.wait_ge(norm.var_in[u], through(1))
                    dve.tensor_tensor(c[u][0:n], z[u][0:n], norm.mean(u, n), ALU.subtract).then_inc(c_in[u], 1)
                for u, n in us:
                    norm.invert(dve, u, through, n)
                    dve.wait_ge(c_in[u], through(1))
                    wait(dve, (put.gone if edges else stored)[u], through(16 * J if edges else 16, 1))
                    dve.tensor_tensor(new[u][0:n], c[u][0:n], norm.inverse(u, n), ALU.mult).then_inc(new_in[u], 1)
            steps(dve, count, body)
    ph.close()


class Kept:

    def __init__(self, nc, stack):
        def sb(name, shape, dt=F32):
            return stack.enter_context(nc.sbuf_tensor(name, shape, dt))

        def dram(name, shape):
            return nc.dram_tensor(name, shape, F32).ap()

        self.src_idx, self.own_idx, self.out_idx = (sb(n, [P, TH], I32) for n in ("src_idx", "own_idx", "out_idx"))
        self.head_row = sb("head_row", [P, 1], I32)
        self.cont, self.cnt, self.dinv = (sb(n, [P, TH]) for n in ("cont", "cnt", "dinv"))
        self.in_head, self.seg_end, self.not_end, self.head_closed, self.not_head_closed = (
            sb(n, [P, T]) for n in ("in_head", "seg_end", "not_end", "head_closed", "not_head_closed"))
        self.tail_ended, self.eps = sb("tail_ended", [P, 1]), sb("eps", [P, 1])
        self.carry_sel, self.tail_sel, self.ident = (sb(n, [P, P]) for n in ("carry_sel", "tail_sel", "ident"))
        self.apart = sb("apart", [P, 4, P])
        self.att_dst, self.att_e = sb("att_dst", [P, TH, HEADS]), sb("att_e", [P, TH, HEADS])
        self.edge_in = sb("edge_in", [P, TH, 5])
        self.w_gcn = [sb(f"w_gcn{i}", [D + 1, D]) for i in range(2)]
        self.w_self = [sb(f"w_self{i}", [D + 1, D]) for i in range(2)]
        self.w_agg = [sb(f"w_agg{i}", [D + 1, D]) for i in range(2)]
        self.w_att = [sb(f"w_att{i}", [D, ATT_ALL]) for i in range(3)]
        self.gat_bias = sb("gat_bias", [D, 3])
        self.gat_bias_row, self.gat_rest_row = sb("gat_bias_row", [P, D]), sb("gat_rest_row", [P, D])
        self.wide_bias = sb("wide_bias", [D, 2, P])
        self.att_rest = [sb(f"att_rest{i}", [P, J, ATT]) for i in range(2)]
        self.w_node, self.w_edge = sb("w_node", [D + 1, D]), sb("w_edge", [5, D])
        self.w_msg, self.w_feat = sb("w_msg", [D, 3, D]), sb("w_feat", [D + 1, D])
        self.l3_cols, self.edge_scale, self.msg_bias = sb("l3_cols", [D, 8]), sb("edge_scale", [D, 1]), sb("msg_bias", [1, D])
        self.msg_scale, self.msg_shift, self.node_scale, self.node_shift = (
            sb(n, [P, D]) for n in ("msg_scale", "msg_shift", "node_scale", "node_shift"))
        self.t_x, self.t_h1, self.t_x1, self.t_y1, self.t_x3 = (
            dram(n, (N, D)) for n in ("t_x", "t_h1", "t_x1", "t_y1", "t_x3"))
        self.t_att = [dram(f"t_att{i}", (N, ATT)) for i in range(3)]
        self.l_x, self.l_s, self.l_h1, self.l_x1, self.l_y1, self.l_x2, self.l_xd, self.l_acc = (
            dram(n, (P, TH, D)) for n in ("l_x", "l_s", "l_h1", "l_x1", "l_y1", "l_x2", "l_xd", "l_acc"))
        self.l_msg, self.l_acc100 = dram("l_msg", (P, TH, ATT)), dram("l_acc100", (P, TH, ATT))


def gnn_resnorm(nc, a, out):
    with ExitStack() as stack:
        k = Kept(nc, stack)
        prepare(nc, a, k)
        dense_chain(nc, a, k)
        own_rows(nc, a, k)
        node_round(nc, a, k, GCN1, k.t_x, k.t_h1, own=k.l_s, keep=k.l_h1, layer=0)
        node_round(nc, a, k, GCN2, k.t_h1, k.t_x1, own=k.l_h1, rest=k.l_x, keep=k.l_x1, layer=1)
        node_round(nc, a, k, SAGE1, k.t_x1, k.t_y1, own=k.l_x1, keep=k.l_y1, layer=0)
        node_round(nc, a, k, SAGE2, k.t_y1, k.t_att[0], own=k.l_y1, rest=k.l_x1, keep=k.l_x2, layer=1)
        attention_weights(nc, k, k.t_att[0], 0)
        node_round(nc, a, k, GAT1, out=k.t_att[1], layer=0)
        attention_weights(nc, k, k.t_att[1], 1)
        node_round(nc, a, k, GAT2, out=k.t_att[2], layer=1)
        attention_weights(nc, k, k.t_att[2], 2)
        node_round(nc, a, k, GAT3, out=k.t_x3, rest=k.l_x2, layer=2)
        node_stats(nc, k)
        message_round(nc, a, k)
        output_pass(nc, k, out, edges=False)
        output_pass(nc, k, out, edges=True)


_INS = ["x", "src", "dst", "edge_attr_4", "L0_gnn_W1", "L0_gnn_b1", "L0_gnn_W2", "L0_gnn_b2", "L1_gnn_W0", "L1_gnn_b0",
        "L1_gnn_W1", "L1_gnn_b1", "L1_gnn_W2", "L1_gnn_b2", "L2_gnn_W", "L2_gnn_att_src", "L2_gnn_att_dst",
        "L2_gnn_bias", "L3_gnn_W_node", "L3_gnn_b_node", "L3_gnn_g_node", "L3_gnn_beta_node", "L3_gnn_W_edge",
        "L3_gnn_b_edge", "L3_gnn_g_edge", "L3_gnn_beta_edge", "L3_gnn_W_msg", "L3_gnn_b_msg", "L3_gnn_g_msg",
        "L3_gnn_beta_msg"]


def kernel(**inputs):
    import concourse.bacc as bacc
    from concourse.bass_utils import run_bass_kernel_spmd as run

    nc = bacc.Bacc("TRN2", target_bir_lowering=False, num_devices=1)
    arrays, args = {}, {}
    for name in _INS:
        array = np.ascontiguousarray(inputs[name])
        arrays[f"in_{name}"] = array
        args[name] = nc.dram_tensor(f"in_{name}", array.shape, mybir.dt.from_np(array.dtype), kind="ExternalInput").ap()
    out = nc.dram_tensor("out_rows", (N, D), F32, kind="ExternalOutput").ap()
    gnn_resnorm(nc, args, out)
    return run(nc, [arrays], core_ids=[0]).results[0]["out_rows"]
```

```python
import numpy as np
import concourse.bass as bass
from concourse import mybir
from contextlib import ExitStack

F32, I32 = mybir.dt.float32, mybir.dt.int32
ALU, ACT, AX = mybir.AluOpType, mybir.ActivationFunctionType, mybir.AxisListType

P = 128
N, E, D = 100000, 50000, 96
HEADS, CH = 4, 24
ATT = D + HEADS
ATT_ALL = ATT + HEADS
T = -(-E // P)
TH = T + 1
LAST = E - (P - 1) * T
J = 4
SLOTS = 2
STEPS = TH // (J * SLOTS)
assert STEPS * J * SLOTS == TH
FAR = 1 << 20
GROUP = P * J
DENSE_FULL = N // GROUP
REST = (N - DENSE_FULL * GROUP) // J
assert REST * J + DENSE_FULL * GROUP == N
DENSE_SLOTS = 4
assert DENSE_FULL + 1 == DENSE_SLOTS * STEPS
EPS = 1e-5
HUGE = 1.0e30


def steps(eng, count, body):
    body(0)
    body(1)
    with eng.Fori(2, count - 1) as step:
        body(step)
    body(count - 1)


def counter(eng, step):
    known = {}

    def through(n, back=0, short=0):
        if isinstance(step, int):
            return n * (step + 1 - back) - short
        if (n, back, short) not in known:
            known[n, back, short] = eng.to_reg(step * n + (n * (1 - back) - short))
        return known[n, back, short]
    return through


def wait(eng, sem, value):
    if not (isinstance(value, int) and value <= 0):
        eng.wait_ge(sem, value)


def wait_apart(eng, entered, *waits):
    eng.wait_ge(entered, 1)
    for sem, value in waits:
        wait(eng, sem, value)


def cols(step, slot, count=J, skip=0):
    return bass.ds(step * (J * SLOTS) + (J * slot + skip), count)


def over_rows(column_tile, width):
    return column_tile.unsqueeze(2).to_broadcast([column_tile.shape[0], column_tile.shape[1], width])


def group_before(sems, u, through, n=1):
    slots = len(sems)
    return sems[(u - 1) % slots], through(n, 1) if u == 0 else through(n)


def turns(eng, front, back):
    def body(step):
        first = isinstance(step, int) and step == 0
        front(step, 0)
        if not first:
            back(step - 1, 1)
        front(step, 1)
        back(step, 0)
    steps(eng, STEPS, body)
    back(STEPS - 1, 1)



def shared_turns(eng, front, back, tail, dense_front, dense_back):
    def body(step):
        first = isinstance(step, int) and step == 0
        front(step, 0)
        if not first:
            back(step - 1, 1)
        if dense_front:
            dense_front(eng, step)
        if tail and not first:
            tail(step - 1, 1)
        front(step, 1)
        back(step, 0)
        if dense_back:
            dense_back(eng, step)
        if tail:
            tail(step, 0)
    steps(eng, STEPS, body)
    back(STEPS - 1, 1)
    if tail:
        tail(STEPS - 1, 1)


class Phase:

    def __init__(self, nc, name):
        self.nc, self.name, self.stack, self.sems = nc, name, ExitStack(), []
        self.entered = self.sem("entered")

    def sb(self, name, shape, dt=F32):
        return self.stack.enter_context(self.nc.sbuf_tensor(f"{self.name}_{name}", shape, dt))

    def ps(self, name, shape=(P, 512)):
        return self.stack.enter_context(self.nc.psum_tensor(f"{self.name}_{name}", list(shape), F32))

    def sem(self, name):
        s = self.nc.alloc_semaphore(f"{self.name}_{name}")
        self.sems.append(s)
        return s

    def pair(self, make, name, *args):
        return [make(f"{name}{u}", *args) for u in range(SLOTS)]

    def part(self, name):
        part = Phase.__new__(Phase)
        part.nc, part.name, part.stack, part.sems, part.entered = self.nc, name, self.stack, self.sems, self.entered
        return part

    def close(self):
        self.stack.close()
        self.nc.clear_and_free_semaphores(self.sems)
        self.nc.all_engine_barrier()


def prepare(nc, a, k):
    ph = Phase(nc, "prep")
    dst_i = ph.sb("dst_i", [P, T], I32)
    prev_i, next_i = ph.sb("prev_i", [P, 1], I32), ph.sb("next_i", [P, 1], I32)
    blank = ph.sb("blank", [P, ATT])
    dst, attr = ph.sb("dst", [P, T]), ph.sb("attr", [P, T, 4])
    prev_tail, next_head = ph.sb("prev_tail", [P, 1]), ph.sb("next_head", [P, 1])
    is_end, valid, tmp = ph.sb("is_end", [P, T]), ph.sb("valid", [P, T]), ph.sb("tmp", [P, T])
    linked, head_ends, head_len = ph.sb("linked", [P, 1]), ph.sb("head_ends", [P, 1]), ph.sb("head_len", [P, 1])
    ones = ph.sb("ones", [P, T])
    row_base = ph.sb("row_base", [P, 1])
    wide = ph.sb("wide", [P, 2, P])
    head_of, tail_of = ph.sb("head_of", [P, P]), ph.sb("tail_of", [P, P])
    later, earlier = ph.sb("later", [P, P]), ph.sb("earlier", [P, P])
    head_out = ph.sb("head_out", [P, 1])
    w1b = ph.sb("w1b", [D + 1, 2, D])
    w0b = ph.sb("w0b", [D + 1, 2, D])
    w2 = ph.sb("w2", [D, 2, 2, D])
    b2 = ph.sb("b2", [1, 2, D])
    bias_at = ph.sb("bias_at", [1, D + 1])
    w_gat = ph.sb("w_gat", [D, 3, D])
    att = ph.sb("att", [D, 3, 2 * HEADS])
    turned = ph.sb("turned", [D, 7, D + 1])
    ps_a, ps_b, ps_c, ps_d = (ph.ps(f"ps{n}") for n in range(4))
    ps_w = [ph.ps("psw0"), ph.ps("psw1")]

    cleared, loaded, masks = ph.sem("cleared"), ph.sem("loaded"), ph.sem("masks")
    link, broad, spread, counted, carried = (ph.sem(n) for n in ("link", "broad", "spread", "counted", "carried"))
    root_in, root_out = ph.sem("root_in"), ph.sem("root_out")
    w_turn, w_copied, w_made, w_kept = (ph.sem(n) for n in ("w_turn", "w_copied", "w_made", "w_kept"))
    loads = [0]

    with nc.Block() as block:
        @block.sync
        def _(sp):
            def load(out, in_):
                with nc.allow_non_contiguous_dma(reason="a few columns of weights and indices"):
                    sp.dma_start(out, in_).then_inc(loaded, 16)
                loads[0] += 16

            sp.wait_ge(cleared, 1)
            load(k.l_acc[:, T, :], blank[:, 0:D])
            load(k.l_acc100[:, T, :], blank[:, :])
            d = a["dst"]
            load(dst_i[0:P - 1, :], d[0:(P - 1) * T].rearrange("(p t) -> p t", t=T))
            load(dst_i[P - 1:P, 0:LAST], d[(P - 1) * T:E].unsqueeze(0))
            load(k.src_idx[0:P - 1, 0:T], a["src"][0:(P - 1) * T].rearrange("(p t) -> p t", t=T))
            load(k.src_idx[P - 1:P, 0:LAST], a["src"][(P - 1) * T:E].unsqueeze(0))
            load(prev_i[1:P, :], d[0:(P - 1) * T].rearrange("(p t) -> p t", t=T)[:, T - 1:T])
            load(next_i[0:P - 2, :], d[T:(P - 1) * T].rearrange("(p t) -> p t", t=T)[:, 0:1])
            load(next_i[P - 2:P - 1, :], d[(P - 1) * T:(P - 1) * T + 1].unsqueeze(0))
            e = a["edge_attr_4"]
            load(attr[0:P - 1, :, :], e[0:(P - 1) * T, :].rearrange("(p t) c -> p t c", t=T))
            load(attr[P - 1:P, 0:LAST, :], e[(P - 1) * T:E, :].unsqueeze(0))
            for n, name in enumerate(("1", "2")):
                load(k.w_gcn[n][0:D, :], a[f"L0_gnn_W{name}"])
                load(k.w_gcn[n][D:D + 1, :], a[f"L0_gnn_b{name}"].unsqueeze(0))
            for i in range(2):
                load(w1b[0:D, i, :], a["L1_gnn_W1"][i])
                load(w1b[D:D + 1, i, :], a["L1_gnn_b1"][i:i + 1, :])
                load(w0b[0:D, i, :], a["L1_gnn_W0"][i])
                load(w0b[D:D + 1, i, :], a["L1_gnn_b0"][i:i + 1, :])
                load(w2[:, i, :, :], a["L1_gnn_W2"][i].rearrange("(s c) n -> c s n", c=D))
                load(b2[0:1, i, :], a["L1_gnn_b2"][i:i + 1, :])
            for i in range(3):
                load(w_gat[:, i, :], a["L2_gnn_W"][i])
                for s, name in enumerate(("L2_gnn_att_src", "L2_gnn_att_dst")):
                    for h in range(HEADS):
                        load(att[h * CH:(h + 1) * CH, i, HEADS * s + h:HEADS * s + h + 1],
                             a[name][i, h:h + 1, :].rearrange("a c -> c a"))
                load(k.gat_bias[:, i:i + 1], a["L2_gnn_bias"][i:i + 1, :].rearrange("a c -> c a"))
            load(k.gat_bias_row[:, :], a["L2_gnn_bias"][2:3, :].to_broadcast([P, D]))
            load(k.w_node[0:D, :], a["L3_gnn_W_node"])
            load(k.w_node[D:D + 1, :], a["L3_gnn_b_node"].unsqueeze(0))
            load(k.w_edge[0:4, :], a["L3_gnn_W_edge"])
            load(k.w_edge[4:5, :], a["L3_gnn_b_edge"].unsqueeze(0))
            load(k.w_msg[:, :, :], a["L3_gnn_W_msg"].rearrange("(s c) n -> c s n", c=D))
            for n, name in enumerate(("L3_gnn_g_node", "L3_gnn_beta_node", "L3_gnn_g_edge", "L3_gnn_beta_edge",
                                      "L3_gnn_g_msg", "L3_gnn_beta_msg")):
                load(k.l3_cols[:, n:n + 1], a[name].unsqueeze(1))
            load(k.msg_bias[0:1, :], a["L3_gnn_b_msg"].unsqueeze(0))

        @block.gpsimd
        def _(pool):
            pool.memset(dst_i[:, :], FAR)
            pool.memset(k.src_idx[:, :], 0)
            pool.memset(prev_i[:, :], -1)
            pool.memset(next_i[:, :], -2)
            pool.memset(att[:, :, :], 0.0)
            pool.memset(blank[:, :], 0.0)
            pool.memset(attr[:, :, :], 0.0)
            pool.memset(k.edge_in[:, :, 4:5], 1.0).then_inc(cleared, 1)
            pool.memset(ones[:, :], 1.0)
            pool.memset(k.cont[:, :], 0.0)
            pool.memset(k.cnt[:, :], 0.0)
            pool.memset(k.ident[:, :], 0.0)
            pool.memset(later[:, :], 1.0)
            pool.memset(earlier[:, :], 1.0)
            pool.memset(bias_at[:, 0:D], 0.0)
            pool.memset(bias_at[:, D:D + 1], 1.0)
            pool.memset(k.eps[:, :], EPS)
            pool.iota(row_base[:, :], pattern=[[0, 1]], base=-1, channel_multiplier=TH,
                      allow_small_or_imprecise_dtypes=True).then_inc(masks, 1)
            pool.wait_ge(masks, 1)
            pool.affine_select(out=k.ident[:, :], in_=k.ident[:, :], compare_op=ALU.not_equal, fill=1.0,
                               base=0, pattern=[[-1, P]], channel_multiplier=1)
            pool.affine_select(out=later[:, :], in_=later[:, :], compare_op=ALU.is_gt, fill=0.0,
                               base=0, pattern=[[1, P]], channel_multiplier=-1)
            pool.affine_select(out=earlier[:, :], in_=earlier[:, :], compare_op=ALU.is_gt, fill=0.0,
                               base=0, pattern=[[-1, P]], channel_multiplier=1).then_inc(masks, 1)

        @block.vector
        def _(dve):
            done = [0]

            def then(ins):
                done[0] += 1
                ins.then_inc(link, 1)
                dve.wait_ge(link, done[0])

            dve.wait_ge(loaded, loads[0])
            dve.wait_ge(masks, 2)
            then(dve.tensor_copy(dst[:, :], dst_i[:, :]))
            dve.tensor_copy(k.edge_in[:, 0:T, 0:4], attr[:, :, :])
            then(dve.tensor_copy(prev_tail[:, :], prev_i[:, :]))
            then(dve.tensor_copy(next_head[:, :], next_i[:, :]))
            head, tail = dst[:, 0:1], dst[:, T - 1:T]
            then(dve.tensor_tensor(k.cont[:, 1:T], dst[:, 1:T], dst[:, 0:T - 1], ALU.is_equal))
            then(dve.tensor_scalar(is_end[:, 0:T - 1], k.cont[:, 1:T], -1.0, 1.0, ALU.mult, ALU.add))
            then(dve.tensor_tensor(is_end[:, T - 1:T], tail, next_head[:, :], ALU.not_equal))
            then(dve.tensor_copy(k.tail_ended[:, :], is_end[:, T - 1:T]))
            then(dve.tensor_scalar(k.in_head[:, :], dst[:, :], head, None, ALU.is_equal))
            then(dve.tensor_tensor(linked[:, :], prev_tail[:, :], head, ALU.is_equal))
            then(dve.tensor_tensor(tmp[:, :], is_end[:, :], k.in_head[:, :], ALU.mult))
            then(dve.tensor_reduce(head_ends[:, :], tmp[:, :], AX.X, ALU.max))
            then(dve.tensor_tensor(head_out[:, :], head_ends[:, :], linked[:, :], ALU.mult))
            then(dve.tensor_scalar(tmp[:, :], k.in_head[:, :], linked[:, :], -1.0, ALU.mult, ALU.mult))
            then(dve.tensor_scalar(tmp[:, :], tmp[:, :], 1.0, None, ALU.add))
            then(dve.tensor_tensor(valid[:, :], is_end[:, :], tmp[:, :], ALU.mult))
            then(dve.scalar_tensor_tensor(out=tmp[:, :], in0=dst[:, :], scalar=float(-FAR), in1=valid[:, :],
                                          op0=ALU.add, op1=ALU.mult))
            then(dve.tensor_scalar(k.out_idx[:, 0:T], tmp[:, :], float(FAR), None, ALU.add))
            then(dve.scalar_tensor_tensor(out=tmp[:, 0:1], in0=head, scalar=float(-FAR), in1=head_out[:, :],
                                          op0=ALU.add, op1=ALU.mult))
            then(dve.tensor_scalar(k.out_idx[:, T:TH], tmp[:, 0:1], float(FAR), None, ALU.add))
            then(dve.tensor_scalar(k.own_idx[:, 0:T], dst[:, :], float(N - 1), None, ALU.min))
            then(dve.tensor_copy(k.own_idx[:, T:TH], head))
            then(dve.tensor_reduce(head_len[:, :], k.in_head[:, :], AX.X, ALU.add))
            then(dve.tensor_tensor(k.head_row[:, :], head_len[:, :], row_base[:, :], ALU.add))
            then(dve.tensor_tensor_scan(k.cnt[:, 0:T], k.cont[:, 0:T], ones[:, :], 0.0, ALU.mult, ALU.add))
            then(dve.tensor_copy(wide[:, 0, :], head.to_broadcast([P, P])))
            dve.tensor_copy(wide[:, 1, :], tail.to_broadcast([P, P])).then_inc(broad, 1)
            dve.wait_ge(spread, 1)
            then(dve.tensor_copy(head_of[:, :], ps_a[:, 0:P]))
            then(dve.tensor_copy(tail_of[:, :], ps_a[:, P:2 * P]))
            then(dve.tensor_scalar(k.carry_sel[:, :], head_of[:, :], tail, None, ALU.is_equal))
            dve.tensor_tensor(k.carry_sel[:, :], k.carry_sel[:, :], later[:, :], ALU.mult).then_inc(counted, 1)
            dve.wait_ge(counted, 1)
            then(dve.tensor_scalar(k.tail_sel[:, :], tail_of[:, :], head, head_out[:, :], ALU.is_equal, ALU.mult))
            then(dve.tensor_tensor(k.tail_sel[:, :], k.tail_sel[:, :], earlier[:, :], ALU.mult))
            for n, (of, mine) in enumerate(((tail_of, tail), (head_of, tail), (tail_of, head), (head_of, head))):
                then(dve.tensor_scalar(k.apart[:, n, :], of[:, :], mine, None, ALU.is_equal))
                then(dve.tensor_scalar(k.apart[:, n, :], k.apart[:, n, :], -1.0, HUGE, ALU.add, ALU.mult))
            then(dve.tensor_copy(k.seg_end[:, :], is_end[:, :]))
            then(dve.memset(k.seg_end[:, T - 1:T], 1.0))
            then(dve.tensor_scalar(k.not_end[:, :], k.seg_end[:, :], -1.0, 1.0, ALU.mult, ALU.add))
            then(dve.tensor_scalar(k.head_closed[:, :], k.in_head[:, :], head_out[:, :], None, ALU.mult))
            then(dve.tensor_scalar(k.not_head_closed[:, :], k.head_closed[:, :], -1.0, 1.0, ALU.mult, ALU.add))
            dve.wait_ge(carried, 1)
            then(dve.tensor_tensor(k.cnt[:, T:TH], ps_b[:, 0:1], head_len[:, :], ALU.add))
            dve.tensor_copy(k.dinv[:, :], k.cnt[:, :]).then_inc(root_in, 1)
            dve.wait_ge(root_out, 1)
            then(dve.reciprocal(k.dinv[:, :], k.dinv[:, :]))
            for n in range(7):
                dve.wait_ge(w_turn, n + 1)
                dve.tensor_copy(turned[:, n, :], ps_w[n % 2][0:D, 0:D + 1]).then_inc(w_copied, 1)
            outs = [k.w_self[0], k.w_agg[0], k.w_self[1], k.w_agg[1]]
            for n in range(4):
                dve.wait_ge(w_made, n + 1)
                dve.tensor_copy(outs[n][:, :], (ps_c, ps_d)[n % 2][0:D + 1, 0:D]).then_inc(w_kept, 1)
            for n in range(3):
                dve.wait_ge(w_made, 5 + n)
                then(dve.tensor_copy(k.w_att[n][:, 0:D], w_gat[:, n, :]))
                dve.tensor_copy(k.w_att[n][:, D:ATT_ALL], (ps_c, ps_d)[n % 2][0:D, 0:2 * HEADS]).then_inc(w_kept, 1)
            dve.wait_ge(w_kept, 7)
            for n in range(2):
                dve.tensor_scalar(turned[:, n, 0:1], k.gat_bias[:, n:n + 1], 0.0, None, ALU.max)
            then(dve.tensor_scalar(k.gat_rest_row[:, :], k.gat_bias_row[:, :], 0.0, None, ALU.max))
            for n in range(2):
                dve.tensor_copy(k.wide_bias[:, n, :], turned[:, n, 0:1].to_broadcast([D, P])).then_inc(broad, 1)
            dve.wait_ge(spread, 3)
            for n in range(2):
                for j in range(J):
                    then(dve.tensor_copy(k.att_rest[n][:, j, :], ps_w[n][:, 0:ATT]))

        @block.scalar
        def _(act):
            act.dma_start(k.t_x[:, :].rearrange("(p n) c -> p (n c)", p=80),
                          a["x"].rearrange("(p n) c -> p (n c)", p=80)).then_inc(k.base_copied, 16)
            act.wait_ge(root_in, 1)
            act.activation(k.dinv[:, :], k.dinv[:, :], ACT.Sqrt, bias=1.0).then_inc(root_out, 1)

        @block.tensor
        def _(pe):
            pe.wait_ge(loaded, loads[0])
            pe.wait_ge(masks, 2)
            ident = k.ident
            pe.wait_ge(broad, 1)
            pe.transpose(ps_a[:, 0:P], wide[:, 0, :], ident[:, :])
            pe.transpose(ps_a[:, P:2 * P], wide[:, 1, :], ident[:, :]).then_inc(spread, 1)
            pe.wait_ge(counted, 1)
            pe.matmul(ps_b[:, 0:1], k.carry_sel[:, :], k.cnt[:, T - 1:T], start=True, stop=True).then_inc(carried, 1)
            takes = [w1b[:, 0, :], w0b[:, 0, :], w1b[:, 1, :], w0b[:, 1, :]] + [w_gat[:, i, :] for i in range(3)]
            for n, w in enumerate(takes):
                if n >= 2:
                    pe.wait_ge(w_copied, n - 1)
                rows = w.shape[0]
                pe.transpose(ps_w[n % 2][0:D, 0:rows], w, ident[0:rows, 0:rows]).then_inc(w_turn, 1)
            for n in range(7):
                ps = (ps_c, ps_d)[n % 2]
                pe.wait_ge(w_copied, min(n + 1, 7))
                if n >= 2:
                    pe.wait_ge(w_kept, n - 1)
                if n < 4:
                    i, part = n // 2, n % 2
                    ins = pe.matmul(ps[0:D + 1, 0:D], turned[:, n, :], w2[:, i, part, :], start=True, stop=part == 1)
                    if part == 0:
                        ins = pe.matmul(ps[0:D + 1, 0:D], bias_at[:, :], b2[0:1, i, :], start=False, stop=True)
                else:
                    ins = pe.matmul(ps[0:D, 0:2 * HEADS], turned[:, n, 0:D], att[:, n - 4, :], start=True, stop=True)
                ins.then_inc(w_made, 1)
            pe.wait_ge(broad, 3)
            for n in range(2):
                pe.matmul(ps_w[n][:, 0:ATT], k.wide_bias[:, n, :], k.w_att[n + 1][:, 0:ATT],
                          start=True, stop=True).then_inc(spread, 1)
    ph.close()


class Norm:

    def __init__(self, ph, name, slots=SLOTS, uses=1):
        self.uses = uses
        self.entered = ph.entered
        self.stat = [ph.sb(f"{name}_stat{u}", [P, J, 6]) for u in range(slots)]
        self.mv = [ph.sb(f"{name}_mv{u}", [P, J, 2]) for u in range(slots)]
        self.root = [ph.sb(f"{name}_root{u}", [P, J]) for u in range(slots)]
        self.stats_in = [ph.sem(f"{name}_stats{u}") for u in range(slots)]
        self.var_in = [ph.sem(f"{name}_var{u}") for u in range(slots)]
        self.rooted = [ph.sem(f"{name}_rooted{u}") for u in range(slots)]
        self.inverted = [ph.sem(f"{name}_inverted{u}") for u in range(slots)]

    def count(self, through, nth):
        return through(self.uses, 0, self.uses - 1 - nth)

    def spread(self, dve, u, rows, through, parts=P, nth=0):
        for j in range(J):
            ins = dve.bn_stats(self.stat[u][0:parts, j, :], rows[:, j, :])
        ins.then_inc(self.stats_in[u], 1)
        wait_apart(dve, self.entered, (self.stats_in[u], self.count(through, nth)))
        for j in range(J):
            ins = dve.bn_aggr(self.mv[u][0:parts, j, :], self.stat[u][0:parts, j, :])
        ins.then_inc(self.var_in[u], 1)

    def take_root(self, act, u, through, scale, bias, parts=P, nth=0):
        act.wait_ge(self.var_in[u], self.count(through, nth))
        act.activation(self.root[u][0:parts, :], self.mv[u][0:parts, :, 1], ACT.Sqrt, scale=scale,
                       bias=bias).then_inc(self.rooted[u], 1)

    def invert(self, dve, u, through, parts=P, nth=0):
        dve.wait_ge(self.rooted[u], self.count(through, nth))
        dve.reciprocal(self.root[u][0:parts, :], self.root[u][0:parts, :]).then_inc(self.inverted[u], 1)
        dve.wait_ge(self.inverted[u], self.count(through, nth))

    def mean(self, u, parts=P):
        return self.mv[u][0:parts, :, 0:1].to_broadcast([parts, J, D])

    def inverse(self, u, parts=P):
        return over_rows(self.root[u][0:parts, :], D)


def four(make, name, *args):
    return [make(f"{name}{u}", *args) for u in range(DENSE_SLOTS)]


def every_place(row, parts):
    return row[0:parts, :].unsqueeze(1).to_broadcast([parts, J, D])


def bank_free(pe, copied, u, through):
    if u >= 2:
        pe.wait_ge(copied[u - 2], through(1))
    else:
        wait(pe, copied[u + 2], through(1, 1))


def dense_parts(step, u):
    return REST if is_last(step) and u == DENSE_SLOTS - 1 else P


def dense_rows(table, step, u, parts=P):
    if parts != P:
        return table[DENSE_FULL * GROUP:N, :].rearrange("(p j) c -> p j c", j=J)
    groups = table[0:DENSE_FULL * GROUP, :].rearrange("(g p j) c -> p g j c", p=P, j=J)
    return groups[:, bass.ds(step * DENSE_SLOTS + u, 1), :, :].rearrange("p g j c -> p (g j) c")


def load_ahead(sp, step, load):
    for u in range(DENSE_SLOTS) if isinstance(step, int) and step == 0 else (DENSE_SLOTS - 1,):
        load(step, u, dense_parts(step, u))


class DenseChain:

    LAYERS = 5

    def __init__(self, ph, a, k):
        self.a, self.k = a, k

        self.x, self.h1, self.x1, self.y1, self.x2, self.x3, self.z, self.c = (
            four(ph.sb, n, [P, J, D]) for n in ("x", "h1", "x1", "y1", "x2", "x3", "z", "c"))
        self.att, self.xt = four(ph.sb, "att", [P, J, ATT]), four(ph.sb, "xt", [D + 1, GROUP])
        self.ps_t = [ph.ps(f"ps_t{n}") for n in range(2)]
        self.ps_y = four(ph.ps, "ps_y")
        self.norm = Norm(ph, "norm", DENSE_SLOTS, uses=5)
        self.loaded, self.stored, self.turned, self.copied, self.made = (
            four(ph.sem, n) for n in ("loaded", "stored", "turned", "copied", "made"))
        self.ready = {n: four(ph.sem, f"{n}_ready") for n in ("h1", "x1", "y1", "x2", "x3", "att")}
        self.z0_in, self.z3_in, self.z4_in, self.scaled, self.centred = (
            four(ph.sem, n) for n in ("z0_in", "z3_in", "z4_in", "scaled", "centred"))
        self.ones_set, self.const_stored = ph.sem("ones_set"), ph.sem("const_stored")
        self.const_loads = 2 * (DENSE_FULL // 15 + 1)

    def groups(self, step):
        return [(u, dense_parts(step, u)) for u in range(DENSE_SLOTS)]

    def layer(self, through, m):
        return through(self.LAYERS, 0, self.LAYERS - 1 - m)

    def load(self, sp, step, u, n=P):
        at = u % DENSE_SLOTS
        if u == DENSE_SLOTS - 1:
            wait(sp, self.z0_in[u], counter(sp, step)(1, 1))
        sp.dma_start(self.x[at][0:n], dense_rows(self.a["x"], step, u, n)).then_inc(self.loaded[at], 16)

    def sync_body(self, sp, step):
        a, k, through = self.a, self.k, counter(sp, step)
        load_ahead(sp, step, lambda step, u, n: self.load(sp, step, u, n))
        for name, table, tile in (("h1", k.t_h1, self.h1), ("x1", k.t_x1, self.x1), ("y1", k.t_y1, self.y1),
                                  ("att", k.t_att[0], self.att), ("x3", k.t_x3, self.x3)):
            for u, n in self.groups(step):
                sp.wait_ge(self.ready[name][u], through(1))
                sp.dma_start(dense_rows(table, step, u, n), tile[u][0:n]).then_inc(self.stored[u], 16)
            if name == "h1" and not is_last(step):
                for u in range(DENSE_SLOTS - 1):
                    sp.wait_ge(self.z0_in[u], through(1))
                    self.load(sp, step, u + DENSE_SLOTS)

    def sync_end(self, sp):
        for u in range(DENSE_SLOTS):
            sp.wait_ge(self.stored[u], 16 * 5 * STEPS)

    def scalar_begin(self, act):
        k = self.k
        for n in range(2):
            t = k.t_att[n + 1][0:DENSE_FULL * GROUP, :].rearrange("(g p j) c -> p g (j c)", p=P, j=J)
            flat = k.att_rest[n][:, :, :].rearrange("p j c -> p (j c)")
            for g in range(0, DENSE_FULL, 15):
                act.dma_start(t[:, g:g + 15, :], flat.unsqueeze(1).to_broadcast([P, 15, J * ATT]))\
                   .then_inc(self.const_stored, 16)
            act.dma_start(dense_rows(k.t_att[n + 1], STEPS - 1, DENSE_SLOTS - 1, REST),
                          k.att_rest[n][0:REST]).then_inc(self.const_stored, 16)

    def scalar_body(self, act, step):
        k, through = self.k, counter(act, step)
        groups = self.groups(step)

        def copy_turned(m):
            for u, n in groups:
                act.wait_ge(self.turned[u], self.layer(through, m))
                ps, xt = self.ps_t[u % 2], self.xt[u]
                if n == P:
                    act.activation(xt[0:D, :], ps[0:D, :], ACT.Copy).then_inc(self.copied[u], 1)
                else:
                    for j in range(J):
                        ins = act.activation(xt[0:D, j * P:j * P + n], ps[0:D, j * P:j * P + n], ACT.Copy)
                    ins.then_inc(self.copied[u], 1)

        def roots(nth, scale, layer_norm):
            for u, n in groups:
                self.norm.take_root(act, u, through, scale, k.eps[0:n, :] if layer_norm else 0.0, n, nth)

        copy_turned(0)
        for u, n in groups:
            act.wait_ge(self.made[u], self.layer(through, 0))
            wait(act, self.stored[u], through(80, 1))
            act.activation(rows_of(self.h1[u][0:n]), self.ps_y[u][0:n, 0:J * D],
                           ACT.Relu).then_inc(self.ready["h1"][u], 1)
        copy_turned(1)
        roots(0, 1.0, True)
        copy_turned(2)
        roots(1, D / (D - 1), False)
        copy_turned(3)
        roots(2, D / (D - 1), False)
        roots(3, 1.0, True)
        copy_turned(4)
        for u, n in groups:
            act.wait_ge(self.made[u], self.layer(through, 4))
            act.activation(rows_of(self.att[u][0:n]), self.ps_y[u][0:n, 0:J * ATT],
                           ACT.Copy).then_inc(self.ready["att"][u], 1)
        roots(4, 1.0, True)

    def scalar_end(self, act):
        act.wait_ge(self.const_stored, 16 * self.const_loads)

    def tensor_body(self, pe, step):
        k, through = self.k, counter(pe, step)
        weights = [k.w_gcn[0], k.w_gcn[1], k.w_self[0], k.w_self[1], k.w_att[0]]
        inputs = [(self.x, self.loaded), (self.h1, self.ready["h1"]), (self.x1, self.ready["x1"]),
                  (self.y1, self.ready["y1"]), (self.x2, self.ready["x2"])]
        for m, (src, is_ready) in enumerate(inputs):
            for u, n in self.groups(step):
                pe.wait_ge(is_ready[u], through(16 if m == 0 else 1))
                if u >= 2:
                    pe.wait_ge(self.copied[u - 2], self.layer(through, m))
                elif m:
                    pe.wait_ge(self.copied[u + 2], self.layer(through, m - 1))
                else:
                    wait(pe, self.copied[u + 2], through(self.LAYERS, 1))
                for j in range(J):
                    ins = pe.transpose(self.ps_t[u % 2][0:D, j * P:j * P + n], src[u][0:n, j, :], k.ident[0:n, 0:n])
                ins.then_inc(self.turned[u], 1)
            rows, width = (D, ATT) if m == 4 else (D + 1, D)
            for u, n in self.groups(step):
                pe.wait_ge(self.copied[u], self.layer(through, m))
                if m == 0:
                    wait(pe, self.ready["att"][u], through(1, 1))
                for j in range(J):
                    ins = pe.matmul(self.ps_y[u][0:n, j * width:(j + 1) * width], self.xt[u][0:rows, j * P:j * P + n],
                                    weights[m][0:rows, 0:width], start=True, stop=True)
                ins.then_inc(self.made[u], 1)

    def vector_begin(self, dve):
        for u in range(DENSE_SLOTS):
            ins = dve.memset(self.xt[u][D:D + 1, :], 1.0)
        ins.then_inc(self.ones_set, 1)

    def vector_body(self, dve, step):
        through, norm = counter(dve, step), self.norm
        groups = self.groups(step)

        def made_rows(u, n):
            return self.ps_y[u][0:n, 0:J * D].rearrange("p (j c) -> p j c", c=D)

        def layer_norm(nth, z_in, centred, out, name):
            for u, n in groups:
                dve.wait_ge(z_in[u], through(1))
                norm.spread(dve, u, self.z[u][0:n], through, n, nth)
            for u, n in groups:
                norm.invert(dve, u, through, n, nth)
                dve.wait_ge(self.centred[u], through(3, 0, 2 - centred))
                dve.tensor_tensor(out[u][0:n], self.c[u][0:n], norm.inverse(u, n), ALU.mult)\
                    .then_inc(self.ready[name][u], 1)

        for u, n in groups:
            dve.wait_ge(self.made[u], self.layer(through, 1))
            wait(dve, self.stored[u], through(80, 1))
            wait(dve, self.centred[u], through(3, 1))
            dve.scalar_tensor_tensor(out=self.z[u][0:n], in0=made_rows(u, n), scalar=0.0, in1=self.x[u][0:n],
                                     op0=ALU.max, op1=ALU.add).then_inc(self.z0_in[u], 1)
        layer_norm(0, self.z0_in, 0, self.x1, "x1")
        for u, n in groups:
            dve.wait_ge(self.made[u], self.layer(through, 2))
            norm.spread(dve, u, made_rows(u, n), through, n, 1)
        for u, n in groups:
            norm.invert(dve, u, through, n, 1)
            dve.tensor_tensor(self.y1[u][0:n], made_rows(u, n), norm.inverse(u, n),
                              ALU.mult).then_inc(self.ready["y1"][u], 1)
        for u, n in groups:
            dve.wait_ge(self.made[u], self.layer(through, 3))
            norm.spread(dve, u, made_rows(u, n), through, n, 2)
        for u, n in groups:
            norm.invert(dve, u, through, n, 2)
            dve.tensor_tensor(self.c[u][0:n], made_rows(u, n), norm.inverse(u, n),
                              ALU.mult).then_inc(self.scaled[u], 1)
        layer_norm(3, self.z3_in, 1, self.x2, "x2")
        layer_norm(4, self.z4_in, 2, self.x3, "x3")

    def gpsimd_body(self, pool, step):
        through = counter(pool, step)

        def centre(nth, centred):
            for u, n in self.groups(step):
                pool.wait_ge(self.norm.var_in[u], self.norm.count(through, nth))
                pool.tensor_tensor(self.c[u][0:n], self.z[u][0:n], self.norm.mean(u, n),
                                   ALU.subtract).then_inc(self.centred[u], 1)

        centre(0, 0)
        for u, n in self.groups(step):
            pool.wait_ge(self.scaled[u], through(1))
            pool.tensor_tensor(self.z[u][0:n], self.c[u][0:n], self.x1[u][0:n], ALU.add).then_inc(self.z3_in[u], 1)
        centre(3, 1)
        for u, n in self.groups(step):
            pool.wait_ge(self.ready["x2"][u], through(1))
            pool.tensor_tensor(self.z[u][0:n], self.x2[u][0:n],
                               self.k.gat_rest_row[0:n, :].unsqueeze(1).to_broadcast([n, J, D]),
                               ALU.add).then_inc(self.z4_in[u], 1)
        centre(4, 2)


def rows_of(tile):
    return tile.rearrange("p j c -> p (j c)")


def by_head(rows):
    return rows[:, :, 0:D].rearrange("p j (h c) -> p j h c", h=HEADS)


def per_head(weights):
    return weights.unsqueeze(3).to_broadcast([P, J, HEADS, CH])


class Rows:

    def __init__(self, ph, gather=None, gather_idx=None, scatter=None, scatter_idx=None, width=D, head_too=False):
        self.ph, self.table, self.idx, self.out, self.out_idx = ph, gather, gather_idx, scatter, scatter_idx
        self.head_too = head_too
        if gather is not None:
            self.rows = ph.pair(ph.sb, "gathered", [P, J, width])
            self.window = ph.pair(ph.sb, "take_window", [P, J], I32)
            self.window_in, self.here = ph.pair(ph.sem, "take_window_in"), ph.pair(ph.sem, "gathered_in")
        if scatter is not None:
            self.out_window = ph.pair(ph.sb, "put_window", [P, J], I32)
            self.out_window_in, self.gone = ph.pair(ph.sem, "put_window_in"), ph.pair(ph.sem, "scattered")

    def count(self, step, u):
        return J - 1 if not self.head_too and is_last(step) and u == SLOTS - 1 else J

    def all_here(self, step, u, through):
        return through(16 * J) - 16 * (J - self.count(step, u)) if is_last(step) else through(16 * J)

    def gather(self, pool, step, u, through, *free):
        wait_apart(pool, self.ph.entered, (self.window_in[u], through(1)), *free)
        for j in range(self.count(step, u)):
            pool.indirect_dma_start(
                out=self.rows[u][:, j, :], out_offset=None, in_=self.table,
                in_offset=bass.IndirectOffsetOnAxis(ap=self.window[u][:, j:j + 1], axis=0)).then_inc(self.here[u], 16)

    def scatter(self, pool, tile, u, through, ready, bound):
        wait_apart(pool, self.ph.entered, (self.out_window_in[u], through(1)), (ready, through(1)))
        for j in range(J):
            pool.indirect_dma_start(
                out=self.out, out_offset=bass.IndirectOffsetOnAxis(ap=self.out_window[u][:, j:j + 1], axis=0),
                in_=tile[:, j, :], in_offset=None, bounds_check=bound, oob_is_err=False).then_inc(self.gone[u], 16)

    def first_windows(self, act):
        for u in range(SLOTS):
            act.activation(self.window[u][:, :], self.idx[:, cols(0, u)], ACT.Copy).then_inc(self.window_in[u], 1)

    def next_window(self, act, step, u, through):
        if not is_last(step):
            wait_apart(act, self.ph.entered, (self.here[u], self.all_here(step, u, through)))
            act.activation(self.window[u][:, :], self.idx[:, cols(step, u, skip=J * SLOTS)],
                           ACT.Copy).then_inc(self.window_in[u], 1)

    def put_window(self, act, step, u, through, back=0):
        wait_apart(act, self.ph.entered, (self.gone[u], through(16 * J, 1)))
        act.activation(self.out_window[u][:, :], self.out_idx[:, cols(step, u, skip=-J * SLOTS * back)],
                       ACT.Copy).then_inc(self.out_window_in[u], 1)


def is_last(step):
    return isinstance(step, int) and step == STEPS - 1


class EdgeFeatures:

    def __init__(self, ph, k, slots):
        self.k, self.slots = k, slots
        self.attr_t = [ph.sb(f"attr_t{u}", [5, GROUP]) for u in range(slots)]
        self.ps_attr = self.ps_feat = [ph.ps(f"ps_feat{u}") for u in range(slots)]
        self.turned, self.copied, self.made, self.kept, self.here = (
            [ph.sem(f"{n}{u}") for u in range(SLOTS)]
            for n in ("attr_turned", "attr_copied", "feat_made", "feat_kept", "attr_here"))
        self.window = ph.pair(ph.sb, "attr_window", [P, J, 5])
        self.entered = ph.entered

    def take(self, act, step, u, through):
        n = edge_places(step, u)
        wait_apart(act, self.entered, (self.turned[u], through(1, 1)))
        act.activation(self.window[u][:, 0:n, :], self.k.edge_in[:, cols(step, u, n), :],
                       ACT.Copy).then_inc(self.here[u], 1)

    def turn(self, pe, step, u, through):
        pe.wait_ge(self.here[u], through(1))
        ps = self.ps_attr[u % self.slots]
        for j in range(edge_places(step, u)):
            ins = pe.transpose(ps[0:5, j * P:(j + 1) * P], self.window[u][:, j, :], self.k.ident[:, :])
        ins.then_inc(self.turned[u], 1)


def edge_places(step, u):
    return J - 1 if is_last(step) and u == SLOTS - 1 else J


def column_stats(dve, ph, stat, lone, values, step, u):
    n = edge_places(step, u)
    v = values[:, 0:n * P].rearrange("c (j p) -> c j p", p=P)
    dve.bn_stats(stat[:, bass.ds(step * SLOTS + u, 1), :].rearrange("c a s -> c (a s)"), v[:, :, 0:P - 1])
    return dve.tensor_copy(lone[:, cols(step, u, n)], v[:, :, P - 1])


def column_scale(dve, act, gamma, beta, mv, root, scale, shift, sems, k, act_side):
    var_in, rooted, link = sems
    if act_side:
        act.wait_ge(var_in, 1)
        act.activation(root, mv[:, 1:2], ACT.Sqrt, bias=k.eps[0:D, :]).then_inc(rooted, 1)
        return
    dve.wait_ge(rooted, 1)
    dve.reciprocal(root, root).then_inc(link, 1)
    dve.wait_ge(link, 1)
    dve.tensor_tensor(scale, gamma, root, ALU.mult).then_inc(link, 1)
    dve.wait_ge(link, 2)
    dve.tensor_tensor(root, mv[:, 0:1], scale, ALU.mult).then_inc(link, 1)
    dve.wait_ge(link, 3)
    dve.tensor_tensor(shift, beta, root, ALU.subtract).then_inc(link, 1)
    dve.wait_ge(link, 4)


def own_rows(nc, a, k):
    ph = Phase(nc, "own")
    take = Rows(ph, a["x"], k.own_idx, k.t_x, k.out_idx, head_too=True)
    x = take.rows
    scaled = ph.pair(ph.sb, "scaled", [P, J, D])
    scaled_in, x_stored, scaled_stored = (ph.pair(ph.sem, n) for n in ("scaled_in", "x_stored", "scaled_stored"))
    ef = EdgeFeatures(ph, k, 1)
    feat = ph.pair(ph.sb, "feat", [D, GROUP])
    feat_read = ph.pair(ph.sem, "feat_read")
    stat, lone = ph.sb("stat", [D, 2 * STEPS + 1, 6]), ph.sb("lone", [D, TH])
    mv, root = ph.sb("mv", [D, 2]), ph.sb("root", [D, 1])
    ps_w = ph.ps("ps_w")
    stat_in, var_in, rooted, link, folded, bias_in = (
        ph.sem(n) for n in ("stat_in", "var_in", "rooted", "link", "folded", "bias_in"))

    ph.sems.append(k.base_copied)
    dense = DenseChain(ph.part("dense"), a, k)

    with nc.Block() as block:
        @block.sync
        def _(sp):
            sp.sem_inc(ph.entered, 1)

            def body(step):
                through = counter(sp, step)
                dense.sync_body(sp, step)
                for u in range(SLOTS):
                    sp.wait_ge(take.here[u], take.all_here(step, u, through))
                    sp.dma_start(k.l_x[:, cols(step, u), :], x[u][:, :, :]).then_inc(x_stored[u], 16)
                    sp.wait_ge(scaled_in[u], through(1))
                    sp.dma_start(k.l_s[:, cols(step, u), :], scaled[u][:, :, :]).then_inc(scaled_stored[u], 16)
            steps(sp, STEPS, body)
            dense.sync_end(sp)
            for u in range(SLOTS):
                sp.wait_ge(x_stored[u], 16 * STEPS)
                sp.wait_ge(scaled_stored[u], 16 * STEPS)

        @block.gpsimd
        def _(pool):
            bound = pool.to_reg(N - 1)

            def body(step):
                through = counter(pool, step)
                before = None if isinstance(step, int) and step == 0 else counter(pool, step - 1)
                if isinstance(step, int) and step == 1:
                    pool.wait_ge(k.base_copied, 16)
                for u in range(SLOTS):
                    take.gather(pool, step, u, through, (x_stored[u], through(16, 1)), (scaled_in[u], through(1, 1)))
                    if before is not None:
                        take.scatter(pool, scaled[u], u, before, scaled_in[u], bound)
                dense.gpsimd_body(pool, step)
            steps(pool, STEPS, body)
            for u in range(SLOTS):
                take.scatter(pool, scaled[u], u, counter(pool, STEPS - 1), scaled_in[u], bound)
            for u in range(SLOTS):
                pool.wait_ge(take.gone[u], 16 * J * STEPS)

        @block.scalar
        def _(act):
            dense.scalar_begin(act)
            take.first_windows(act)

            def body(step):
                through = counter(act, step)
                dense.scalar_body(act, step)
                for u in range(SLOTS):
                    take.next_window(act, step, u, through)
                    take.put_window(act, step, u, through)
                    ef.take(act, step, u, through)
                    n = edge_places(step, u) * P
                    act.wait_ge(ef.turned[u], through(1))
                    act.activation(ef.attr_t[0][:, 0:n], ef.ps_attr[0][0:5, 0:n], ACT.Copy).then_inc(ef.copied[u], 1)
                    act.wait_ge(ef.made[u], through(1))
                    wait(act, feat_read[u], through(1, 1))
                    act.activation(feat[u][:, 0:n], ef.ps_feat[0][0:D, 0:n], ACT.Relu).then_inc(ef.kept[u], 1)
            steps(act, STEPS, body)
            dense.scalar_end(act)
            column_scale(None, act, None, None, mv, root[:, :], None, None, (var_in, rooted, link), k, True)

        @block.tensor
        def _(pe):
            pe.wait_ge(dense.ones_set, 1)

            def body(step):
                through = counter(pe, step)
                dense.tensor_body(pe, step)
                for u in range(SLOTS):
                    wait(pe, *group_before(ef.kept, u, through))
                    ef.turn(pe, step, u, through)
                    n = edge_places(step, u) * P
                    pe.wait_ge(ef.copied[u], through(1))
                    pe.matmul(ef.ps_feat[0][0:D, 0:n], k.w_edge[:, :], ef.attr_t[0][:, 0:n],
                              start=True, stop=True).then_inc(ef.made[u], 1)
            steps(pe, STEPS, body)
            pe.wait_ge(folded, 1)
            pe.matmul(ps_w[0:1, 0:D], k.l3_cols[:, 7:8], k.w_msg[:, 2, :], start=True, stop=True).then_inc(bias_in, 1)

        @block.vector
        def _(dve):
            dense.vector_begin(dve)

            def body(step):
                through = counter(dve, step)
                dense.vector_body(dve, step)
                for u in range(SLOTS):
                    dve.wait_ge(take.here[u], take.all_here(step, u, through))
                    wait(dve, take.gone[u], through(16 * J, 1))
                    wait(dve, scaled_stored[u], through(16, 1))
                    dve.tensor_tensor(scaled[u][:, :, :], x[u][:, :, :], over_rows(k.dinv[:, cols(step, u)], D),
                                      ALU.mult).then_inc(scaled_in[u], 1)
                    wait_apart(dve, ph.entered, (ef.kept[u], through(1)))
                    column_stats(dve, ph, stat, lone, feat[u], step, u).then_inc(feat_read[u], 1)
            steps(dve, STEPS, body)
            dve.wait_ge(feat_read[0], STEPS)
            dve.wait_ge(feat_read[1], STEPS)
            dve.bn_stats(stat[:, 2 * STEPS, :], lone[:, 0:LAST]).then_inc(stat_in, 1)
            dve.wait_ge(stat_in, 1)
            dve.bn_aggr(mv[:, :], stat[:, :, :].rearrange("c a s -> c (a s)")).then_inc(var_in, 1)
            column_scale(dve, None, k.l3_cols[:, 2:3], k.l3_cols[:, 3:4], mv, root[:, :], k.edge_scale[:, :],
                         k.l3_cols[:, 7:8], (var_in, rooted, link), k, False)
            dve.tensor_scalar(k.w_feat[0:D, :], k.w_msg[:, 2, :], k.edge_scale[:, :], None, ALU.mult).then_inc(folded, 1)
            dve.wait_ge(bias_in, 1)
            dve.tensor_tensor(k.msg_bias[:, :], ps_w[0:1, 0:D], k.msg_bias[:, :], ALU.add)
    ph.close()


GCN1, GCN2, SAGE1, SAGE2, GAT1, GAT2, GAT3 = "gcn1", "gcn2", "sage1", "sage2", "gat1", "gat2", "gat3"


def node_round(nc, a, k, kind, table=None, out=None, own=None, rest=None, keep=None, layer=0):
    assert SLOTS == 2
    gat, sage, gcn = kind in (GAT1, GAT2, GAT3), kind in (SAGE1, SAGE2), kind in (GCN1, GCN2)
    C = ATT if gat else D
    A_WIDTH = D + 1 if sage else C
    OUT = ATT if kind in (SAGE2, GAT1, GAT2) else D
    normed = kind in (GCN2, SAGE2, GAT3)
    over_std = sage
    multiplied = kind != GAT3
    ph = Phase(nc, kind)
    put = Rows(ph, table, k.src_idx, out, k.out_idx)
    acc = ph.pair(ph.sb, "acc", [P, J, A_WIDTH])
    cont = ph.pair(ph.sb, "cont", [P, J])
    new = ph.pair(ph.sb, "new", [P, J, OUT])
    head_part = ph.sb("head_part", [P, C])
    xt = ph.pair(ph.sb, "xt", [D + 1, GROUP])
    ps_x, ps_y = ph.pair(ph.ps, "ps_x"), ph.pair(ph.ps, "ps_y")
    ps_carry = ph.ps("ps_carry")
    link = [ph.pair(ph.sem, f"summed{j}_") for j in range(J)]
    windows, acc_stored = ph.pair(ph.sem, "windows"), ph.pair(ph.sem, "acc_stored")
    carried, head_here, ones_set, started = (ph.sem(n) for n in ("carried", "head_here", "ones_set", "started"))
    input_in, turned, copied, made = (ph.pair(ph.sem, n) for n in ("input_in", "turned", "copied", "made"))
    new_in, new_stored, step_a, step_b, step_c = (
        ph.pair(ph.sem, n) for n in ("new_in", "new_stored", "step_a", "step_b", "step_c"))
    if gcn or gat:
        mixed = ph.pair(ph.sb, "mixed", [P, J, D])
        mix_a, mix_b = ph.pair(ph.sem, "mix_a"), ph.pair(ph.sem, "mix_b")
    if own is not None:
        mine, own_in = ph.pair(ph.sb, "mine", [P, J, D]), ph.pair(ph.sem, "own_in")
    if rest is not None:
        resid, rest_in = ph.pair(ph.sb, "resid", [P, J, D]), ph.pair(ph.sem, "rest_in")
    if sage:
        own_t, ps_o = ph.pair(ph.sb, "own_t", [D + 1, GROUP]), ph.pair(ph.ps, "ps_o")
        unit = Norm(ph, "unit")
    if gat:
        msg, weighted = ph.pair(ph.sb, "msg", [P, J, ATT]), ph.pair(ph.sb, "weighted", [P, J, ATT])
        den = ph.pair(ph.sb, "den", [P, J, HEADS])
        msg_in, weighed, ex_in = (ph.pair(ph.sem, n) for n in ("msg_in", "weighed", "ex_in"))
    if normed:
        norm = Norm(ph, "norm")
        z, c = ph.pair(ph.sb, "z", [P, J, D]), ph.pair(ph.sb, "c", [P, J, D])
        z_in, c_in = ph.pair(ph.sem, "z_in"), ph.pair(ph.sem, "c_in")
    if kind == SAGE2:
        x2, x2t = ph.pair(ph.sb, "x2", [P, J, D]), ph.sb("x2t", [D, GROUP])
        ps_u = ph.ps("ps_u")
        x2_in, x2_turned, x2_copied, x2_made = (
            ph.pair(ph.sem, n) for n in ("x2_in", "x2_turned", "x2_copied", "x2_made"))
    l_acc = k.l_acc100 if gat else k.l_acc
    kept = None if keep is None else (x2 if kind == SAGE2 else new)
    kept_in = None if keep is None else (x2_in if kind == SAGE2 else new_in)

    def msgs(step, u):
        return edge_places(step, u)

    with nc.Block() as block:
        @block.sync
        def _(sp):
            sp.sem_inc(ph.entered, 1)

            def load_rows(step, u, through):
                if gat:
                    wait(sp, link[J - 1][u], through(1, 1))
                    n = msgs(step, u)
                    sp.dma_start(msg[u][:, 0:n, :], k.l_msg[:, cols(step, u, n), :]).then_inc(msg_in[u], 16)
                if own is not None:
                    wait(sp, (mix_b if gcn else turned)[u], through(1, 1))
                    sp.dma_start(mine[u][:, :, :], own[:, cols(step, u), :]).then_inc(own_in[u], 16)

            def load_rest(step, u, through):
                if rest is not None:
                    wait(sp, z_in[u], through(1, 1))
                    sp.dma_start(resid[u][:, :, :], rest[:, cols(step, u), :]).then_inc(rest_in[u], 16)

            def store_sums(step, u, through):
                n = msgs(step, u)
                sp.wait_ge(link[n - 1][u], through(1))
                sp.dma_start(l_acc[:, cols(step, u, n), :], acc[u][:, 0:n, 0:C]).then_inc(acc_stored[u], 16)

            def store_new(step, u):
                if keep is not None:
                    sp.wait_ge(kept_in[u], counter(sp, step)(1))
                    sp.dma_start(keep[:, cols(step, u), :], kept[u][:, :, :]).then_inc(new_stored[u], 16)

            def body(step):
                through = counter(sp, step)
                load_rows(step, 0, through)
                load_rows(step, 1, through)
                load_rest(step, 0, through)
                store_sums(step, 0, through)
                if not (isinstance(step, int) and step == 0):
                    store_new(step - 1, 1)
                load_rest(step, 1, through)
                store_sums(step, 1, through)
                store_new(step, 0)
            steps(sp, STEPS, body)
            store_new(STEPS - 1, 1)
            for u in range(SLOTS):
                if keep is not None:
                    sp.wait_ge(new_stored[u], 16 * STEPS)

        @block.gpsimd
        def _(pool):
            bound = pool.to_reg(N - 1)

            def body(step):
                through = counter(pool, step)
                before = None if isinstance(step, int) and step == 0 else counter(pool, step - 1)
                for u in range(SLOTS):
                    if not gat:
                        put.gather(pool, step, u, through, (link[J - 1][u], through(1, 1)))
                    if before is not None:
                        put.scatter(pool, new[u], u, before, new_in[u], bound)
            steps(pool, STEPS, body)
            for u in range(SLOTS):
                pool.wait_ge(acc_stored[u], 16 * STEPS)
            pool.indirect_dma_start(
                out=head_part[:, :], out_offset=None, in_=l_acc.rearrange("p t c -> (p t) c"),
                in_offset=bass.IndirectOffsetOnAxis(ap=k.head_row[:, 0:1], axis=0)).then_inc(head_here, 16)
            for u in range(SLOTS):
                put.scatter(pool, new[u], u, counter(pool, STEPS - 1), new_in[u], bound)
            for u in range(SLOTS):
                pool.wait_ge(put.gone[u], 16 * J * STEPS)

        @block.scalar
        def _(act):
            if not gat:
                put.first_windows(act)

            def front(step, u):
                through = counter(act, step)
                wait_apart(act, ph.entered, (link[J - 1][u], through(1, 1)))
                if sage:
                    wait_apart(act, ph.entered, (turned[u], through(1, 1)))
                    act.activation(acc[u][:, :, D], k.cnt[:, cols(step, u)], ACT.Copy)
                if gat:
                    n = msgs(step, u)
                    act.activation(weighted[u][:, 0:n, D:ATT], k.att_e[:, cols(step, u, n), :], ACT.Copy)
                act.activation(cont[u][:, :], k.cont[:, cols(step, u)], ACT.Copy).then_inc(windows[u], 1)
                if not gat:
                    put.next_window(act, step, u, through)
                if multiplied:
                    rows = D + 1 if sage else D
                    act.wait_ge(turned[u], through(1))
                    wait(act, made[u], through(1, 1))
                    if kind in (GAT1, GAT2):
                        act.activation(xt[u][0:D, :], ps_x[u][0:D, :], ACT.Relu,
                                       bias=k.gat_bias[:, layer:layer + 1]).then_inc(copied[u], 1)
                    elif sage:
                        act.activation(own_t[u][0:D, :], ps_o[u][0:D, :], ACT.Copy)
                        act.activation(xt[u][0:rows, :], ps_x[u][0:rows, :], ACT.Copy).then_inc(copied[u], 1)
                    else:
                        act.activation(xt[u][0:D, :], ps_x[u][0:D, :], ACT.Copy).then_inc(copied[u], 1)

            def back(step, u):
                through = counter(act, step)
                put.put_window(act, step, u, through)
                if over_std:
                    unit.take_root(act, u, through, D / (D - 1), 0.0)
                if normed:
                    norm.take_root(act, u, through, 1.0, k.eps[:, :])
                if kind == SAGE2:
                    act.wait_ge(x2_turned[u], through(1))
                    act.activation(x2t[:, :], ps_u[0:D, :], ACT.Copy).then_inc(x2_copied[u], 1)
            turns(act, front, back)

        @block.tensor
        def _(pe):
            pe.wait_ge(ones_set, 1)

            def carry(step, u):
                if is_last(step) and u == SLOTS - 1:
                    pe.wait_ge(link[J - 2][u], STEPS)
                    pe.matmul(ps_carry[:, 0:C], k.carry_sel[:, :], acc[u][:, J - 2, 0:C],
                              start=True, stop=True).then_inc(carried, 1)

            def front(step, u):
                through = counter(pe, step)
                carry(step, u)
                if not multiplied:
                    return
                if sage:
                    pe.wait_ge(own_in[u], through(16))
                    wait(pe, copied[u], through(1, 1))
                    for j in range(J):
                        pe.transpose(ps_o[u][0:D, j * P:(j + 1) * P], mine[u][:, j, :], k.ident[:, :])
                    pe.wait_ge(link[J - 1][u], through(1))
                    for j in range(J):
                        ins = pe.transpose(ps_x[u][0:D + 1, j * P:(j + 1) * P], acc[u][:, j, :], k.ident[:, :])
                else:
                    pe.wait_ge(mix_b[u], through(1))
                    wait(pe, copied[u], through(1, 1))
                    for j in range(J):
                        ins = pe.transpose(ps_x[u][0:D, j * P:(j + 1) * P], mixed[u][:, j, :], k.ident[:, :])
                ins.then_inc(turned[u], 1)

            def back(step, u):
                if not multiplied:
                    return
                through = counter(pe, step)
                pe.wait_ge(copied[u], through(1))
                wait(pe, (z_in if normed else new_in)[u], through(1, 1))
                for j in range(J):
                    at = slice(j * P, (j + 1) * P)
                    if gcn:
                        ins = pe.matmul(ps_y[u][:, j * D:(j + 1) * D], xt[u][:, at], k.w_gcn[layer][:, :],
                                        start=True, stop=True)
                    elif sage:
                        pe.matmul(ps_y[u][:, j * D:(j + 1) * D], own_t[u][:, at], k.w_self[layer][:, :],
                                  start=True, stop=False)
                        ins = pe.matmul(ps_y[u][:, j * D:(j + 1) * D], xt[u][:, at], k.w_agg[layer][:, :],
                                        start=False, stop=True)
                    else:
                        ins = pe.matmul(ps_y[u][:, j * ATT_ALL:(j + 1) * ATT_ALL], xt[u][0:D, at],
                                        k.w_att[layer + 1][:, :], start=True, stop=True)
                ins.then_inc(made[u], 1)
                if kind == SAGE2:
                    pe.wait_ge(x2_in[u], through(1))
                    wait(pe, new_in[1 - u], through(1, 1) if u == 0 else through(1))
                    for j in range(J):
                        ins = pe.transpose(ps_u[0:D, j * P:(j + 1) * P], x2[u][:, j, :], k.ident[:, :])
                    ins.then_inc(x2_turned[u], 1)
                    pe.wait_ge(x2_copied[u], through(1))
                    for j in range(J):
                        ins = pe.matmul(ps_u[:, j * ATT_ALL:(j + 1) * ATT_ALL], x2t[:, j * P:(j + 1) * P],
                                        k.w_att[0][:, :], start=True, stop=True)
                    ins.then_inc(x2_made[u], 1)
            turns(pe, front, back)

        @block.vector
        def _(dve):
            for u in range(SLOTS):
                dve.memset(xt[u][D:D + 1, :], 1.0)
                if sage:
                    dve.memset(own_t[u][D:D + 1, :], 1.0)
            dve.memset(acc[1][:, J - 1, 0:C], 0.0).then_inc(ones_set, 1)
            dve.wait_ge(ones_set, 1)

            def front(step, u):
                through = counter(dve, step)
                n = msgs(step, u)
                if gat:
                    dve.wait_ge(msg_in[u], through(16))
                    dve.tensor_tensor(by_head(weighted[u][:, 0:n, :]), by_head(msg[u][:, 0:n, :]),
                                      k.att_e[:, cols(step, u, n), :].unsqueeze(3).to_broadcast([P, n, HEADS, CH]),
                                      ALU.mult).then_inc(weighed[u], 1)
                    dve.wait_ge(weighed[u], through(1))
                else:
                    dve.wait_ge(put.here[u], put.all_here(step, u, through))
                rows = weighted[u] if gat else put.rows[u]
                dve.wait_ge(windows[u], through(1))
                wait(dve, acc_stored[u], through(16, 1))
                if sage:
                    wait(dve, turned[u], through(1, 1))
                for j in range(n):
                    if j:
                        dve.wait_ge(link[j - 1][u], through(1))
                        before = acc[u][:, j - 1, 0:C]
                    else:
                        wait(dve, link[J - 1][1 - u], through(1, 1) if u == 0 else through(1))
                        before = acc[1 - u][:, J - 1, 0:C]
                    dve.scalar_tensor_tensor(out=acc[u][:, j, 0:C], in0=before, scalar=cont[u][:, j:j + 1],
                                             in1=rows[:, j, :], op0=ALU.mult, op1=ALU.add).then_inc(link[j][u], 1)
                if n < J:
                    dve.wait_ge(carried, 1)
                    dve.wait_ge(head_here, 16)
                    dve.tensor_tensor(acc[u][:, J - 1, 0:C], ps_carry[:, 0:C], head_part[:, :],
                                      ALU.add).then_inc(link[J - 1][u], 1)
                if gcn:
                    dve.wait_ge(link[J - 1][u], through(1))
                    dve.wait_ge(own_in[u], through(16))
                    wait(dve, turned[u], through(1, 1))
                    dve.tensor_tensor(mine[u][:, :, :], acc[u][:, :, :], mine[u][:, :, :], ALU.add).then_inc(step_a[u], 1)
                    dve.wait_ge(step_a[u], through(1))
                    dve.tensor_tensor(mixed[u][:, :, :], mine[u][:, :, :], over_rows(k.dinv[:, cols(step, u)], D),
                                      ALU.mult).then_inc(mix_b[u], 1)
                if gat:
                    dve.wait_ge(link[J - 1][u], through(1))
                    dve.tensor_scalar(den[u][:, :, :], acc[u][:, :, D:ATT], 1e-16, None, ALU.add).then_inc(step_a[u], 1)
                    dve.wait_ge(step_a[u], through(1))
                    dve.reciprocal(den[u][:, :, :], den[u][:, :, :]).then_inc(mix_a[u], 1)
                    dve.wait_ge(mix_a[u], through(1))
                    if multiplied:
                        wait(dve, turned[u], through(1, 1))
                    dve.tensor_tensor(by_head(mixed[u]), by_head(acc[u]), per_head(den[u][:, :, :]),
                                      ALU.mult).then_inc(mix_b[u], 1)

            def back(step, u):
                through = counter(dve, step)
                y = ps_y[u][:, 0:J * D].rearrange("p (j c) -> p j c", c=D)

                def new_free():
                    wait(dve, put.gone[u], through(16 * J, 1))
                    if keep is not None:
                        wait(dve, new_stored[u], through(16, 1))

                if kind == GCN1:
                    dve.wait_ge(made[u], through(1))
                    new_free()
                    dve.scalar_tensor_tensor(out=new[u][:, :, :], in0=y, scalar=0.0,
                                             in1=over_rows(k.dinv[:, cols(step, u)], D),
                                             op0=ALU.max, op1=ALU.mult).then_inc(new_in[u], 1)
                elif kind == GCN2:
                    dve.wait_ge(made[u], through(1))
                    dve.wait_ge(rest_in[u], through(16))
                    dve.scalar_tensor_tensor(out=z[u][:, :, :], in0=y, scalar=0.0, in1=resid[u][:, :, :],
                                             op0=ALU.max, op1=ALU.add).then_inc(z_in[u], 1)
                elif sage:
                    dve.wait_ge(made[u], through(1))
                    unit.spread(dve, u, y, through)
                    unit.invert(dve, u, through)
                    if kind == SAGE1:
                        new_free()
                        dve.tensor_tensor(new[u][:, :, :], y, unit.inverse(u), ALU.mult).then_inc(new_in[u], 1)
                    else:
                        dve.wait_ge(rest_in[u], through(16))
                        dve.tensor_tensor(c[u][:, :, :], y, unit.inverse(u), ALU.mult).then_inc(step_a[u], 1)
                        dve.wait_ge(step_a[u], through(1))
                        dve.tensor_tensor(z[u][:, :, :], c[u][:, :, :], resid[u][:, :, :], ALU.add).then_inc(z_in[u], 1)
                elif kind in (GAT1, GAT2):
                    dve.wait_ge(made[u], through(1))
                    new_free()
                    y = ps_y[u][:, 0:J * ATT_ALL].rearrange("p (j c) -> p j c", c=ATT_ALL)
                    dve.tensor_scalar(k.att_dst[:, cols(step, u), :], y[:, :, ATT:ATT_ALL], 1.0, None, ALU.mult)
                    dve.tensor_copy(new[u][:, :, :], y[:, :, 0:ATT]).then_inc(new_in[u], 1)
                else:
                    dve.wait_ge(mix_b[u], through(1))
                    dve.tensor_tensor(c[u][:, :, :], mixed[u][:, :, :],
                                      k.gat_bias_row[:, :].unsqueeze(1).to_broadcast([P, J, D]),
                                      ALU.add).then_inc(step_b[u], 1)
                    dve.wait_ge(step_b[u], through(1))
                    dve.wait_ge(rest_in[u], through(16))
                    dve.scalar_tensor_tensor(out=z[u][:, :, :], in0=c[u][:, :, :], scalar=0.0, in1=resid[u][:, :, :],
                                             op0=ALU.max, op1=ALU.add).then_inc(z_in[u], 1)
                if normed:
                    dve.wait_ge(z_in[u], through(1))
                    norm.spread(dve, u, z[u], through)
                    dve.wait_ge(norm.var_in[u], through(1))
                    dve.tensor_tensor(c[u][:, :, :], z[u][:, :, :], norm.mean(u), ALU.subtract).then_inc(c_in[u], 1)
                    norm.invert(dve, u, through)
                    dve.wait_ge(c_in[u], through(1))
                    if kind == SAGE2:
                        wait(dve, new_stored[u], through(16, 1))
                        wait(dve, x2_turned[u], through(1, 1))
                        dve.tensor_tensor(x2[u][:, :, :], c[u][:, :, :], norm.inverse(u), ALU.mult).then_inc(x2_in[u], 1)
                        dve.wait_ge(x2_made[u], through(1))
                        wait(dve, put.gone[u], through(16 * J, 1))
                        y = ps_u[:, 0:J * ATT_ALL].rearrange("p (j c) -> p j c", c=ATT_ALL)
                        dve.tensor_scalar(k.att_dst[:, cols(step, u), :], y[:, :, ATT:ATT_ALL], 1.0, None, ALU.mult)
                        dve.tensor_copy(new[u][:, :, :], y[:, :, 0:ATT]).then_inc(new_in[u], 1)
                    else:
                        new_free()
                        dve.tensor_tensor(new[u][:, :, :], c[u][:, :, :], norm.inverse(u), ALU.mult)\
                            .then_inc(new_in[u], 1)
            turns(dve, front, back)
    ph.close()


def attention_weights(nc, k, table, layer):
    ph = Phase(nc, f"logits{layer}")
    take = Rows(ph, table, k.src_idx, width=ATT)
    row_stored, logit_in = ph.pair(ph.sem, "row_stored"), ph.pair(ph.sem, "logit_in")
    e, run = k.att_e, ph.sb("run", [P, TH, HEADS])
    peak = ph.sb("peak", [P, 2, HEADS])
    whole = ph.sb("whole", [P, 2, HEADS])
    lone = ph.sb("lone", [P, HEADS])
    reset = ph.sb("reset", [P, T])
    values = ph.sb("values", [P, T])
    wide = ph.sb("wide", [P, 2 * HEADS, P])
    seen = ph.sb("seen", [P, HEADS, P])
    ps_tail, ps_head, ps_sel = ph.ps("ps_tail"), ph.ps("ps_head"), ph.ps("ps_sel")
    link, opened, wide_in, turned, ready, exp_in = (
        ph.sem(n) for n in ("link", "opened", "wide_in", "turned", "ready", "exp_in"))

    with nc.Block() as block:
        @block.sync
        def _(sp):
            sp.sem_inc(ph.entered, 1)

            def body(step):
                through = counter(sp, step)
                for u in range(SLOTS):
                    n = edge_places(step, u)
                    sp.wait_ge(take.here[u], take.all_here(step, u, through))
                    sp.dma_start(k.l_msg[:, cols(step, u, n), :], take.rows[u][:, 0:n, :]).then_inc(row_stored[u], 16)
            steps(sp, STEPS, body)
            for u in range(SLOTS):
                sp.wait_ge(row_stored[u], 16 * STEPS)

        @block.gpsimd
        def _(pool):
            def body(step):
                through = counter(pool, step)
                for u in range(SLOTS):
                    take.gather(pool, step, u, through, (row_stored[u], through(16, 1)), (logit_in[u], through(1, 1)))
            steps(pool, STEPS, body)

        @block.scalar
        def _(act):
            take.first_windows(act)

            def body(step):
                through = counter(act, step)
                for u in range(SLOTS):
                    n = edge_places(step, u)
                    wait_apart(act, ph.entered, (take.here[u], take.all_here(step, u, through)))
                    act.activation(e[:, cols(step, u, n), :], take.rows[u][:, 0:n, D:ATT], ACT.Copy)\
                        .then_inc(logit_in[u], 1)
                    take.next_window(act, step, u, through)
            steps(act, STEPS, body)
            act.wait_ge(ready, 1)
            act.activation(e[:, 0:T, :], e[:, 0:T, :], ACT.Exp).then_inc(exp_in, 1)

        @block.tensor
        def _(pe):
            pe.wait_ge(opened, 1)
            pe.matmul(ps_sel[:, 0:HEADS], k.tail_sel[:, :], k.att_dst[:, T, :], start=True, stop=True)\
                .then_inc(turned, 1)
            pe.wait_ge(wide_in, 1)
            for n in range(2 * HEADS):
                ps = (ps_tail, ps_head)[n // HEADS]
                ins = pe.transpose(ps[:, (n % HEADS) * P:(n % HEADS + 1) * P], wide[:, n, :], k.ident[:, :])
            ins.then_inc(turned, 1)

        @block.vector
        def _(dve):
            done = [0]

            def then(ins):
                done[0] += 1
                ins.then_inc(link, 1)
                dve.wait_ge(link, done[0])

            d = k.att_dst
            then(dve.tensor_copy(reset[:, :], k.cont[:, 0:T]))
            dve.tensor_scalar(reset[:, :], reset[:, :], -1.0, HUGE, ALU.add, ALU.mult).then_inc(opened, 1)
            dve.wait_ge(opened, 1)
            dve.wait_ge(turned, 1)
            then(dve.scalar_tensor_tensor(out=d[:, T - 1, :], in0=d[:, T - 1, :], scalar=k.tail_ended[:, :],
                                          in1=ps_sel[:, 0:HEADS], op0=ALU.mult, op1=ALU.add))
            for h in range(HEADS):
                then(dve.tensor_tensor(values[:, :], d[:, 0:T, h], k.seg_end[:, :], ALU.mult))
                then(dve.tensor_tensor_scan(run[:, 0:T, h][:, ::-1], k.not_end[:, ::-1], values[:, ::-1], 0.0,
                                            ALU.mult, ALU.add))
                then(dve.tensor_tensor(run[:, 0:T, h], run[:, 0:T, h], k.not_head_closed[:, :], ALU.mult))
                then(dve.scalar_tensor_tensor(out=run[:, 0:T, h], in0=k.head_closed[:, :], scalar=d[:, T, h:h + 1],
                                              in1=run[:, 0:T, h], op0=ALU.mult, op1=ALU.add))
            for u in range(SLOTS):
                dve.wait_ge(logit_in[u], STEPS)
            then(dve.tensor_tensor(run[:, 0:T, :], run[:, 0:T, :], e[:, 0:T, :], ALU.add))
            then(dve.scalar_tensor_tensor(out=e[:, 0:T, :], in0=run[:, 0:T, :], scalar=0.2, in1=run[:, 0:T, :],
                                          op0=ALU.mult, op1=ALU.max))
            for h in range(HEADS):
                then(dve.tensor_tensor_scan(run[:, 0:T, h], reset[:, :], e[:, 0:T, h], 0.0, ALU.add, ALU.max))
                then(dve.tensor_copy(peak[:, 0, h:h + 1], run[:, T - 1, h:h + 1]))
                then(dve.tensor_scalar(values[:, :], k.in_head[:, :], -1.0, HUGE, ALU.add, ALU.mult))
                then(dve.tensor_tensor(values[:, :], values[:, :], e[:, 0:T, h], ALU.add))
                then(dve.tensor_reduce(peak[:, 1, h:h + 1], values[:, :], AX.X, ALU.max))
            flat = peak[:, :, :].rearrange("p s h -> p (s h)")
            dve.tensor_copy(wide[:, :, :], flat.unsqueeze(2).to_broadcast([P, 2 * HEADS, P])).then_inc(wide_in, 1)
            dve.wait_ge(turned, 2)
            for mine in range(2):
                for part, ps in enumerate((ps_tail, ps_head)):
                    then(dve.tensor_tensor(seen[:, :, :], ps[:, :].rearrange("p (h q) -> p h q", q=P),
                                           k.apart[:, 2 * mine + part, :].unsqueeze(1).to_broadcast([P, HEADS, P]),
                                           ALU.add))
                    out = whole[:, mine, :] if part == 0 else lone[:, :]
                    then(dve.tensor_reduce(out, seen[:, :, :], AX.X, ALU.max))
                then(dve.tensor_tensor(whole[:, mine, :], whole[:, mine, :], lone[:, :], ALU.max))
            then(dve.tensor_copy(run[:, T - 1, :], whole[:, 0, :]))
            for h in range(HEADS):
                then(dve.tensor_tensor(values[:, :], run[:, 0:T, h], k.seg_end[:, :], ALU.mult))
                then(dve.tensor_tensor_scan(run[:, 0:T, h][:, ::-1], k.not_end[:, ::-1], values[:, ::-1], 0.0,
                                            ALU.mult, ALU.add))
                then(dve.tensor_scalar(values[:, :], k.in_head[:, :], -1.0, -1.0, ALU.add, ALU.mult))
                then(dve.tensor_tensor(run[:, 0:T, h], run[:, 0:T, h], values[:, :], ALU.mult))
                then(dve.scalar_tensor_tensor(out=run[:, 0:T, h], in0=k.in_head[:, :], scalar=whole[:, 1, h:h + 1],
                                              in1=run[:, 0:T, h], op0=ALU.mult, op1=ALU.add))
            dve.tensor_tensor(e[:, 0:T, :], e[:, 0:T, :], run[:, 0:T, :], ALU.subtract).then_inc(ready, 1)
    ph.close()


def rows_from_columns(dve, pe, k, columns, rows, wide, ps, wide_in, turned):
    if dve is not None:
        for n, column in enumerate(columns):
            ins = dve.tensor_copy(wide[:, n, :], column.to_broadcast([D, P]))
        ins.then_inc(wide_in, 1)
        dve.wait_ge(turned, 1)
        for n, row in enumerate(rows):
            dve.tensor_copy(row, ps[:, n * P:n * P + D])
    else:
        pe.wait_ge(wide_in, 1)
        for n in range(len(columns)):
            ins = pe.transpose(ps[:, n * P:n * P + D], wide[:, n, :], k.ident[0:D, 0:D])
        ins.then_inc(turned, 1)


class DenseOutput:

    def __init__(self, ph, k, out):
        self.k, self.out = k, out
        self.x, self.y_scaled, self.z, self.c, self.new = (
            four(ph.sb, n, [P, J, D]) for n in ("x", "y_scaled", "z", "c", "new"))
        self.xt = four(ph.sb, "xt", [D + 1, GROUP])
        self.ps_x, self.ps_y = ph.ps("ps_x"), ph.ps("ps_y")
        self.norm = Norm(ph, "norm", DENSE_SLOTS)
        self.loaded, self.turned, self.copied, self.made, self.scaled_in, self.shifted, self.z_in, self.c_in, \
            self.new_in, self.stored = (
                four(ph.sem, n) for n in ("loaded", "turned", "copied", "made", "scaled_in", "shifted", "z_in",
                                          "c_in", "new_in", "stored"))
        self.ones_set = ph.sem("ones_set")

    def groups(self, step):
        return [(u, dense_parts(step, u)) for u in range(DENSE_SLOTS)]

    def load(self, sp, step, u, n=P):
        at = u % DENSE_SLOTS
        if u == DENSE_SLOTS - 1:
            wait(sp, self.z_in[u], counter(sp, step)(1, 1))
        sp.dma_start(self.x[at][0:n], dense_rows(self.k.t_x3, step, u, n)).then_inc(self.loaded[at], 16)

    def sync_begin(self, sp, step):
        load_ahead(sp, step, lambda step, u, n: self.load(sp, step, u, n))

    def sync_body(self, sp, step):
        through = counter(sp, step)
        if not is_last(step):
            for u in range(DENSE_SLOTS - 1):
                sp.wait_ge(self.z_in[u], through(1))
                self.load(sp, step, u + DENSE_SLOTS)
        for u, n in self.groups(step):
            sp.wait_ge(self.new_in[u], through(1))
            sp.dma_start(dense_rows(self.out, step, u, n), self.new[u][0:n]).then_inc(self.stored[u], 16)

    def sync_end(self, sp):
        for u in range(DENSE_SLOTS):
            sp.wait_ge(self.stored[u], 16 * STEPS)

    def tensor_front(self, pe, step):
        k, through = self.k, counter(pe, step)

        def turn(u, n):
            pe.wait_ge(self.loaded[u], through(16))
            wait(pe, *group_before(self.copied, u, through))
            for j in range(J):
                ins = pe.transpose(self.ps_x[0:D, j * P:j * P + n], self.x[u][0:n, j, :], k.ident[0:n, 0:n])
            ins.then_inc(self.turned[u], 1)

        def product(u, n):
            pe.wait_ge(self.copied[u], through(1))
            wait(pe, *group_before(self.scaled_in, u, through))
            for j in range(J):
                ins = pe.matmul(self.ps_y[0:n, j * D:(j + 1) * D], self.xt[u][:, j * P:j * P + n], k.w_node[:, :],
                                start=True, stop=True)
            ins.then_inc(self.made[u], 1)

        groups = self.groups(step)
        turn(*groups[0])
        for u in range(1, DENSE_SLOTS):
            turn(*groups[u])
            product(*groups[u - 1])
        product(*groups[-1])

    def scalar_front(self, act, step):
        through = counter(act, step)
        for u, n in self.groups(step):
            act.wait_ge(self.turned[u], through(1))
            wait(act, self.made[u], through(1, 1))
            if n == P:
                act.activation(self.xt[u][0:D, :], self.ps_x[0:D, :], ACT.Copy).then_inc(self.copied[u], 1)
            else:
                for j in range(J):
                    ins = act.activation(self.xt[u][0:D, j * P:j * P + n], self.ps_x[0:D, j * P:j * P + n], ACT.Copy)
                ins.then_inc(self.copied[u], 1)

    def scalar_back(self, act, step):
        through = counter(act, step)
        for u, n in self.groups(step):
            self.norm.take_root(act, u, through, 1.0, self.k.eps[0:n, :], n)

    def vector_begin(self, dve):
        for u in range(DENSE_SLOTS):
            ins = dve.memset(self.xt[u][D:D + 1, :], 1.0)
        ins.then_inc(self.ones_set, 1)

    def vector_front(self, dve, step):
        k, through = self.k, counter(dve, step)
        for u, n in self.groups(step):
            dve.wait_ge(self.loaded[u], through(16))
            wait(dve, self.c_in[u], through(1, 1))
            dve.tensor_tensor(self.c[u][0:n], self.x[u][0:n], every_place(k.node_shift, n), ALU.add)\
                .then_inc(self.shifted[u], 1)
            dve.wait_ge(self.made[u], through(1))
            dve.scalar_tensor_tensor(
                out=self.y_scaled[u][0:n], in0=self.ps_y[0:n, 0:J * D].rearrange("p (j c) -> p j c", c=D), scalar=0.0,
                in1=every_place(k.node_scale, n), op0=ALU.max, op1=ALU.mult).then_inc(self.scaled_in[u], 1)
        for u, n in self.groups(step):
            dve.wait_ge(self.shifted[u], through(1))
            dve.wait_ge(self.scaled_in[u], through(1))
            dve.tensor_tensor(self.z[u][0:n], self.c[u][0:n], self.y_scaled[u][0:n], ALU.add)\
                .then_inc(self.z_in[u], 1)
        for u, n in self.groups(step):
            dve.wait_ge(self.z_in[u], through(1))
            self.norm.spread(dve, u, self.z[u][0:n], through, n)

    def vector_back(self, dve, step):
        norm, through = self.norm, counter(dve, step)
        for u, n in self.groups(step):
            dve.wait_ge(norm.var_in[u], through(1))
            dve.tensor_tensor(self.c[u][0:n], self.z[u][0:n], norm.mean(u, n), ALU.subtract)\
                .then_inc(self.c_in[u], 1)
        for u, n in self.groups(step):
            norm.invert(dve, u, through, n)
            dve.wait_ge(self.c_in[u], through(1))
            wait(dve, self.stored[u], through(16, 1))
            dve.tensor_tensor(self.new[u][0:n], self.c[u][0:n], norm.inverse(u, n), ALU.mult)\
                .then_inc(self.new_in[u], 1)


def message_round(nc, k, out):
    ph = Phase(nc, "msg")
    src = Rows(ph, k.t_x3, k.src_idx)
    ph.name = "msg_dst"
    dst = Rows(ph, k.t_x3, k.own_idx, head_too=True)
    ph.name = "msg"
    ef = EdgeFeatures(ph, k, 2)
    src_t, dst_t = ph.pair(ph.sb, "src_t", [D, GROUP]), ph.pair(ph.sb, "dst_t", [D, GROUP])
    feat_t = ph.pair(ph.sb, "feat_t", [D + 1, GROUP])
    rows = ph.pair(ph.sb, "rows", [P, J, D])
    acc, cont = ph.pair(ph.sb, "acc", [P, J, D]), ph.pair(ph.sb, "cont", [P, J])
    head_part = ph.sb("head_part", [P, D])
    stat, lone = ph.sb("stat", [D, 2 * STEPS + 1, 6]), ph.sb("lone", [D, TH])
    mv, root, both = ph.sb("mv", [D, 2]), ph.sb("root", [D, 1]), ph.sb("both", [D, 2])
    wide = ph.sb("wide", [D, 2, P])
    ps_s, ps_d, ps_m, ps_z = (ph.ps(n) for n in ("ps_s", "ps_d", "ps_m", "ps_z"))
    ps_c = ps_s
    dense = DenseOutput(ph.part("dense_out"), k, out)
    link = [ph.pair(ph.sem, f"summed{j}_") for j in range(J)]
    (src_turned, dst_turned, src_copied, dst_copied, rows_made, rows_in, across_turned, across_read,
     acc_stored, dst_stored, windows) = (
        ph.pair(ph.sem, n) for n in ("src_turned", "dst_turned", "src_copied", "dst_copied", "rows_made",
                                     "rows_in", "across_turned", "across_read", "acc_stored",
                                     "dst_stored", "windows"))
    carried, head_here, ones_set, bias_in, stat_in, var_in, rooted, chain, wide_in, wide_turned = (
        ph.sem(n) for n in ("carried", "head_here", "ones_set", "bias_in", "stat_in", "var_in", "rooted", "chain",
                            "wide_in", "wide_turned"))

    with nc.Block() as block:
        @block.sync
        def _(sp):
            sp.sem_inc(ph.entered, 1)
            sp.dma_start(k.w_feat[D:D + 1, :], k.msg_bias[0:1, :]).then_inc(bias_in, 16)

            def body(step):
                through = counter(sp, step)
                dense.sync_begin(sp, step)
                for u in range(SLOTS):
                    n = edge_places(step, u)
                    sp.wait_ge(dst.here[u], through(16 * J))
                    sp.dma_start(k.l_xd[:, cols(step, u), :], dst.rows[u][:, :, :]).then_inc(dst_stored[u], 16)
                    if u == 0:
                        if not (isinstance(step, int) and step == 0):
                            store(step - 1, 1)
                    else:
                        store(step, 0)
                dense.sync_body(sp, step)

            def store(step, u):
                n = edge_places(step, u)
                sp.wait_ge(link[n - 1][u], counter(sp, step)(1))
                sp.dma_start(k.l_acc[:, cols(step, u, n), :], acc[u][:, 0:n, :]).then_inc(acc_stored[u], 16)
            steps(sp, STEPS, body)
            dense.sync_end(sp)
            store(STEPS - 1, 1)
            sp.wait_ge(link[J - 1][1], STEPS)
            sp.dma_start(k.l_acc[:, T:TH, :], acc[1][:, J - 1:J, :]).then_inc(acc_stored[1], 16)
            sp.wait_ge(acc_stored[0], 16 * STEPS)
            sp.wait_ge(acc_stored[1], 16 * STEPS + 16)
            for u in range(SLOTS):
                sp.wait_ge(dst_stored[u], 16 * STEPS)

        @block.gpsimd
        def _(pool):
            def body(step):
                through = counter(pool, step)
                for u in range(SLOTS):
                    src.gather(pool, step, u, through, (src_turned[u], through(1, 1)))
                    dst.gather(pool, step, u, through, (dst_turned[u], through(1, 1)), (dst_stored[u], through(16, 1)))
            steps(pool, STEPS, body)
            pool.wait_ge(acc_stored[0], 16 * STEPS)
            pool.wait_ge(acc_stored[1], 16 * STEPS)
            pool.indirect_dma_start(
                out=head_part[:, :], out_offset=None, in_=k.l_acc.rearrange("p t c -> (p t) c"),
                in_offset=bass.IndirectOffsetOnAxis(ap=k.head_row[:, 0:1], axis=0)).then_inc(head_here, 16)

        @block.scalar
        def _(act):
            src.first_windows(act)
            dst.first_windows(act)

            def front(step, u):
                through = counter(act, step)
                n = edge_places(step, u) * P
                wait_apart(act, ph.entered, (link[J - 1][u], through(1, 1)))
                act.activation(cont[u][:, :], k.cont[:, cols(step, u)], ACT.Copy).then_inc(windows[u], 1)
                ef.take(act, step, u, through)
                act.wait_ge(src_turned[u], through(1))
                wait(act, rows_made[u], through(1, 1))
                act.activation(src_t[u][:, 0:n], ps_s[0:D, 0:n], ACT.Copy).then_inc(src_copied[u], 1)
                act.wait_ge(ef.turned[u], through(1))
                wait(act, ef.made[u], through(1, 1))
                act.activation(ef.attr_t[u][:, 0:n], ef.ps_attr[u][0:5, 0:n], ACT.Copy).then_inc(ef.copied[u], 1)
                src.next_window(act, step, u, through)
                dst.next_window(act, step, u, through)

            def back(step, u):
                through = counter(act, step)
                n = edge_places(step, u) * P
                act.wait_ge(ef.made[u], through(1))
                act.activation(feat_t[u][0:D, 0:n], ef.ps_feat[u][0:D, 0:n], ACT.Relu).then_inc(ef.kept[u], 1)
                act.wait_ge(rows_made[u], through(1))
                wait(act, link[J - 1][u], through(1, 1))
                wait(act, across_turned[u], through(1, 1))
                act.activation(rows_of(rows[u][:, :, :])[:, 0:n // P * D], ps_m[:, 0:n // P * D],
                               ACT.Relu).then_inc(rows_in[u], 1)
            shared_turns(act, front, back, None, dense.scalar_front, dense.scalar_back)
            column_scale(None, act, None, None, mv, root[:, :], None, None, (var_in, rooted, chain), k, True)

        @block.tensor
        def _(pe):
            pe.wait_ge(ones_set, 1)
            pe.wait_ge(bias_in, 16)
            pe.wait_ge(dense.ones_set, 1)

            def front(step, u):
                through = counter(pe, step)
                n = edge_places(step, u)
                pe.wait_ge(src.here[u], src.all_here(step, u, through))
                wait(pe, *group_before(src_copied, u, through))
                for j in range(n):
                    ins = pe.transpose(ps_s[0:D, j * P:(j + 1) * P], src.rows[u][:, j, :], k.ident[:, :])
                ins.then_inc(src_turned[u], 1)
                pe.wait_ge(dst.here[u], through(16 * J))
                wait(pe, *group_before(dst_copied, u, through))
                for j in range(n):
                    ins = pe.transpose(ps_d[0:D, j * P:(j + 1) * P], dst.rows[u][:, j, :], k.ident[:, :])
                ins.then_inc(dst_turned[u], 1)
                wait(pe, ef.kept[u], through(1, 1))
                ef.turn(pe, step, u, through)

            def back(step, u):
                through = counter(pe, step)
                n = edge_places(step, u)
                pe.wait_ge(ef.copied[u], through(1))
                pe.matmul(ef.ps_feat[u][0:D, 0:n * P], k.w_edge[:, :], ef.attr_t[u][:, 0:n * P],
                          start=True, stop=True).then_inc(ef.made[u], 1)
                pe.wait_ge(src_copied[u], through(1))
                pe.wait_ge(dst_copied[u], through(1))
                pe.wait_ge(ef.kept[u], through(1))
                wait(pe, *group_before(rows_in, u, through))
                for j in range(n):
                    at = slice(j * P, (j + 1) * P)
                    out = ps_m[:, j * D:(j + 1) * D]
                    pe.matmul(out, src_t[u][:, at], k.w_msg[:, 0, :], start=True, stop=False)
                    pe.matmul(out, dst_t[u][:, at], k.w_msg[:, 1, :], start=False, stop=False)
                    ins = pe.matmul(out, feat_t[u][:, at], k.w_feat[:, :], start=False, stop=True)
                ins.then_inc(rows_made[u], 1)

            def tail(step, u):
                through = counter(pe, step)
                n = edge_places(step, u)
                pe.wait_ge(rows_in[u], through(1))
                wait(pe, *group_before(across_read, u, through))
                for j in range(n):
                    ins = pe.transpose(ps_z[0:D, j * P:(j + 1) * P], rows[u][:, j, :], k.ident[:, :])
                ins.then_inc(across_turned[u], 1)
                if is_last(step) and u == SLOTS - 1:
                    pe.wait_ge(link[J - 2][u], STEPS)
                    pe.matmul(ps_c[:, 0:D], k.carry_sel[:, :], acc[u][:, J - 2, :], start=True, stop=True)\
                        .then_inc(carried, 1)
            shared_turns(pe, front, back, tail, dense.tensor_front, None)
            rows_from_columns(None, pe, k, [None] * 2, None, wide, ps_c, wide_in, wide_turned)

        @block.vector
        def _(dve):
            for u in range(SLOTS):
                dve.memset(feat_t[u][D:D + 1, :], 1.0)
            dve.memset(acc[1][:, J - 1, :], 0.0).then_inc(ones_set, 1)
            dve.wait_ge(ones_set, 1)
            dense.vector_begin(dve)

            def front(step, u):
                through = counter(dve, step)
                n = edge_places(step, u) * P
                dve.wait_ge(dst_turned[u], through(1))
                wait(dve, rows_made[u], through(1, 1))
                dve.tensor_copy(dst_t[u][:, 0:n], ps_d[0:D, 0:n]).then_inc(dst_copied[u], 1)

            def back(step, u):
                through = counter(dve, step)
                n = edge_places(step, u)
                dve.wait_ge(rows_in[u], through(1))
                dve.wait_ge(windows[u], through(1))
                wait(dve, acc_stored[u], through(16, 1))
                for j in range(n):
                    if j:
                        dve.wait_ge(link[j - 1][u], through(1))
                        before = acc[u][:, j - 1, :]
                    else:
                        wait(dve, link[J - 1][1 - u], through(1, 1) if u == 0 else through(1))
                        before = acc[1 - u][:, J - 1, :]
                    dve.scalar_tensor_tensor(out=acc[u][:, j, :], in0=before, scalar=cont[u][:, j:j + 1],
                                             in1=rows[u][:, j, :], op0=ALU.mult, op1=ALU.add).then_inc(link[j][u], 1)
                if n < J:
                    dve.wait_ge(carried, 1)
                    dve.wait_ge(head_here, 16)
                    dve.tensor_tensor(acc[u][:, J - 1, :], ps_c[:, 0:D], head_part[:, :],
                                      ALU.add).then_inc(link[J - 1][u], 1)

            def tail(step, u):
                through = counter(dve, step)
                wait_apart(dve, ph.entered, (across_turned[u], through(1)))
                column_stats(dve, ph, stat, lone, ps_z[0:D, :], step, u).then_inc(across_read[u], 1)
            shared_turns(dve, front, back, tail, dense.vector_front, dense.vector_back)
            dve.wait_ge(across_read[0], STEPS)
            dve.wait_ge(across_read[1], STEPS)
            dve.bn_stats(stat[:, 2 * STEPS, :], lone[:, 0:LAST]).then_inc(stat_in, 1)
            dve.wait_ge(stat_in, 1)
            dve.bn_aggr(mv[:, :], stat[:, :, :].rearrange("c a s -> c (a s)")).then_inc(var_in, 1)
            column_scale(dve, None, k.l3_cols[:, 4:5], k.l3_cols[:, 5:6], mv, root[:, :], both[:, 0:1],
                         both[:, 1:2], (var_in, rooted, chain), k, False)
            rows_from_columns(dve, None, k, [both[:, 0:1], both[:, 1:2]], [k.msg_scale[:, :], k.msg_shift[:, :]],
                              wide, ps_c, wide_in, wide_turned)
    ph.close()


def node_stats(nc, k):
    ph = Phase(nc, "stats")
    x, xt, across = four(ph.sb, "x", [P, J, D]), four(ph.sb, "xt", [D + 1, GROUP]), four(ph.sb, "across", [D, GROUP])
    ps_x, ps_z = ph.pair(ph.ps, "ps_x"), four(ph.ps, "ps_z")
    ps_w = ph.ps("ps_w")
    stat = ph.sb("stat", [D, DENSE_FULL + 1, 6])
    mv, root, both, wide = ph.sb("mv", [D, 2]), ph.sb("root", [D, 1]), ph.sb("both", [D, 2]), ph.sb("wide", [D, 2, P])
    loaded, turned, copied, made, kept, read = (
        four(ph.sem, n) for n in ("loaded", "turned", "copied", "made", "kept", "read"))
    ones_set, var_in, rooted, chain, wide_in, wide_turned = (
        ph.sem(n) for n in ("ones_set", "var_in", "rooted", "chain", "wide_in", "wide_turned"))

    with nc.Block() as block:
        @block.sync
        def _(sp):
            sp.sem_inc(ph.entered, 1)

            def body(step):
                through = counter(sp, step)
                for u in range(DENSE_SLOTS):
                    n = dense_parts(step, u)
                    wait(sp, turned[u], through(1, 1))
                    sp.dma_start(x[u][0:n], dense_rows(k.t_x3, step, u, n)).then_inc(loaded[u], 16)
            steps(sp, STEPS, body)

        @block.tensor
        def _(pe):
            pe.wait_ge(ones_set, 1)

            def body(step):
                through = counter(pe, step)
                for u in range(DENSE_SLOTS):
                    n = dense_parts(step, u)
                    pe.wait_ge(loaded[u], through(16))
                    bank_free(pe, copied, u, through)
                    for j in range(J):
                        ins = pe.transpose(ps_x[u % 2][0:D, j * n:(j + 1) * n], x[u][0:n, j, :], k.ident[0:n, 0:n])
                    ins.then_inc(turned[u], 1)
                for u in range(DENSE_SLOTS):
                    n = dense_parts(step, u) * J
                    pe.wait_ge(copied[u], through(1))
                    wait(pe, kept[u], through(1, 1))
                    pe.matmul(ps_z[u][0:D, 0:n], k.w_node[:, :], xt[u][:, 0:n], start=True, stop=True)\
                        .then_inc(made[u], 1)
            steps(pe, STEPS, body)
            rows_from_columns(None, pe, k, [None] * 2, None, wide, ps_w, wide_in, wide_turned)

        @block.scalar
        def _(act):
            def body(step):
                through = counter(act, step)
                for u in range(DENSE_SLOTS):
                    n = dense_parts(step, u) * J
                    act.wait_ge(turned[u], through(1))
                    wait(act, made[u], through(1, 1))
                    act.activation(xt[u][0:D, 0:n], ps_x[u % 2][0:D, 0:n], ACT.Copy).then_inc(copied[u], 1)
                for u in range(DENSE_SLOTS):
                    n = dense_parts(step, u) * J
                    act.wait_ge(made[u], through(1))
                    wait(act, read[u], through(1, 1))
                    act.activation(across[u][:, 0:n], ps_z[u][0:D, 0:n], ACT.Relu).then_inc(kept[u], 1)
            steps(act, STEPS, body)
            column_scale(None, act, None, None, mv, root[:, :], None, None, (var_in, rooted, chain), k, True)

        @block.vector
        def _(dve):
            for u in range(DENSE_SLOTS):
                ins = dve.memset(xt[u][D:D + 1, :], 1.0)
            ins.then_inc(ones_set, 1)
            def body(step):
                through = counter(dve, step)
                for u in range(DENSE_SLOTS):
                    n = dense_parts(step, u) * J
                    wait_apart(dve, ph.entered, (kept[u], through(1)))
                    dve.bn_stats(stat[:, bass.ds(step * DENSE_SLOTS + u, 1), :].rearrange("c a s -> c (a s)"),
                                 across[u][:, 0:n]).then_inc(read[u], 1)
            steps(dve, STEPS, body)
            for u in range(DENSE_SLOTS):
                dve.wait_ge(read[u], STEPS)
            dve.bn_aggr(mv[:, :], stat[:, :, :].rearrange("c a s -> c (a s)")).then_inc(var_in, 1)
            column_scale(dve, None, k.l3_cols[:, 0:1], k.l3_cols[:, 1:2], mv, root[:, :], both[:, 0:1],
                         both[:, 1:2], (var_in, rooted, chain), k, False)
            rows_from_columns(dve, None, k, [both[:, 0:1], both[:, 1:2]], [k.node_scale[:, :], k.node_shift[:, :]],
                              wide, ps_w, wide_in, wide_turned)
    ph.close()


def output_pass(nc, k, out):
    ph = Phase(nc, "out_edges")
    put = Rows(ph, None, None, out, k.out_idx)
    x, y_scaled, z, c, new = (ph.pair(ph.sb, n, [P, J, D]) for n in ("x", "y_scaled", "z", "c", "new"))
    xt = ph.pair(ph.sb, "xt", [D + 1, GROUP])
    ps_x, ps_y = ph.pair(ph.ps, "ps_x"), ph.pair(ph.ps, "ps_y")
    norm = Norm(ph, "norm")
    loaded, turned, copied, made, scaled_in, shifted, z_in, c_in, new_in = (
        ph.pair(ph.sem, n) for n in ("loaded", "turned", "copied", "made", "scaled_in", "shifted", "z_in", "c_in",
                                     "new_in"))
    ones_set = ph.sem("ones_set")
    sums, sums_in = ph.pair(ph.sb, "sums", [P, J, D]), ph.pair(ph.sem, "sums_in")
    parts = ph.pair(ph.sb, "parts", [P, J, D])
    part_a, part_b, part_c, placed = (ph.pair(ph.sem, n) for n in ("part_a", "part_b", "part_c", "placed"))

    with nc.Block() as block:
        @block.sync
        def _(sp):
            sp.sem_inc(ph.entered, 1)

            def body(step):
                through = counter(sp, step)
                for u in range(SLOTS):
                    wait(sp, z_in[u], through(1, 1))
                    sp.dma_start(sums[u][:, :, :], k.l_acc[:, cols(step, u), :]).then_inc(sums_in[u], 16)
                    sp.dma_start(x[u][:, :, :], k.l_xd[:, cols(step, u), :]).then_inc(loaded[u], 16)
            steps(sp, STEPS, body)

        @block.gpsimd
        def _(pool):
            bound = pool.to_reg(N - 1)

            def body(step):
                through = counter(pool, step)
                for u in range(SLOTS):
                    put.scatter(pool, new[u], u, through, new_in[u], bound)
            steps(pool, STEPS, body)
            for u in range(SLOTS):
                pool.wait_ge(put.gone[u], 16 * J * STEPS)

        @block.tensor
        def _(pe):
            pe.wait_ge(ones_set, 1)

            def body(step):
                through = counter(pe, step)
                for u in range(SLOTS):
                    pe.wait_ge(loaded[u], through(16))
                    wait(pe, copied[u], through(1, 1))
                    for j in range(J):
                        ins = pe.transpose(ps_x[u][0:D, j * P:(j + 1) * P], x[u][:, j, :], k.ident[:, :])
                    ins.then_inc(turned[u], 1)
                for u in range(SLOTS):
                    pe.wait_ge(copied[u], through(1))
                    wait(pe, scaled_in[u], through(1, 1))
                    for j in range(J):
                        ins = pe.matmul(ps_y[u][:, j * D:(j + 1) * D], xt[u][:, j * P:(j + 1) * P], k.w_node[:, :],
                                        start=True, stop=True)
                    ins.then_inc(made[u], 1)
            steps(pe, STEPS, body)

        @block.scalar
        def _(act):
            def body(step):
                through = counter(act, step)
                for u in range(SLOTS):
                    act.wait_ge(turned[u], through(1))
                    wait(act, made[u], through(1, 1))
                    act.activation(xt[u][0:D, :], ps_x[u][0:D, :], ACT.Copy).then_inc(copied[u], 1)
                for u in range(SLOTS):
                    put.put_window(act, step, u, through)
                    norm.take_root(act, u, through, 1.0, k.eps[:, :])
            steps(act, STEPS, body)

        @block.vector
        def _(dve):
            for u in range(SLOTS):
                ins = dve.memset(xt[u][D:D + 1, :], 1.0)
            ins.then_inc(ones_set, 1)
            def body(step):
                through = counter(dve, step)
                for u in range(SLOTS):
                    dve.tensor_tensor(parts[u][:, :, :], over_rows(k.cnt[:, cols(step, u)], D),
                                      every_place(k.msg_shift, P), ALU.mult).then_inc(part_a[u], 1)
                    dve.wait_ge(sums_in[u], through(16))
                    dve.tensor_tensor(sums[u][:, :, :], sums[u][:, :, :], every_place(k.msg_scale, P),
                                      ALU.mult).then_inc(part_b[u], 1)
                    dve.wait_ge(part_a[u], through(1))
                    dve.wait_ge(part_b[u], through(1))
                    dve.tensor_tensor(parts[u][:, :, :], parts[u][:, :, :], sums[u][:, :, :],
                                      ALU.add).then_inc(part_c[u], 1)
                    dve.wait_ge(loaded[u], through(16))
                    wait(dve, c_in[u], through(1, 1))
                    dve.tensor_tensor(c[u][:, :, :], x[u][:, :, :], every_place(k.node_shift, P), ALU.add)\
                        .then_inc(placed[u], 1)
                    dve.wait_ge(made[u], through(1))
                    dve.scalar_tensor_tensor(
                        out=y_scaled[u][:, :, :], in0=ps_y[u][:, 0:J * D].rearrange("p (j c) -> p j c", c=D), scalar=0.0,
                        in1=every_place(k.node_scale, P), op0=ALU.max, op1=ALU.mult).then_inc(scaled_in[u], 1)
                    dve.wait_ge(placed[u], through(1))
                    dve.wait_ge(part_c[u], through(1))
                    dve.tensor_tensor(c[u][:, :, :], c[u][:, :, :], parts[u][:, :, :], ALU.add)\
                        .then_inc(shifted[u], 1)
                for u in range(SLOTS):
                    dve.wait_ge(shifted[u], through(1))
                    dve.wait_ge(scaled_in[u], through(1))
                    dve.tensor_tensor(z[u][:, :, :], c[u][:, :, :], y_scaled[u][:, :, :], ALU.add).then_inc(z_in[u], 1)
                for u in range(SLOTS):
                    dve.wait_ge(z_in[u], through(1))
                    norm.spread(dve, u, z[u][:, :, :], through)
                for u in range(SLOTS):
                    dve.wait_ge(norm.var_in[u], through(1))
                    dve.tensor_tensor(c[u][:, :, :], z[u][:, :, :], norm.mean(u), ALU.subtract).then_inc(c_in[u], 1)
                for u in range(SLOTS):
                    norm.invert(dve, u, through)
                    dve.wait_ge(c_in[u], through(1))
                    wait(dve, put.gone[u], through(16 * J, 1))
                    dve.tensor_tensor(new[u][:, :, :], c[u][:, :, :], norm.inverse(u), ALU.mult).then_inc(new_in[u], 1)
            steps(dve, STEPS, body)
    ph.close()


class Kept:

    def __init__(self, nc, stack):
        def sb(name, shape, dt=F32):
            return stack.enter_context(nc.sbuf_tensor(name, shape, dt))

        def dram(name, shape):
            return nc.dram_tensor(name, shape, F32).ap()

        self.src_idx, self.own_idx, self.out_idx = (sb(n, [P, TH], I32) for n in ("src_idx", "own_idx", "out_idx"))
        self.head_row = sb("head_row", [P, 1], I32)
        self.cont, self.cnt, self.dinv = (sb(n, [P, TH]) for n in ("cont", "cnt", "dinv"))
        self.in_head, self.seg_end, self.not_end, self.head_closed, self.not_head_closed = (
            sb(n, [P, T]) for n in ("in_head", "seg_end", "not_end", "head_closed", "not_head_closed"))
        self.tail_ended, self.eps = sb("tail_ended", [P, 1]), sb("eps", [P, 1])
        self.carry_sel, self.tail_sel, self.ident = (sb(n, [P, P]) for n in ("carry_sel", "tail_sel", "ident"))
        self.apart = sb("apart", [P, 4, P])
        self.att_dst, self.att_e = sb("att_dst", [P, TH, HEADS]), sb("att_e", [P, TH, HEADS])
        self.edge_in = sb("edge_in", [P, TH, 5])
        self.w_gcn = [sb(f"w_gcn{i}", [D + 1, D]) for i in range(2)]
        self.w_self = [sb(f"w_self{i}", [D + 1, D]) for i in range(2)]
        self.w_agg = [sb(f"w_agg{i}", [D + 1, D]) for i in range(2)]
        self.w_att = [sb(f"w_att{i}", [D, ATT_ALL]) for i in range(3)]
        self.gat_bias = sb("gat_bias", [D, 3])
        self.gat_bias_row, self.gat_rest_row = sb("gat_bias_row", [P, D]), sb("gat_rest_row", [P, D])
        self.wide_bias = sb("wide_bias", [D, 2, P])
        self.att_rest = [sb(f"att_rest{i}", [P, J, ATT]) for i in range(2)]
        self.w_node, self.w_edge = sb("w_node", [D + 1, D]), sb("w_edge", [5, D])
        self.w_msg, self.w_feat = sb("w_msg", [D, 3, D]), sb("w_feat", [D + 1, D])
        self.l3_cols, self.edge_scale, self.msg_bias = sb("l3_cols", [D, 8]), sb("edge_scale", [D, 1]), sb("msg_bias", [1, D])
        self.msg_scale, self.msg_shift, self.node_scale, self.node_shift = (
            sb(n, [P, D]) for n in ("msg_scale", "msg_shift", "node_scale", "node_shift"))
        self.t_x, self.t_h1, self.t_x1, self.t_y1, self.t_x3 = (
            dram(n, (N, D)) for n in ("t_x", "t_h1", "t_x1", "t_y1", "t_x3"))
        self.t_att = [dram(f"t_att{i}", (N, ATT)) for i in range(3)]
        self.base_copied = nc.alloc_semaphore("base_copied")
        self.l_x, self.l_s, self.l_h1, self.l_x1, self.l_y1, self.l_x2, self.l_xd, self.l_acc = (
            dram(n, (P, TH, D)) for n in ("l_x", "l_s", "l_h1", "l_x1", "l_y1", "l_x2", "l_xd", "l_acc"))
        self.l_msg, self.l_acc100 = dram("l_msg", (P, TH, ATT)), dram("l_acc100", (P, TH, ATT))


def gnn_resnorm(nc, a, out):
    with ExitStack() as stack:
        k = Kept(nc, stack)
        prepare(nc, a, k)
        own_rows(nc, a, k)
        node_round(nc, a, k, GCN1, k.t_x, k.t_h1, own=k.l_s, keep=k.l_h1, layer=0)
        node_round(nc, a, k, GCN2, k.t_h1, k.t_x1, own=k.l_h1, rest=k.l_x, keep=k.l_x1, layer=1)
        node_round(nc, a, k, SAGE1, k.t_x1, k.t_y1, own=k.l_x1, keep=k.l_y1, layer=0)
        node_round(nc, a, k, SAGE2, k.t_y1, k.t_att[0], own=k.l_y1, rest=k.l_x1, keep=k.l_x2, layer=1)
        attention_weights(nc, k, k.t_att[0], 0)
        node_round(nc, a, k, GAT1, out=k.t_att[1], layer=0)
        attention_weights(nc, k, k.t_att[1], 1)
        node_round(nc, a, k, GAT2, out=k.t_att[2], layer=1)
        attention_weights(nc, k, k.t_att[2], 2)
        node_round(nc, a, k, GAT3, out=k.t_x3, rest=k.l_x2, layer=2)
        node_stats(nc, k)
        message_round(nc, k, out)
        output_pass(nc, k, out)


_INS = ["x", "src", "dst", "edge_attr_4", "L0_gnn_W1", "L0_gnn_b1", "L0_gnn_W2", "L0_gnn_b2", "L1_gnn_W0", "L1_gnn_b0",
        "L1_gnn_W1", "L1_gnn_b1", "L1_gnn_W2", "L1_gnn_b2", "L2_gnn_W", "L2_gnn_att_src", "L2_gnn_att_dst",
        "L2_gnn_bias", "L3_gnn_W_node", "L3_gnn_b_node", "L3_gnn_g_node", "L3_gnn_beta_node", "L3_gnn_W_edge",
        "L3_gnn_b_edge", "L3_gnn_g_edge", "L3_gnn_beta_edge", "L3_gnn_W_msg", "L3_gnn_b_msg", "L3_gnn_g_msg",
        "L3_gnn_beta_msg"]


def kernel(**inputs):
    import concourse.bacc as bacc
    from concourse.bass_utils import run_bass_kernel_spmd as run

    nc = bacc.Bacc("TRN2", target_bir_lowering=False, num_devices=1)
    arrays, args = {}, {}
    for name in _INS:
        array = np.ascontiguousarray(inputs[name])
        arrays[f"in_{name}"] = array
        args[name] = nc.dram_tensor(f"in_{name}", array.shape, mybir.dt.from_np(array.dtype), kind="ExternalInput").ap()
    out = nc.dram_tensor("out_rows", (N, D), F32, kind="ExternalOutput").ap()
    gnn_resnorm(nc, args, out)
    return run(nc, [arrays], core_ids=[0]).results[0]["out_rows"]
```

```python
import numpy as np
import concourse.bass as bass
from concourse import mybir
from contextlib import ExitStack

F32, I32 = mybir.dt.float32, mybir.dt.int32
ALU, ACT, AX = mybir.AluOpType, mybir.ActivationFunctionType, mybir.AxisListType

P = 128
N, E, D = 100000, 50000, 96
HEADS, CH = 4, 24
ATT = D + HEADS
ATT_ALL = ATT + HEADS
T = -(-E // P)
TH = T + 1
LAST = E - (P - 1) * T
J = 4
SLOTS = 2
STEPS = TH // (J * SLOTS)
assert STEPS * J * SLOTS == TH
FAR = 1 << 20
GROUP = P * J
DENSE_FULL = N // GROUP
REST = (N - DENSE_FULL * GROUP) // J
assert REST * J + DENSE_FULL * GROUP == N
DENSE_SLOTS = 4
assert DENSE_FULL + 1 == DENSE_SLOTS * STEPS
EARLY = 4
EPS = 1e-5
HUGE = 1.0e30


def steps(eng, count, body, peeled=2):
    for step in range(peeled):
        body(step)
    with eng.Fori(peeled, count - 1) as step:
        body(step)
    body(count - 1)


def counter(eng, step):
    known = {}

    def through(n, back=0, short=0):
        if isinstance(step, int):
            return n * (step + 1 - back) - short
        if (n, back, short) not in known:
            known[n, back, short] = eng.to_reg(step * n + (n * (1 - back) - short))
        return known[n, back, short]
    return through


def wait(eng, sem, value):
    if not (isinstance(value, int) and value <= 0):
        eng.wait_ge(sem, value)


def wait_apart(eng, entered, *waits):
    eng.wait_ge(entered, 1)
    for sem, value in waits:
        wait(eng, sem, value)


def cols(step, slot, count=J, skip=0):
    return bass.ds(step * (J * SLOTS) + (J * slot + skip), count)


def over_rows(column_tile, width):
    return column_tile.unsqueeze(2).to_broadcast([column_tile.shape[0], column_tile.shape[1], width])


def group_before(sems, u, through, n=1):
    slots = len(sems)
    return sems[(u - 1) % slots], through(n, 1) if u == 0 else through(n)


def turns(eng, *parts, between=(None, None)):
    assert SLOTS == 2 and max(lag for _, lag in parts) <= 2

    def body(step):
        for u in range(SLOTS):
            for part, lag in parts:
                ago, slot = (lag - u + 1) // 2, (u - lag) % 2
                if not isinstance(step, int) or step >= ago:
                    part(step - ago, slot)
            if between[u]:
                between[u](eng, step)
    steps(eng, STEPS, body)
    for group in range(SLOTS * STEPS, SLOTS * STEPS + 2):
        for part, lag in parts:
            if group - lag < SLOTS * STEPS:
                part((group - lag) // 2, (group - lag) % 2)


class Phase:

    def __init__(self, nc, name):
        self.nc, self.name, self.stack, self.sems = nc, name, ExitStack(), []
        self.entered = self.sem("entered")

    def sb(self, name, shape, dt=F32):
        return self.stack.enter_context(self.nc.sbuf_tensor(f"{self.name}_{name}", shape, dt))

    def ps(self, name, shape=(P, 512)):
        return self.stack.enter_context(self.nc.psum_tensor(f"{self.name}_{name}", list(shape), F32))

    def sem(self, name):
        s = self.nc.alloc_semaphore(f"{self.name}_{name}")
        self.sems.append(s)
        return s

    def pair(self, make, name, *args):
        return [make(f"{name}{u}", *args) for u in range(SLOTS)]

    def part(self, name):
        part = Phase.__new__(Phase)
        part.nc, part.name, part.stack, part.sems, part.entered = self.nc, name, self.stack, self.sems, self.entered
        return part

    def close(self):
        self.stack.close()
        self.nc.clear_and_free_semaphores(self.sems)
        self.nc.all_engine_barrier()


def prepare(nc, a, k):
    ph = Phase(nc, "prep")
    dst_i = ph.sb("dst_i", [P, T], I32)
    prev_i, next_i = ph.sb("prev_i", [P, 1], I32), ph.sb("next_i", [P, 1], I32)
    blank = ph.sb("blank", [P, ATT])
    dst, attr = ph.sb("dst", [P, T]), ph.sb("attr", [P, T, 4])
    prev_tail, next_head = ph.sb("prev_tail", [P, 1]), ph.sb("next_head", [P, 1])
    is_end, valid, tmp = ph.sb("is_end", [P, T]), ph.sb("valid", [P, T]), ph.sb("tmp", [P, T])
    linked, head_ends, head_len = ph.sb("linked", [P, 1]), ph.sb("head_ends", [P, 1]), ph.sb("head_len", [P, 1])
    ones = ph.sb("ones", [P, T])
    row_base = ph.sb("row_base", [P, 1])
    wide = ph.sb("wide", [P, 2, P])
    head_of, tail_of = ph.sb("head_of", [P, P]), ph.sb("tail_of", [P, P])
    later, earlier = ph.sb("later", [P, P]), ph.sb("earlier", [P, P])
    head_out = ph.sb("head_out", [P, 1])
    w1b = ph.sb("w1b", [D + 1, 2, D])
    w0b = ph.sb("w0b", [D + 1, 2, D])
    w2 = ph.sb("w2", [D, 2, 2, D])
    b2 = ph.sb("b2", [1, 2, D])
    bias_at = ph.sb("bias_at", [1, D + 1])
    w_gat = ph.sb("w_gat", [D, 3, D])
    att = ph.sb("att", [D, 3, 2 * HEADS])
    turned = ph.sb("turned", [D, 7, D + 1])
    ps_a, ps_b, ps_c, ps_d = (ph.ps(f"ps{n}") for n in range(4))
    ps_w = [ph.ps("psw0"), ph.ps("psw1")]

    cleared, loaded, masks = ph.sem("cleared"), ph.sem("loaded"), ph.sem("masks")
    link, broad, spread, counted, carried = (ph.sem(n) for n in ("link", "broad", "spread", "counted", "carried"))
    root_in, root_out = ph.sem("root_in"), ph.sem("root_out")
    w_turn, w_copied, w_made, w_kept = (ph.sem(n) for n in ("w_turn", "w_copied", "w_made", "w_kept"))
    loads = [0]

    with nc.Block() as block:
        @block.sync
        def _(sp):
            def load(out, in_):
                with nc.allow_non_contiguous_dma(reason="a few columns of weights and indices"):
                    sp.dma_start(out, in_).then_inc(loaded, 16)
                loads[0] += 16

            sp.wait_ge(cleared, 1)
            load(k.l_acc[:, T, :], blank[:, 0:D])
            load(k.l_acc100[:, T, :], blank[:, :])
            load(k.l_msg[:, T, :], blank[:, :])
            d = a["dst"]
            load(dst_i[0:P - 1, :], d[0:(P - 1) * T].rearrange("(p t) -> p t", t=T))
            load(dst_i[P - 1:P, 0:LAST], d[(P - 1) * T:E].unsqueeze(0))
            load(k.src_idx[0:P - 1, 0:T], a["src"][0:(P - 1) * T].rearrange("(p t) -> p t", t=T))
            load(k.src_idx[P - 1:P, 0:LAST], a["src"][(P - 1) * T:E].unsqueeze(0))
            load(prev_i[1:P, :], d[0:(P - 1) * T].rearrange("(p t) -> p t", t=T)[:, T - 1:T])
            load(next_i[0:P - 2, :], d[T:(P - 1) * T].rearrange("(p t) -> p t", t=T)[:, 0:1])
            load(next_i[P - 2:P - 1, :], d[(P - 1) * T:(P - 1) * T + 1].unsqueeze(0))
            e = a["edge_attr_4"]
            load(attr[0:P - 1, :, :], e[0:(P - 1) * T, :].rearrange("(p t) c -> p t c", t=T))
            load(attr[P - 1:P, 0:LAST, :], e[(P - 1) * T:E, :].unsqueeze(0))
            for n, name in enumerate(("1", "2")):
                load(k.w_gcn[n][0:D, :], a[f"L0_gnn_W{name}"])
                load(k.w_gcn[n][D:D + 1, :], a[f"L0_gnn_b{name}"].unsqueeze(0))
            for i in range(2):
                load(w1b[0:D, i, :], a["L1_gnn_W1"][i])
                load(w1b[D:D + 1, i, :], a["L1_gnn_b1"][i:i + 1, :])
                load(w0b[0:D, i, :], a["L1_gnn_W0"][i])
                load(w0b[D:D + 1, i, :], a["L1_gnn_b0"][i:i + 1, :])
                load(w2[:, i, :, :], a["L1_gnn_W2"][i].rearrange("(s c) n -> c s n", c=D))
                load(b2[0:1, i, :], a["L1_gnn_b2"][i:i + 1, :])
            for i in range(3):
                load(w_gat[:, i, :], a["L2_gnn_W"][i])
                for s, name in enumerate(("L2_gnn_att_src", "L2_gnn_att_dst")):
                    for h in range(HEADS):
                        load(att[h * CH:(h + 1) * CH, i, HEADS * s + h:HEADS * s + h + 1],
                             a[name][i, h:h + 1, :].rearrange("a c -> c a"))
                load(k.gat_bias[:, i:i + 1], a["L2_gnn_bias"][i:i + 1, :].rearrange("a c -> c a"))
            load(k.gat_bias_row[:, :], a["L2_gnn_bias"][2:3, :].to_broadcast([P, D]))
            load(k.w_node[0:D, :], a["L3_gnn_W_node"])
            load(k.w_node[D:D + 1, :], a["L3_gnn_b_node"].unsqueeze(0))
            load(k.w_edge[0:4, :], a["L3_gnn_W_edge"])
            load(k.w_edge[4:5, :], a["L3_gnn_b_edge"].unsqueeze(0))
            load(k.w_msg[:, :, :], a["L3_gnn_W_msg"].rearrange("(s c) n -> c s n", c=D))
            for n, name in enumerate(("L3_gnn_g_node", "L3_gnn_beta_node", "L3_gnn_g_edge", "L3_gnn_beta_edge",
                                      "L3_gnn_g_msg", "L3_gnn_beta_msg")):
                load(k.l3_cols[:, n:n + 1], a[name].unsqueeze(1))
            load(k.msg_bias[0:1, :], a["L3_gnn_b_msg"].unsqueeze(0))

        @block.gpsimd
        def _(pool):
            pool.memset(dst_i[:, :], FAR)
            pool.memset(k.src_idx[:, :], 0)
            pool.memset(prev_i[:, :], -1)
            pool.memset(next_i[:, :], -2)
            pool.memset(att[:, :, :], 0.0)
            pool.memset(blank[:, :], 0.0)
            pool.memset(attr[:, :, :], 0.0)
            pool.memset(k.edge_in[:, :, 4:5], 1.0).then_inc(cleared, 1)
            pool.memset(ones[:, :], 1.0)
            pool.memset(k.cont[:, :], 0.0)
            pool.memset(k.cnt[:, :], 0.0)
            pool.memset(k.ident[:, :], 0.0)
            pool.memset(later[:, :], 1.0)
            pool.memset(earlier[:, :], 1.0)
            pool.memset(bias_at[:, 0:D], 0.0)
            pool.memset(bias_at[:, D:D + 1], 1.0)
            pool.memset(k.eps[:, :], EPS)
            pool.iota(row_base[:, :], pattern=[[0, 1]], base=-1, channel_multiplier=TH,
                      allow_small_or_imprecise_dtypes=True).then_inc(masks, 1)
            pool.wait_ge(masks, 1)
            pool.affine_select(out=k.ident[:, :], in_=k.ident[:, :], compare_op=ALU.not_equal, fill=1.0,
                               base=0, pattern=[[-1, P]], channel_multiplier=1)
            pool.affine_select(out=later[:, :], in_=later[:, :], compare_op=ALU.is_gt, fill=0.0,
                               base=0, pattern=[[1, P]], channel_multiplier=-1)
            pool.affine_select(out=earlier[:, :], in_=earlier[:, :], compare_op=ALU.is_gt, fill=0.0,
                               base=0, pattern=[[-1, P]], channel_multiplier=1).then_inc(masks, 1)

        @block.vector
        def _(dve):
            done = [0]

            def then(ins):
                done[0] += 1
                ins.then_inc(link, 1)
                dve.wait_ge(link, done[0])

            dve.wait_ge(loaded, loads[0])
            dve.wait_ge(masks, 2)
            then(dve.tensor_copy(dst[:, :], dst_i[:, :]))
            dve.tensor_copy(k.edge_in[:, 0:T, 0:4], attr[:, :, :])
            then(dve.tensor_copy(prev_tail[:, :], prev_i[:, :]))
            then(dve.tensor_copy(next_head[:, :], next_i[:, :]))
            head, tail = dst[:, 0:1], dst[:, T - 1:T]
            then(dve.tensor_tensor(k.cont[:, 1:T], dst[:, 1:T], dst[:, 0:T - 1], ALU.is_equal))
            then(dve.tensor_scalar(is_end[:, 0:T - 1], k.cont[:, 1:T], -1.0, 1.0, ALU.mult, ALU.add))
            then(dve.tensor_tensor(is_end[:, T - 1:T], tail, next_head[:, :], ALU.not_equal))
            then(dve.tensor_copy(k.tail_ended[:, :], is_end[:, T - 1:T]))
            then(dve.tensor_scalar(k.in_head[:, :], dst[:, :], head, None, ALU.is_equal))
            then(dve.tensor_tensor(linked[:, :], prev_tail[:, :], head, ALU.is_equal))
            then(dve.tensor_tensor(tmp[:, :], is_end[:, :], k.in_head[:, :], ALU.mult))
            then(dve.tensor_reduce(head_ends[:, :], tmp[:, :], AX.X, ALU.max))
            then(dve.tensor_tensor(head_out[:, :], head_ends[:, :], linked[:, :], ALU.mult))
            then(dve.tensor_scalar(tmp[:, :], k.in_head[:, :], linked[:, :], -1.0, ALU.mult, ALU.mult))
            then(dve.tensor_scalar(tmp[:, :], tmp[:, :], 1.0, None, ALU.add))
            then(dve.tensor_tensor(valid[:, :], is_end[:, :], tmp[:, :], ALU.mult))
            then(dve.scalar_tensor_tensor(out=tmp[:, :], in0=dst[:, :], scalar=float(-FAR), in1=valid[:, :],
                                          op0=ALU.add, op1=ALU.mult))
            then(dve.tensor_scalar(k.out_idx[:, 0:T], tmp[:, :], float(FAR), None, ALU.add))
            then(dve.scalar_tensor_tensor(out=tmp[:, 0:1], in0=head, scalar=float(-FAR), in1=head_out[:, :],
                                          op0=ALU.add, op1=ALU.mult))
            then(dve.tensor_scalar(k.out_idx[:, T:TH], tmp[:, 0:1], float(FAR), None, ALU.add))
            then(dve.tensor_scalar(k.own_idx[:, 0:T], dst[:, :], float(N - 1), None, ALU.min))
            then(dve.tensor_copy(k.own_idx[:, T:TH], head))
            then(dve.tensor_reduce(head_len[:, :], k.in_head[:, :], AX.X, ALU.add))
            then(dve.tensor_tensor(k.head_row[:, :], head_len[:, :], row_base[:, :], ALU.add))
            then(dve.tensor_tensor_scan(k.cnt[:, 0:T], k.cont[:, 0:T], ones[:, :], 0.0, ALU.mult, ALU.add))
            then(dve.tensor_copy(wide[:, 0, :], head.to_broadcast([P, P])))
            dve.tensor_copy(wide[:, 1, :], tail.to_broadcast([P, P])).then_inc(broad, 1)
            dve.wait_ge(spread, 1)
            then(dve.tensor_copy(head_of[:, :], ps_a[:, 0:P]))
            then(dve.tensor_copy(tail_of[:, :], ps_a[:, P:2 * P]))
            then(dve.tensor_scalar(k.carry_sel[:, :], head_of[:, :], tail, None, ALU.is_equal))
            dve.tensor_tensor(k.carry_sel[:, :], k.carry_sel[:, :], later[:, :], ALU.mult).then_inc(counted, 1)
            dve.wait_ge(counted, 1)
            then(dve.tensor_scalar(k.tail_sel[:, :], tail_of[:, :], head, head_out[:, :], ALU.is_equal, ALU.mult))
            then(dve.tensor_tensor(k.tail_sel[:, :], k.tail_sel[:, :], earlier[:, :], ALU.mult))
            for n, (of, mine) in enumerate(((tail_of, tail), (head_of, tail), (tail_of, head), (head_of, head))):
                then(dve.tensor_scalar(k.apart[:, n, :], of[:, :], mine, None, ALU.is_equal))
                then(dve.tensor_scalar(k.apart[:, n, :], k.apart[:, n, :], -1.0, HUGE, ALU.add, ALU.mult))
            then(dve.tensor_copy(k.seg_end[:, :], is_end[:, :]))
            then(dve.memset(k.seg_end[:, T - 1:T], 1.0))
            then(dve.tensor_scalar(k.not_end[:, :], k.seg_end[:, :], -1.0, 1.0, ALU.mult, ALU.add))
            then(dve.tensor_scalar(k.head_closed[:, :], k.in_head[:, :], head_out[:, :], None, ALU.mult))
            then(dve.tensor_scalar(k.not_head_closed[:, :], k.head_closed[:, :], -1.0, 1.0, ALU.mult, ALU.add))
            dve.wait_ge(carried, 1)
            then(dve.tensor_tensor(k.cnt[:, T:TH], ps_b[:, 0:1], head_len[:, :], ALU.add))
            dve.tensor_copy(k.dinv[:, :], k.cnt[:, :]).then_inc(root_in, 1)
            dve.wait_ge(root_out, 1)
            then(dve.reciprocal(k.dinv[:, :], k.dinv[:, :]))
            for n in range(7):
                dve.wait_ge(w_turn, n + 1)
                dve.tensor_copy(turned[:, n, :], ps_w[n % 2][0:D, 0:D + 1]).then_inc(w_copied, 1)
            outs = [k.w_self[0], k.w_agg[0], k.w_self[1], k.w_agg[1]]
            for n in range(4):
                dve.wait_ge(w_made, n + 1)
                dve.tensor_copy(outs[n][:, :], (ps_c, ps_d)[n % 2][0:D + 1, 0:D]).then_inc(w_kept, 1)
            for n in range(3):
                dve.wait_ge(w_made, 5 + n)
                then(dve.tensor_copy(k.w_att[n][:, 0:D], w_gat[:, n, :]))
                dve.tensor_copy(k.w_att[n][:, D:ATT_ALL], (ps_c, ps_d)[n % 2][0:D, 0:2 * HEADS]).then_inc(w_kept, 1)
            dve.wait_ge(w_kept, 7)
            for n in range(2):
                dve.tensor_scalar(turned[:, n, 0:1], k.gat_bias[:, n:n + 1], 0.0, None, ALU.max)
            then(dve.tensor_scalar(k.gat_rest_row[:, :], k.gat_bias_row[:, :], 0.0, None, ALU.max))
            for n in range(2):
                dve.tensor_copy(k.wide_bias[:, n, :], turned[:, n, 0:1].to_broadcast([D, P])).then_inc(broad, 1)
            dve.wait_ge(spread, 3)
            for n in range(2):
                for j in range(J):
                    then(dve.tensor_copy(k.att_rest[n][:, j, :], ps_w[n][:, 0:ATT]))

        @block.scalar
        def _(act):
            act.dma_start(k.t_x[:, :].rearrange("(p n) c -> p (n c)", p=80),
                          a["x"].rearrange("(p n) c -> p (n c)", p=80)).then_inc(k.base_copied, 16)
            act.wait_ge(root_in, 1)
            act.activation(k.dinv[:, :], k.dinv[:, :], ACT.Sqrt, bias=1.0).then_inc(root_out, 1)

        @block.tensor
        def _(pe):
            pe.wait_ge(loaded, loads[0])
            pe.wait_ge(masks, 2)
            ident = k.ident
            pe.wait_ge(broad, 1)
            pe.transpose(ps_a[:, 0:P], wide[:, 0, :], ident[:, :])
            pe.transpose(ps_a[:, P:2 * P], wide[:, 1, :], ident[:, :]).then_inc(spread, 1)
            pe.wait_ge(counted, 1)
            pe.matmul(ps_b[:, 0:1], k.carry_sel[:, :], k.cnt[:, T - 1:T], start=True, stop=True).then_inc(carried, 1)
            takes = [w1b[:, 0, :], w0b[:, 0, :], w1b[:, 1, :], w0b[:, 1, :]] + [w_gat[:, i, :] for i in range(3)]
            for n, w in enumerate(takes):
                if n >= 2:
                    pe.wait_ge(w_copied, n - 1)
                rows = w.shape[0]
                pe.transpose(ps_w[n % 2][0:D, 0:rows], w, ident[0:rows, 0:rows]).then_inc(w_turn, 1)
            for n in range(7):
                ps = (ps_c, ps_d)[n % 2]
                pe.wait_ge(w_copied, min(n + 1, 7))
                if n >= 2:
                    pe.wait_ge(w_kept, n - 1)
                if n < 4:
                    i, part = n // 2, n % 2
                    ins = pe.matmul(ps[0:D + 1, 0:D], turned[:, n, :], w2[:, i, part, :], start=True, stop=part == 1)
                    if part == 0:
                        ins = pe.matmul(ps[0:D + 1, 0:D], bias_at[:, :], b2[0:1, i, :], start=False, stop=True)
                else:
                    ins = pe.matmul(ps[0:D, 0:2 * HEADS], turned[:, n, 0:D], att[:, n - 4, :], start=True, stop=True)
                ins.then_inc(w_made, 1)
            pe.wait_ge(broad, 3)
            for n in range(2):
                pe.matmul(ps_w[n][:, 0:ATT], k.wide_bias[:, n, :], k.w_att[n + 1][:, 0:ATT],
                          start=True, stop=True).then_inc(spread, 1)
    ph.close()


class Norm:

    def __init__(self, ph, name, slots=SLOTS, uses=1):
        self.uses = uses
        self.entered = ph.entered
        self.stat = [ph.sb(f"{name}_stat{u}", [P, J, 6]) for u in range(slots)]
        self.mv = [ph.sb(f"{name}_mv{u}", [P, J, 2]) for u in range(slots)]
        self.root = [ph.sb(f"{name}_root{u}", [P, J]) for u in range(slots)]
        self.stats_in = [ph.sem(f"{name}_stats{u}") for u in range(slots)]
        self.var_in = [ph.sem(f"{name}_var{u}") for u in range(slots)]
        self.rooted = [ph.sem(f"{name}_rooted{u}") for u in range(slots)]
        self.inverted = [ph.sem(f"{name}_inverted{u}") for u in range(slots)]

    def count(self, through, nth):
        return through(self.uses, 0, self.uses - 1 - nth)

    def spread(self, dve, u, rows, through, parts=P, nth=0):
        for j in range(J):
            ins = dve.bn_stats(self.stat[u][0:parts, j, :], rows[:, j, :])
        ins.then_inc(self.stats_in[u], 1)
        wait_apart(dve, self.entered, (self.stats_in[u], self.count(through, nth)))
        for j in range(J):
            ins = dve.bn_aggr(self.mv[u][0:parts, j, :], self.stat[u][0:parts, j, :])
        ins.then_inc(self.var_in[u], 1)

    def take_root(self, act, u, through, scale, bias, parts=P, nth=0):
        act.wait_ge(self.var_in[u], self.count(through, nth))
        act.activation(self.root[u][0:parts, :], self.mv[u][0:parts, :, 1], ACT.Sqrt, scale=scale,
                       bias=bias).then_inc(self.rooted[u], 1)

    def invert(self, dve, u, through, parts=P, nth=0):
        dve.wait_ge(self.rooted[u], self.count(through, nth))
        dve.reciprocal(self.root[u][0:parts, :], self.root[u][0:parts, :]).then_inc(self.inverted[u], 1)
        dve.wait_ge(self.inverted[u], self.count(through, nth))

    def mean(self, u, parts=P):
        return self.mv[u][0:parts, :, 0:1].to_broadcast([parts, J, D])

    def inverse(self, u, parts=P):
        return over_rows(self.root[u][0:parts, :], D)


def four(make, name, *args):
    return [make(f"{name}{u}", *args) for u in range(DENSE_SLOTS)]


def every_place(row, parts):
    return row[0:parts, :].unsqueeze(1).to_broadcast([parts, J, D])


def bank_free(pe, copied, u, through):
    if u >= 2:
        pe.wait_ge(copied[u - 2], through(1))
    else:
        wait(pe, copied[u + 2], through(1, 1))


def dense_parts(step, u):
    return REST if is_last(step) and u == DENSE_SLOTS - 1 else P


def dense_rows(table, step, u, parts=P):
    if parts != P:
        return table[DENSE_FULL * GROUP:N, :].rearrange("(p j) c -> p j c", j=J)
    groups = table[0:DENSE_FULL * GROUP, :].rearrange("(g p j) c -> p g j c", p=P, j=J)
    return groups[:, bass.ds(step * DENSE_SLOTS + u, 1), :, :].rearrange("p g j c -> p (g j) c")


def load_ahead(sp, step, load):
    for u in range(DENSE_SLOTS) if isinstance(step, int) and step == 0 else (DENSE_SLOTS - 1,):
        load(step, u, dense_parts(step, u))


class DenseChain:

    STAGES, HALF = 6, 3
    PAIRS = (0, 1), (2, 3)
    LAYERS = 5
    LAYER_OF = {0: 0, 1: 1, 2: 2, 3: 3, 5: 4}
    BANKS_BEFORE = (-2, -1, None, 0, 2), (4, None, 5, 6, 8)

    def __init__(self, ph, a, k):
        self.a, self.k = a, k

        self.x, self.h1, self.x1, self.y1, self.x2, self.x3, self.z, self.c = (
            four(ph.sb, n, [P, J, D]) for n in ("x", "h1", "x1", "y1", "x2", "x3", "z", "c"))
        self.att, self.xt = four(ph.sb, "att", [P, J, ATT]), four(ph.sb, "xt", [D + 1, GROUP])
        self.ps_t = [ph.ps(f"ps_t{n}") for n in range(2)]
        self.ps_y = four(ph.ps, "ps_y")
        self.norm = Norm(ph, "norm", DENSE_SLOTS, uses=5)
        self.loaded, self.stored, self.turned, self.copied, self.made = (
            four(ph.sem, n) for n in ("loaded", "stored", "turned", "copied", "made"))
        self.ready = {n: four(ph.sem, f"{n}_ready") for n in ("h1", "x1", "y1", "x2", "x3", "att")}
        self.z0_in, self.z3_in, self.z4_in, self.scaled, self.centred = (
            four(ph.sem, n) for n in ("z0_in", "z3_in", "z4_in", "scaled", "centred"))
        self.ones_set, self.const_stored = ph.sem("ones_set"), ph.sem("const_stored")

    def run_step(self, eng, step, stage, beside=None):
        for m in range(self.STAGES):
            stage(eng, step, 0, m)
            if m >= self.HALF:
                stage(eng, step, 1, m - self.HALF)
            elif not (isinstance(step, int) and step == 0):
                stage(eng, step - 1, 1, m + self.HALF)
            if beside:
                beside(m)

    def run_rest(self, eng, stage):
        for m in range(self.HALF, self.STAGES):
            stage(eng, STEPS - 1, 1, m)

    def groups(self, step, pair):
        return [(u, dense_parts(step, u)) for u in self.PAIRS[pair]]

    def layer(self, through, m):
        return through(self.LAYERS, 0, self.LAYERS - 1 - m)

    def load(self, sp, step, u, n=P):
        at = u % DENSE_SLOTS
        if u == DENSE_SLOTS - 1:
            wait(sp, self.z0_in[u], counter(sp, step)(1, 1))
        sp.dma_start(self.x[at][0:n], dense_rows(self.a["x"], step, u, n)).then_inc(self.loaded[at], 16)

    def sync_stage(self, sp, step, pair, m):
        k, through = self.k, counter(sp, step)
        if pair == 0 and m == 0:
            load_ahead(sp, step, lambda step, u, n: self.load(sp, step, u, n))
        stores = {0: [("h1", k.t_h1, self.h1)], 1: [("x1", k.t_x1, self.x1)], 2: [("y1", k.t_y1, self.y1)],
                  5: [("att", k.t_att[0], self.att), ("x3", k.t_x3, self.x3)]}
        for name, table, tile in stores.get(m, []):
            for u, n in self.groups(step, pair):
                sp.wait_ge(self.ready[name][u], through(1))
                sp.dma_start(dense_rows(table, step, u, n), tile[u][0:n]).then_inc(self.stored[u], 16)
        if pair == 0 and m == 3:
            self.store_constant_rows(sp, step)
        if m == 1 and not is_last(step):
            for u in self.PAIRS[pair]:
                if u < DENSE_SLOTS - 1:
                    sp.wait_ge(self.z0_in[u], through(1))
                    self.load(sp, step, u + DENSE_SLOTS)

    def sync_end(self, sp):
        for u in range(DENSE_SLOTS):
            sp.wait_ge(self.stored[u], 16 * 5 * STEPS)
        sp.wait_ge(self.const_stored, 16 * 2 * (STEPS + 1))

    def store_constant_rows(self, sp, step):
        full = DENSE_SLOTS - 1 if is_last(step) else DENSE_SLOTS
        for n, rows in enumerate(self.k.att_rest):
            table = self.k.t_att[n + 1]
            groups = table[0:DENSE_FULL * GROUP, :].rearrange("(g p j) c -> p g (j c)", p=P, j=J)
            sp.dma_start(groups[:, bass.ds(step * DENSE_SLOTS, full), :],
                         rows_of(rows[:, :, :]).unsqueeze(1).to_broadcast([P, full, J * ATT]))\
              .then_inc(self.const_stored, 16)
            if is_last(step):
                sp.dma_start(dense_rows(table, step, DENSE_SLOTS - 1, REST), rows[0:REST])\
                  .then_inc(self.const_stored, 16)

    def scalar_stage(self, act, step, pair, m):
        k, through = self.k, counter(act, step)
        groups = self.groups(step, pair)
        if m in self.LAYER_OF:
            for u, n in groups:
                act.wait_ge(self.turned[u], self.layer(through, self.LAYER_OF[m]))
                ps, xt = self.ps_t[u % 2], self.xt[u]
                if n == P:
                    act.activation(xt[0:D, :], ps[0:D, :], ACT.Copy).then_inc(self.copied[u], 1)
                else:
                    for j in range(J):
                        ins = act.activation(xt[0:D, j * P:j * P + n], ps[0:D, j * P:j * P + n], ACT.Copy)
                    ins.then_inc(self.copied[u], 1)
        if m == 0:
            for u, n in groups:
                act.wait_ge(self.made[u], self.layer(through, 0))
                wait(act, self.stored[u], through(80, 1))
                act.activation(rows_of(self.h1[u][0:n]), self.ps_y[u][0:n, 0:J * D],
                               ACT.Relu).then_inc(self.ready["h1"][u], 1)
        if m == 5:
            for u, n in groups:
                act.wait_ge(self.made[u], self.layer(through, 4))
                act.activation(rows_of(self.att[u][0:n]), self.ps_y[u][0:n, 0:J * ATT],
                               ACT.Copy).then_inc(self.ready["att"][u], 1)
        if m > 0:
            layer_norm = m in (1, 4, 5)
            for u, n in groups:
                self.norm.take_root(act, u, through, 1.0 if layer_norm else D / (D - 1),
                                    k.eps[0:n, :] if layer_norm else 0.0, n, m - 1)

    def tensor_stage(self, pe, step, pair, m):
        if m not in self.LAYER_OF:
            return
        k, through, layer = self.k, counter(pe, step), self.LAYER_OF[m]
        weights = [k.w_gcn[0], k.w_gcn[1], k.w_self[0], k.w_self[1], k.w_att[0]][layer]
        source, is_ready = [(self.x, self.loaded), (self.h1, self.ready["h1"]), (self.x1, self.ready["x1"]),
                            (self.y1, self.ready["y1"]), (self.x2, self.ready["x2"])][layer]
        before = self.BANKS_BEFORE[pair][layer]
        if pair == 1 and is_last(step) and m >= self.HALF:
            before = None
        for u, n in self.groups(step, pair):
            pe.wait_ge(is_ready[u], through(16 if layer == 0 else 1))
            if before is not None:
                wait(pe, self.copied[(u + 2) % DENSE_SLOTS], through(self.LAYERS, 0, self.LAYERS - before))
            for j in range(J):
                ins = pe.transpose(self.ps_t[u % 2][0:D, j * P:j * P + n], source[u][0:n, j, :], k.ident[0:n, 0:n])
            ins.then_inc(self.turned[u], 1)
        rows, width = (D, ATT) if layer == 4 else (D + 1, D)
        for u, n in self.groups(step, pair):
            pe.wait_ge(self.copied[u], self.layer(through, layer))
            if layer == 0:
                wait(pe, self.ready["att"][u], through(1, 1))
            for j in range(J):
                ins = pe.matmul(self.ps_y[u][0:n, j * width:(j + 1) * width], self.xt[u][0:rows, j * P:j * P + n],
                                weights[0:rows, 0:width], start=True, stop=True)
            ins.then_inc(self.made[u], 1)

    def vector_begin(self, dve):
        for u in range(DENSE_SLOTS):
            ins = dve.memset(self.xt[u][D:D + 1, :], 1.0)
        ins.then_inc(self.ones_set, 1)

    def vector_stage(self, dve, step, pair, m):
        if m == 0:
            return
        through, norm = counter(dve, step), self.norm
        groups = self.groups(step, pair)

        def made_rows(u, n):
            return self.ps_y[u][0:n, 0:J * D].rearrange("p (j c) -> p j c", c=D)

        if m == 1:
            for u, n in groups:
                dve.wait_ge(self.made[u], self.layer(through, 1))
                wait(dve, self.stored[u], through(80, 1))
                wait(dve, self.centred[u], through(3, 1))
                dve.scalar_tensor_tensor(out=self.z[u][0:n], in0=made_rows(u, n), scalar=0.0, in1=self.x[u][0:n],
                                         op0=ALU.max, op1=ALU.add).then_inc(self.z0_in[u], 1)
        if m in (2, 3):
            for u, n in groups:
                dve.wait_ge(self.made[u], self.layer(through, m))
                norm.spread(dve, u, made_rows(u, n), through, n, m - 1)
            for u, n in groups:
                norm.invert(dve, u, through, n, m - 1)
                out, is_in = (self.y1, self.ready["y1"]) if m == 2 else (self.c, self.scaled)
                dve.tensor_tensor(out[u][0:n], made_rows(u, n), norm.inverse(u, n), ALU.mult).then_inc(is_in[u], 1)
            return
        z_in, centred, out, name = {1: (self.z0_in, 0, self.x1, "x1"), 4: (self.z3_in, 1, self.x2, "x2"),
                                    5: (self.z4_in, 2, self.x3, "x3")}[m]
        for u, n in groups:
            dve.wait_ge(z_in[u], through(1))
            norm.spread(dve, u, self.z[u][0:n], through, n, m - 1)
        for u, n in groups:
            dve.wait_ge(norm.var_in[u], norm.count(through, m - 1))
            dve.tensor_tensor(self.c[u][0:n], self.z[u][0:n], norm.mean(u, n), ALU.subtract)\
                .then_inc(self.centred[u], 1)
        for u, n in groups:
            norm.invert(dve, u, through, n, m - 1)
            dve.wait_ge(self.centred[u], through(3, 0, 2 - centred))
            dve.tensor_tensor(out[u][0:n], self.c[u][0:n], norm.inverse(u, n), ALU.mult)\
                .then_inc(self.ready[name][u], 1)

    def gpsimd_stage(self, pool, step, pair, m):
        through = counter(pool, step)
        groups = self.groups(step, pair)
        if m == 3:
            for u, n in groups:
                pool.wait_ge(self.scaled[u], through(1))
                pool.tensor_tensor(self.z[u][0:n], self.c[u][0:n], self.x1[u][0:n], ALU.add)\
                    .then_inc(self.z3_in[u], 1)
        if m == 4:
            for u, n in groups:
                pool.wait_ge(self.ready["x2"][u], through(1))
                pool.tensor_tensor(self.z[u][0:n], self.x2[u][0:n],
                                   self.k.gat_rest_row[0:n, :].unsqueeze(1).to_broadcast([n, J, D]),
                                   ALU.add).then_inc(self.z4_in[u], 1)


def rows_of(tile):
    return tile.rearrange("p j c -> p (j c)")


def by_head(rows):
    return rows[:, :, 0:D].rearrange("p j (h c) -> p j h c", h=HEADS)


def per_head(weights):
    return weights.unsqueeze(3).to_broadcast([P, J, HEADS, CH])


class Rows:

    def __init__(self, ph, gather=None, gather_idx=None, scatter=None, scatter_idx=None, width=D, head_too=False):
        self.ph, self.table, self.idx, self.out, self.out_idx = ph, gather, gather_idx, scatter, scatter_idx
        self.head_too = head_too
        if gather is not None:
            self.rows = ph.pair(ph.sb, "gathered", [P, J, width])
            self.window = ph.pair(ph.sb, "take_window", [P, J], I32)
            self.window_in, self.here = ph.pair(ph.sem, "take_window_in"), ph.pair(ph.sem, "gathered_in")
        if scatter is not None:
            self.out_window = ph.pair(ph.sb, "put_window", [P, J], I32)
            self.out_window_in, self.gone = ph.pair(ph.sem, "put_window_in"), ph.pair(ph.sem, "scattered")

    def count(self, step, u):
        return J - 1 if not self.head_too and is_last(step) and u == SLOTS - 1 else J

    def all_here(self, step, u, through):
        return through(16 * J) - 16 * (J - self.count(step, u)) if is_last(step) else through(16 * J)

    def gather(self, pool, step, u, through, *free):
        wait_apart(pool, self.ph.entered, (self.window_in[u], through(1)), *free)
        for j in range(self.count(step, u)):
            pool.indirect_dma_start(
                out=self.rows[u][:, j, :], out_offset=None, in_=self.table,
                in_offset=bass.IndirectOffsetOnAxis(ap=self.window[u][:, j:j + 1], axis=0)).then_inc(self.here[u], 16)

    def scatter(self, pool, tile, u, through, ready, bound, left_out=0):
        wait_apart(pool, self.ph.entered, (self.out_window_in[u], through(1, left_out)), (ready, through(1)))
        for j in range(J):
            pool.indirect_dma_start(
                out=self.out, out_offset=bass.IndirectOffsetOnAxis(ap=self.out_window[u][:, j:j + 1], axis=0),
                in_=tile[:, j, :], in_offset=None, bounds_check=bound, oob_is_err=False).then_inc(self.gone[u], 16)

    def first_windows(self, act):
        for u in range(SLOTS):
            act.activation(self.window[u][:, :], self.idx[:, cols(0, u)], ACT.Copy).then_inc(self.window_in[u], 1)

    def next_window(self, act, step, u, through):
        if not is_last(step):
            wait_apart(act, self.ph.entered, (self.here[u], self.all_here(step, u, through)))
            act.activation(self.window[u][:, :], self.idx[:, cols(step, u, skip=J * SLOTS)],
                           ACT.Copy).then_inc(self.window_in[u], 1)

    def put_window(self, act, step, u, through, left_out=0):
        wait_apart(act, self.ph.entered, (self.gone[u], through(16 * J, 1 + left_out)))
        act.activation(self.out_window[u][:, :], self.out_idx[:, cols(step, u)],
                       ACT.Copy).then_inc(self.out_window_in[u], 1)


def is_last(step):
    return isinstance(step, int) and step == STEPS - 1


class EdgeFeatures:

    def __init__(self, ph, k, slots):
        self.k, self.slots = k, slots
        self.attr_t = [ph.sb(f"attr_t{u}", [5, GROUP]) for u in range(slots)]
        self.ps_attr = self.ps_feat = [ph.ps(f"ps_feat{u}") for u in range(slots)]
        self.turned, self.copied, self.made, self.kept, self.here = (
            [ph.sem(f"{n}{u}") for u in range(SLOTS)]
            for n in ("attr_turned", "attr_copied", "feat_made", "feat_kept", "attr_here"))
        self.window = ph.pair(ph.sb, "attr_window", [P, J, 5])
        self.entered = ph.entered

    def take(self, act, step, u, through):
        n = edge_places(step, u)
        wait_apart(act, self.entered, (self.turned[u], through(1, 1)))
        act.activation(self.window[u][:, 0:n, :], self.k.edge_in[:, cols(step, u, n), :],
                       ACT.Copy).then_inc(self.here[u], 1)

    def turn(self, pe, step, u, through):
        pe.wait_ge(self.here[u], through(1))
        ps = self.ps_attr[u % self.slots]
        for j in range(edge_places(step, u)):
            ins = pe.transpose(ps[0:5, j * P:(j + 1) * P], self.window[u][:, j, :], self.k.ident[:, :])
        ins.then_inc(self.turned[u], 1)


def edge_places(step, u):
    return J - 1 if is_last(step) and u == SLOTS - 1 else J


def column_stats(dve, ph, stat, lone, values, step, u):
    n = edge_places(step, u)
    v = values[:, 0:n * P].rearrange("c (j p) -> c j p", p=P)
    dve.bn_stats(stat[:, bass.ds(step * SLOTS + u, 1), :].rearrange("c a s -> c (a s)"), v[:, :, 0:P - 1])
    return dve.tensor_copy(lone[:, cols(step, u, n)], v[:, :, P - 1])


def column_scale(dve, act, gamma, beta, mv, root, scale, shift, sems, k, act_side):
    var_in, rooted, link = sems
    if act_side:
        act.wait_ge(var_in, 1)
        act.activation(root, mv[:, 1:2], ACT.Sqrt, bias=k.eps[0:D, :]).then_inc(rooted, 1)
        return
    dve.wait_ge(rooted, 1)
    dve.reciprocal(root, root).then_inc(link, 1)
    dve.wait_ge(link, 1)
    dve.tensor_tensor(scale, gamma, root, ALU.mult).then_inc(link, 1)
    dve.wait_ge(link, 2)
    dve.tensor_tensor(root, mv[:, 0:1], scale, ALU.mult).then_inc(link, 1)
    dve.wait_ge(link, 3)
    dve.tensor_tensor(shift, beta, root, ALU.subtract).then_inc(link, 1)
    dve.wait_ge(link, 4)


def own_rows(nc, a, k):
    ph = Phase(nc, "own")
    take = Rows(ph, a["x"], k.own_idx, k.t_x, k.out_idx, head_too=True)
    x = take.rows
    scaled = ph.pair(ph.sb, "scaled", [P, J, D])
    scaled_in, x_stored, scaled_stored = (ph.pair(ph.sem, n) for n in ("scaled_in", "x_stored", "scaled_stored"))
    ef = EdgeFeatures(ph, k, 1)
    feat = ph.pair(ph.sb, "feat", [D, GROUP])
    feat_read = ph.pair(ph.sem, "feat_read")
    stat, lone = ph.sb("stat", [D, 2 * STEPS + 1, 6]), ph.sb("lone", [D, TH])
    mv, root = ph.sb("mv", [D, 2]), ph.sb("root", [D, 1])
    ps_w = ph.ps("ps_w")
    stat_in, var_in, rooted, link, folded, bias_in = (
        ph.sem(n) for n in ("stat_in", "var_in", "rooted", "link", "folded", "bias_in"))

    ph.sems.append(k.base_copied)
    early_rows = ph.sb("early_rows", [P, EARLY * J * SLOTS, D])
    early_in, early_gone = ph.sem("early_in"), ph.sem("early_gone")
    dense = DenseChain(ph.part("dense"), a, k)

    with nc.Block() as block:
        @block.sync
        def _(sp):
            sp.sem_inc(ph.entered, 1)

            def keep_rows(step, u):
                through = counter(sp, step)
                sp.wait_ge(take.here[u], take.all_here(step, u, through))
                sp.dma_start(k.l_x[:, cols(step, u), :], x[u][:, :, :]).then_inc(x_stored[u], 16)
                sp.wait_ge(scaled_in[u], through(1))
                sp.dma_start(k.l_s[:, cols(step, u), :], scaled[u][:, :, :]).then_inc(scaled_stored[u], 16)

            def body(step):
                first = isinstance(step, int) and step == 0

                def beside(m):
                    if m == 4:
                        keep_rows(step, 0)
                    if m == 1 and not first:
                        keep_rows(step - 1, 1)
                dense.run_step(sp, step, dense.sync_stage, beside)
            steps(sp, STEPS, body, EARLY + 1)
            keep_rows(STEPS - 1, 1)
            dense.run_rest(sp, dense.sync_stage)
            dense.sync_end(sp)
            for u in range(SLOTS):
                sp.wait_ge(x_stored[u], 16 * STEPS)
                sp.wait_ge(scaled_stored[u], 16 * STEPS)
            sp.dma_start(early_rows[:, :, :], k.l_s[:, 0:EARLY * J * SLOTS, :]).then_inc(early_in, 16)

        @block.gpsimd
        def _(pool):
            bound = pool.to_reg(N - 1)

            def body(step):
                through = counter(pool, step)
                before = None if isinstance(step, int) and step <= EARLY else counter(pool, step - 1)
                if isinstance(step, int) and step == EARLY:
                    pool.wait_ge(k.base_copied, 16)

                def rows_part(m):
                    if m in (1, 4):
                        u = m // 4
                        take.gather(pool, step, u, through, (x_stored[u], through(16, 1)),
                                    (scaled_in[u], through(1, 1)))
                        if before is not None:
                            take.scatter(pool, scaled[u], u, before, scaled_in[u], bound, EARLY)
                dense.run_step(pool, step, dense.gpsimd_stage, rows_part)
            steps(pool, STEPS, body, EARLY + 1)
            dense.run_rest(pool, dense.gpsimd_stage)
            for u in range(SLOTS):
                take.scatter(pool, scaled[u], u, counter(pool, STEPS - 1), scaled_in[u], bound, EARLY)
            pool.wait_ge(early_in, 16)
            for t in range(EARLY * J * SLOTS):
                pool.indirect_dma_start(
                    out=k.t_x, out_offset=bass.IndirectOffsetOnAxis(ap=k.out_idx[:, t:t + 1], axis=0),
                    in_=early_rows[:, t, :], in_offset=None, bounds_check=bound, oob_is_err=False)\
                    .then_inc(early_gone, 16)
            pool.wait_ge(early_gone, 16 * EARLY * J * SLOTS)
            for u in range(SLOTS):
                pool.wait_ge(take.gone[u], 16 * J * (STEPS - EARLY))

        @block.scalar
        def _(act):
            take.first_windows(act)

            def take_attributes(step, u):
                ef.take(act, step, u, counter(act, step))

            def copy_attributes(step, u):
                n = edge_places(step, u) * P
                act.wait_ge(ef.turned[u], counter(act, step)(1))
                act.activation(ef.attr_t[0][:, 0:n], ef.ps_attr[0][0:5, 0:n], ACT.Copy).then_inc(ef.copied[u], 1)

            def keep_features(step, u):
                through = counter(act, step)
                n = edge_places(step, u) * P
                act.wait_ge(ef.made[u], through(1))
                wait(act, feat_read[u], through(1, 1))
                act.activation(feat[u][:, 0:n], ef.ps_feat[0][0:D, 0:n], ACT.Relu).then_inc(ef.kept[u], 1)

            def windows(step, u):
                through = counter(act, step)
                take.next_window(act, step, u, through)
                if not (isinstance(step, int) and step < EARLY):
                    take.put_window(act, step, u, through, EARLY)

            plan = {0: [(take_attributes, 0, 0), (windows, 1, 1)], 1: [(copy_attributes, 0, 0)],
                    2: [(take_attributes, 1, 0)], 3: [(keep_features, 0, 0)],
                    4: [(copy_attributes, 1, 0), (windows, 0, 0)], 5: [(keep_features, 1, 0)]}

            def body(step):
                first = isinstance(step, int) and step == 0

                def beside(m):
                    for part, u, ago in plan[m]:
                        if not (ago and first):
                            part(step - ago, u)
                dense.run_step(act, step, dense.scalar_stage, beside)
            steps(act, STEPS, body, EARLY + 1)
            windows(STEPS - 1, 1)
            dense.run_rest(act, dense.scalar_stage)
            column_scale(None, act, None, None, mv, root[:, :], None, None, (var_in, rooted, link), k, True)

        @block.tensor
        def _(pe):
            pe.wait_ge(dense.ones_set, 1)

            def body(step):
                through = counter(pe, step)

                def turn(u):
                    wait(pe, *group_before(ef.kept, u, through))
                    ef.turn(pe, step, u, through)

                def product(u):
                    n = edge_places(step, u) * P
                    pe.wait_ge(ef.copied[u], through(1))
                    pe.matmul(ef.ps_feat[0][0:D, 0:n], k.w_edge[:, :], ef.attr_t[0][:, 0:n],
                              start=True, stop=True).then_inc(ef.made[u], 1)

                plan = {0: (turn, 0), 2: (product, 0), 3: (turn, 1), 5: (product, 1)}

                def beside(m):
                    if m in plan:
                        part, u = plan[m]
                        part(u)
                dense.run_step(pe, step, dense.tensor_stage, beside)
            steps(pe, STEPS, body, EARLY + 1)
            dense.run_rest(pe, dense.tensor_stage)
            pe.wait_ge(folded, 1)
            pe.matmul(ps_w[0:1, 0:D], k.l3_cols[:, 7:8], k.w_msg[:, 2, :], start=True, stop=True).then_inc(bias_in, 1)

        @block.vector
        def _(dve):
            dense.vector_begin(dve)

            def scale_rows(step, u):
                through = counter(dve, step)
                dve.wait_ge(take.here[u], take.all_here(step, u, through))
                if not (isinstance(step, int) and step <= EARLY):
                    wait(dve, take.gone[u], through(16 * J, 1 + EARLY))
                wait(dve, scaled_stored[u], through(16, 1))
                dve.tensor_tensor(scaled[u][:, :, :], x[u][:, :, :], over_rows(k.dinv[:, cols(step, u)], D),
                                  ALU.mult).then_inc(scaled_in[u], 1)

            def statistics(step, u):
                wait_apart(dve, ph.entered, (ef.kept[u], counter(dve, step)(1)))
                column_stats(dve, ph, stat, lone, feat[u], step, u).then_inc(feat_read[u], 1)

            plan = {0: (scale_rows, 1, 1), 3: (statistics, 0, 0), 4: (scale_rows, 0, 0), 5: (statistics, 1, 0)}

            def body(step):
                first = isinstance(step, int) and step == 0

                def beside(m):
                    part, u, ago = plan.get(m, (None, 0, 0))
                    if part and not (ago and first):
                        part(step - ago, u)
                dense.run_step(dve, step, dense.vector_stage, beside)
            steps(dve, STEPS, body, EARLY + 1)
            scale_rows(STEPS - 1, 1)
            dense.run_rest(dve, dense.vector_stage)
            dve.wait_ge(feat_read[0], STEPS)
            dve.wait_ge(feat_read[1], STEPS)
            dve.bn_stats(stat[:, 2 * STEPS, :], lone[:, 0:LAST]).then_inc(stat_in, 1)
            dve.wait_ge(stat_in, 1)
            dve.bn_aggr(mv[:, :], stat[:, :, :].rearrange("c a s -> c (a s)")).then_inc(var_in, 1)
            column_scale(dve, None, k.l3_cols[:, 2:3], k.l3_cols[:, 3:4], mv, root[:, :], k.edge_scale[:, :],
                         k.l3_cols[:, 7:8], (var_in, rooted, link), k, False)
            dve.tensor_scalar(k.w_feat[0:D, :], k.w_msg[:, 2, :], k.edge_scale[:, :], None, ALU.mult).then_inc(folded, 1)
            dve.wait_ge(bias_in, 1)
            dve.tensor_tensor(k.msg_bias[:, :], ps_w[0:1, 0:D], k.msg_bias[:, :], ALU.add)
    ph.close()


GCN1, GCN2, SAGE1, SAGE2, GAT1, GAT2, GAT3 = "gcn1", "gcn2", "sage1", "sage2", "gat1", "gat2", "gat3"


def node_round(nc, a, k, kind, table=None, out=None, own=None, rest=None, keep=None, layer=0):
    assert SLOTS == 2
    gat, sage, gcn = kind in (GAT1, GAT2, GAT3), kind in (SAGE1, SAGE2), kind in (GCN1, GCN2)
    C = ATT if gat else D
    A_WIDTH = D + 1 if sage else C
    OUT = ATT if kind in (SAGE2, GAT1, GAT2) else D
    normed = kind in (GCN2, SAGE2, GAT3)
    over_std = sage
    multiplied = kind != GAT3
    ph = Phase(nc, kind)
    put = Rows(ph, table, k.src_idx, out, k.out_idx)
    acc = ph.pair(ph.sb, "acc", [P, J, A_WIDTH])
    cont = ph.pair(ph.sb, "cont", [P, J])
    new = ph.pair(ph.sb, "new", [P, J, OUT])
    head_part = ph.sb("head_part", [P, C])
    xt = ph.pair(ph.sb, "xt", [D + 1, GROUP])
    ps_x, ps_y = ph.pair(ph.ps, "ps_x"), ph.pair(ph.ps, "ps_y")
    ps_carry = ph.ps("ps_carry")
    link = [ph.pair(ph.sem, f"summed{j}_") for j in range(J)]
    windows, acc_stored = ph.pair(ph.sem, "windows"), ph.pair(ph.sem, "acc_stored")
    carried, head_here, ones_set, started = (ph.sem(n) for n in ("carried", "head_here", "ones_set", "started"))
    input_in, turned, copied, made = (ph.pair(ph.sem, n) for n in ("input_in", "turned", "copied", "made"))
    new_in, new_stored, step_a, step_b = (
        ph.pair(ph.sem, n) for n in ("new_in", "new_stored", "step_a", "step_b"))
    if gcn or gat:
        mixed = ph.pair(ph.sb, "mixed", [P, J, D])
        mix_a, mix_b = ph.pair(ph.sem, "mix_a"), ph.pair(ph.sem, "mix_b")
    if own is not None:
        mine, own_in = ph.pair(ph.sb, "mine", [P, J, D]), ph.pair(ph.sem, "own_in")
    if rest is not None:
        resid, rest_in = ph.pair(ph.sb, "resid", [P, J, D]), ph.pair(ph.sem, "rest_in")
    if sage:
        own_t, ps_o = ph.pair(ph.sb, "own_t", [D + 1, GROUP]), ph.pair(ph.ps, "ps_o")
        unit = Norm(ph, "unit")
    if gat:
        msg, weighted = ph.pair(ph.sb, "msg", [P, J, ATT]), ph.pair(ph.sb, "weighted", [P, J, ATT])
        den = ph.pair(ph.sb, "den", [P, J, HEADS])
        msg_in, weighed, ex_in = (ph.pair(ph.sem, n) for n in ("msg_in", "weighed", "ex_in"))
    if normed:
        norm = Norm(ph, "norm")
        z, c = ph.pair(ph.sb, "z", [P, J, D]), ph.pair(ph.sb, "c", [P, J, D])
        z_in, c_in = ph.pair(ph.sem, "z_in"), ph.pair(ph.sem, "c_in")
    if kind == SAGE2:
        x2, x2t = ph.pair(ph.sb, "x2", [P, J, D]), ph.sb("x2t", [D, GROUP])
        ps_u = ph.ps("ps_u")
        x2_in, x2_turned, x2_copied, x2_made = (
            ph.pair(ph.sem, n) for n in ("x2_in", "x2_turned", "x2_copied", "x2_made"))
    late = 3 if kind == SAGE2 else 2
    l_acc = k.l_acc100 if gat else k.l_acc
    kept = None if keep is None else (x2 if kind == SAGE2 else new)
    kept_in = None if keep is None else (x2_in if kind == SAGE2 else new_in)

    def msgs(step, u):
        return edge_places(step, u)

    with nc.Block() as block:
        @block.sync
        def _(sp):
            sp.sem_inc(ph.entered, 1)

            def load_rows(step, u, through):
                at = cols(step, u, skip=0 if through is None else J * SLOTS)
                if gat:
                    if through:
                        sp.wait_ge(weighed[u], through(1))
                    sp.dma_start(msg[u][:, :, :], k.l_msg[:, at, :]).then_inc(msg_in[u], 16)
                if own is not None:
                    if through:
                        sp.wait_ge((mix_b if gcn else turned)[u], through(1))
                    sp.dma_start(mine[u][:, :, :], own[:, at, :]).then_inc(own_in[u], 16)

            def load_rest(step, u, through):
                if rest is not None:
                    wait(sp, z_in[u], through(1, 1))
                    sp.dma_start(resid[u][:, :, :], rest[:, cols(step, u), :]).then_inc(rest_in[u], 16)

            def store_sums(step, u, through):
                n = msgs(step, u)
                sp.wait_ge(link[n - 1][u], through(1))
                sp.dma_start(l_acc[:, cols(step, u, n), :], acc[u][:, 0:n, 0:C]).then_inc(acc_stored[u], 16)

            def store_new(step, u):
                if keep is not None:
                    sp.wait_ge(kept_in[u], counter(sp, step)(1))
                    sp.dma_start(keep[:, cols(step, u), :], kept[u][:, :, :]).then_inc(new_stored[u], 16)

            def body(step):
                through = counter(sp, step)
                if isinstance(step, int) and step == 0:
                    load_rows(0, 0, None)
                    load_rows(0, 1, None)
                load_rest(step, 0, through)
                store_sums(step, 0, through)
                if not is_last(step):
                    load_rows(step, 0, through)
                if not (isinstance(step, int) and step == 0):
                    store_new(step - 1, 1)
                load_rest(step, 1, through)
                store_sums(step, 1, through)
                if not is_last(step):
                    load_rows(step, 1, through)
                store_new(step, 0)
            steps(sp, STEPS, body)
            store_new(STEPS - 1, 1)
            for u in range(SLOTS):
                if keep is not None:
                    sp.wait_ge(new_stored[u], 16 * STEPS)

        @block.gpsimd
        def _(pool):
            bound = pool.to_reg(N - 1)

            def body(step):
                through = counter(pool, step)
                for u in range(SLOTS):
                    if not gat:
                        put.gather(pool, step, u, through, (link[J - 1][u], through(1, 1)))
                    ago, slot = divmod(late - u + 1, 2)
                    slot = 1 - slot
                    if not isinstance(step, int) or step >= ago:
                        put.scatter(pool, new[slot], slot, counter(pool, step - ago), new_in[slot], bound)
            steps(pool, STEPS, body)
            for u in range(SLOTS):
                pool.wait_ge(acc_stored[u], 16 * STEPS)
            pool.indirect_dma_start(
                out=head_part[:, :], out_offset=None, in_=l_acc.rearrange("p t c -> (p t) c"),
                in_offset=bass.IndirectOffsetOnAxis(ap=k.head_row[:, 0:1], axis=0)).then_inc(head_here, 16)
            for group in range(SLOTS * STEPS - late, SLOTS * STEPS):
                put.scatter(pool, new[group % 2], group % 2, counter(pool, group // 2), new_in[group % 2], bound)
            for u in range(SLOTS):
                pool.wait_ge(put.gone[u], 16 * J * STEPS)

        @block.scalar
        def _(act):
            if not gat:
                put.first_windows(act)

            def flags(step, u):
                through = counter(act, step)
                wait_apart(act, ph.entered, (link[J - 1][u], through(1, 1)))
                if sage:
                    wait_apart(act, ph.entered, (turned[u], through(1, 1)))
                    act.activation(acc[u][:, :, D], k.cnt[:, cols(step, u)], ACT.Copy)
                if gat:
                    n = msgs(step, u)
                    act.activation(weighted[u][:, 0:n, D:ATT], k.att_e[:, cols(step, u, n), :], ACT.Copy)
                act.activation(cont[u][:, :], k.cont[:, cols(step, u)], ACT.Copy).then_inc(windows[u], 1)

            def front(step, u):
                through = counter(act, step)
                if not gat:
                    put.next_window(act, step, u, through)
                if multiplied:
                    rows = D + 1 if sage else D
                    act.wait_ge(turned[u], through(1))
                    wait(act, made[u], through(1, 1))
                    if kind in (GAT1, GAT2):
                        act.activation(xt[u][0:D, :], ps_x[u][0:D, :], ACT.Relu,
                                       bias=k.gat_bias[:, layer:layer + 1]).then_inc(copied[u], 1)
                    elif sage:
                        act.activation(own_t[u][0:D, :], ps_o[u][0:D, :], ACT.Copy)
                        act.activation(xt[u][0:rows, :], ps_x[u][0:rows, :], ACT.Copy).then_inc(copied[u], 1)
                    else:
                        act.activation(xt[u][0:D, :], ps_x[u][0:D, :], ACT.Copy).then_inc(copied[u], 1)

            def back(step, u):
                through = counter(act, step)
                if over_std:
                    unit.take_root(act, u, through, D / (D - 1), 0.0)
                if normed:
                    norm.take_root(act, u, through, 1.0, k.eps[:, :])
                if kind != SAGE2:
                    put.put_window(act, step, u, through)

            def tail(step, u):
                through = counter(act, step)
                act.wait_ge(x2_turned[u], through(1))
                act.activation(x2t[:, :], ps_u[0:D, :], ACT.Copy).then_inc(x2_copied[u], 1)
                put.put_window(act, step, u, through)
            if kind == SAGE2:
                turns(act, (flags, 0), (tail, 2), (front, 0), (back, 1))
            else:
                turns(act, (flags, 0), (front, 0), (back, 1))

        @block.tensor
        def _(pe):
            pe.wait_ge(ones_set, 1)

            def carry(step, u):
                if is_last(step) and u == SLOTS - 1:
                    pe.wait_ge(link[J - 2][u], STEPS)
                    pe.matmul(ps_carry[:, 0:C], k.carry_sel[:, :], acc[u][:, J - 2, 0:C],
                              start=True, stop=True).then_inc(carried, 1)

            def front(step, u):
                through = counter(pe, step)
                carry(step, u)
                if not multiplied:
                    return
                if sage:
                    pe.wait_ge(own_in[u], through(16))
                    wait(pe, copied[u], through(1, 1))
                    for j in range(J):
                        pe.transpose(ps_o[u][0:D, j * P:(j + 1) * P], mine[u][:, j, :], k.ident[:, :])
                    pe.wait_ge(link[J - 1][u], through(1))
                    for j in range(J):
                        ins = pe.transpose(ps_x[u][0:D + 1, j * P:(j + 1) * P], acc[u][:, j, :], k.ident[:, :])
                else:
                    pe.wait_ge(mix_b[u], through(1))
                    wait(pe, copied[u], through(1, 1))
                    for j in range(J):
                        ins = pe.transpose(ps_x[u][0:D, j * P:(j + 1) * P], mixed[u][:, j, :], k.ident[:, :])
                ins.then_inc(turned[u], 1)

            def back(step, u):
                if not multiplied:
                    return
                through = counter(pe, step)
                pe.wait_ge(copied[u], through(1))
                wait(pe, (z_in if normed else new_in)[u], through(1, 1))
                for j in range(J):
                    at = slice(j * P, (j + 1) * P)
                    if gcn:
                        ins = pe.matmul(ps_y[u][:, j * D:(j + 1) * D], xt[u][:, at], k.w_gcn[layer][:, :],
                                        start=True, stop=True)
                    elif sage:
                        pe.matmul(ps_y[u][:, j * D:(j + 1) * D], own_t[u][:, at], k.w_self[layer][:, :],
                                  start=True, stop=False)
                        ins = pe.matmul(ps_y[u][:, j * D:(j + 1) * D], xt[u][:, at], k.w_agg[layer][:, :],
                                        start=False, stop=True)
                    else:
                        ins = pe.matmul(ps_y[u][:, j * ATT_ALL:(j + 1) * ATT_ALL], xt[u][0:D, at],
                                        k.w_att[layer + 1][:, :], start=True, stop=True)
                ins.then_inc(made[u], 1)

            def tail(step, u):
                through = counter(pe, step)
                pe.wait_ge(x2_in[u], through(1))
                wait(pe, *group_before(new_in, u, through))
                for j in range(J):
                    ins = pe.transpose(ps_u[0:D, j * P:(j + 1) * P], x2[u][:, j, :], k.ident[:, :])
                ins.then_inc(x2_turned[u], 1)
                pe.wait_ge(x2_copied[u], through(1))
                for j in range(J):
                    ins = pe.matmul(ps_u[:, j * ATT_ALL:(j + 1) * ATT_ALL], x2t[:, j * P:(j + 1) * P],
                                    k.w_att[0][:, :], start=True, stop=True)
                ins.then_inc(x2_made[u], 1)
            if kind == SAGE2:
                turns(pe, (back, 1), (tail, 2), (front, 0))
            else:
                turns(pe, (back, 1), (front, 0))

        @block.vector
        def _(dve):
            for u in range(SLOTS):
                dve.memset(xt[u][D:D + 1, :], 1.0)
                if sage:
                    dve.memset(own_t[u][D:D + 1, :], 1.0)
            dve.memset(acc[1][:, J - 1, 0:C], 0.0).then_inc(ones_set, 1)
            dve.wait_ge(ones_set, 1)

            def front(step, u):
                through = counter(dve, step)
                n = msgs(step, u)
                if gat:
                    dve.wait_ge(msg_in[u], through(16))
                    dve.tensor_tensor(by_head(weighted[u][:, 0:n, :]), by_head(msg[u][:, 0:n, :]),
                                      k.att_e[:, cols(step, u, n), :].unsqueeze(3).to_broadcast([P, n, HEADS, CH]),
                                      ALU.mult).then_inc(weighed[u], 1)
                    dve.wait_ge(weighed[u], through(1))
                else:
                    dve.wait_ge(put.here[u], put.all_here(step, u, through))
                rows = weighted[u] if gat else put.rows[u]
                dve.wait_ge(windows[u], through(1))
                wait(dve, acc_stored[u], through(16, 1))
                if sage:
                    wait(dve, turned[u], through(1, 1))
                for j in range(n):
                    if j:
                        dve.wait_ge(link[j - 1][u], through(1))
                        before = acc[u][:, j - 1, 0:C]
                    else:
                        wait(dve, link[J - 1][1 - u], through(1, 1) if u == 0 else through(1))
                        before = acc[1 - u][:, J - 1, 0:C]
                    dve.scalar_tensor_tensor(out=acc[u][:, j, 0:C], in0=before, scalar=cont[u][:, j:j + 1],
                                             in1=rows[:, j, :], op0=ALU.mult, op1=ALU.add).then_inc(link[j][u], 1)
                if n < J:
                    dve.wait_ge(carried, 1)
                    dve.wait_ge(head_here, 16)
                    dve.tensor_tensor(acc[u][:, J - 1, 0:C], ps_carry[:, 0:C], head_part[:, :],
                                      ALU.add).then_inc(link[J - 1][u], 1)
                if gcn:
                    dve.wait_ge(link[J - 1][u], through(1))
                    dve.wait_ge(own_in[u], through(16))
                    wait(dve, turned[u], through(1, 1))
                    dve.tensor_tensor(mine[u][:, :, :], acc[u][:, :, :], mine[u][:, :, :], ALU.add).then_inc(step_a[u], 1)
                    dve.wait_ge(step_a[u], through(1))
                    dve.tensor_tensor(mixed[u][:, :, :], mine[u][:, :, :], over_rows(k.dinv[:, cols(step, u)], D),
                                      ALU.mult).then_inc(mix_b[u], 1)
                if gat:
                    dve.wait_ge(link[J - 1][u], through(1))
                    dve.tensor_scalar(den[u][:, :, :], acc[u][:, :, D:ATT], 1e-16, None, ALU.add).then_inc(step_a[u], 1)
                    dve.wait_ge(step_a[u], through(1))
                    dve.reciprocal(den[u][:, :, :], den[u][:, :, :]).then_inc(mix_a[u], 1)
                    dve.wait_ge(mix_a[u], through(1))
                    if multiplied:
                        wait(dve, turned[u], through(1, 1))
                    dve.tensor_tensor(by_head(mixed[u]), by_head(acc[u]), per_head(den[u][:, :, :]),
                                      ALU.mult).then_inc(mix_b[u], 1)

            def back(step, u):
                through = counter(dve, step)
                y = ps_y[u][:, 0:J * D].rearrange("p (j c) -> p j c", c=D)

                def new_free():
                    wait(dve, put.gone[u], through(16 * J, 1))
                    if keep is not None:
                        wait(dve, new_stored[u], through(16, 1))

                if kind == GCN1:
                    dve.wait_ge(made[u], through(1))
                    new_free()
                    dve.scalar_tensor_tensor(out=new[u][:, :, :], in0=y, scalar=0.0,
                                             in1=over_rows(k.dinv[:, cols(step, u)], D),
                                             op0=ALU.max, op1=ALU.mult).then_inc(new_in[u], 1)
                elif kind == GCN2:
                    dve.wait_ge(made[u], through(1))
                    dve.wait_ge(rest_in[u], through(16))
                    dve.scalar_tensor_tensor(out=z[u][:, :, :], in0=y, scalar=0.0, in1=resid[u][:, :, :],
                                             op0=ALU.max, op1=ALU.add).then_inc(z_in[u], 1)
                elif sage:
                    dve.wait_ge(made[u], through(1))
                    unit.spread(dve, u, y, through)
                    unit.invert(dve, u, through)
                    if kind == SAGE1:
                        new_free()
                        dve.tensor_tensor(new[u][:, :, :], y, unit.inverse(u), ALU.mult).then_inc(new_in[u], 1)
                    else:
                        dve.wait_ge(rest_in[u], through(16))
                        dve.tensor_tensor(c[u][:, :, :], y, unit.inverse(u), ALU.mult).then_inc(step_a[u], 1)
                        dve.wait_ge(step_a[u], through(1))
                        dve.tensor_tensor(z[u][:, :, :], c[u][:, :, :], resid[u][:, :, :], ALU.add).then_inc(z_in[u], 1)
                elif kind in (GAT1, GAT2):
                    dve.wait_ge(made[u], through(1))
                    new_free()
                    y = ps_y[u][:, 0:J * ATT_ALL].rearrange("p (j c) -> p j c", c=ATT_ALL)
                    dve.tensor_scalar(k.att_dst[:, cols(step, u), :], y[:, :, ATT:ATT_ALL], 1.0, None, ALU.mult)
                    dve.tensor_copy(new[u][:, :, :], y[:, :, 0:ATT]).then_inc(new_in[u], 1)
                else:
                    dve.wait_ge(mix_b[u], through(1))
                    dve.tensor_tensor(c[u][:, :, :], mixed[u][:, :, :],
                                      k.gat_bias_row[:, :].unsqueeze(1).to_broadcast([P, J, D]),
                                      ALU.add).then_inc(step_b[u], 1)
                    dve.wait_ge(step_b[u], through(1))
                    dve.wait_ge(rest_in[u], through(16))
                    dve.scalar_tensor_tensor(out=z[u][:, :, :], in0=c[u][:, :, :], scalar=0.0, in1=resid[u][:, :, :],
                                             op0=ALU.max, op1=ALU.add).then_inc(z_in[u], 1)
                if normed:
                    dve.wait_ge(z_in[u], through(1))
                    norm.spread(dve, u, z[u], through)
                    dve.wait_ge(norm.var_in[u], through(1))
                    dve.tensor_tensor(c[u][:, :, :], z[u][:, :, :], norm.mean(u), ALU.subtract).then_inc(c_in[u], 1)
                    norm.invert(dve, u, through)
                    dve.wait_ge(c_in[u], through(1))
                    if kind == SAGE2:
                        wait(dve, new_stored[u], through(16, 1))
                        wait(dve, x2_turned[u], through(1, 1))
                        dve.tensor_tensor(x2[u][:, :, :], c[u][:, :, :], norm.inverse(u), ALU.mult).then_inc(x2_in[u], 1)
                    else:
                        new_free()
                        dve.tensor_tensor(new[u][:, :, :], c[u][:, :, :], norm.inverse(u), ALU.mult)\
                            .then_inc(new_in[u], 1)

            def tail(step, u):
                through = counter(dve, step)
                dve.wait_ge(x2_made[u], through(1))
                wait(dve, put.gone[u], through(16 * J, 1))
                y = ps_u[:, 0:J * ATT_ALL].rearrange("p (j c) -> p j c", c=ATT_ALL)
                dve.tensor_scalar(k.att_dst[:, cols(step, u), :], y[:, :, ATT:ATT_ALL], 1.0, None, ALU.mult)
                dve.tensor_copy(new[u][:, :, :], y[:, :, 0:ATT]).then_inc(new_in[u], 1)
            if kind == SAGE2:
                turns(dve, (front, 0), (back, 1), (tail, 2))
            else:
                turns(dve, (front, 0), (back, 1))
    ph.close()


def attention_weights(nc, k, table, layer):
    ph = Phase(nc, f"logits{layer}")
    take = Rows(ph, table, k.src_idx, width=ATT)
    row_stored, logit_in = ph.pair(ph.sem, "row_stored"), ph.pair(ph.sem, "logit_in")
    e, run = k.att_e, ph.sb("run", [P, TH, HEADS])
    peak = ph.sb("peak", [P, 2, HEADS])
    whole = ph.sb("whole", [P, 2, HEADS])
    lone = ph.sb("lone", [P, HEADS])
    reset = ph.sb("reset", [P, T])
    values = ph.sb("values", [P, T])
    wide = ph.sb("wide", [P, 2 * HEADS, P])
    seen = ph.sb("seen", [P, HEADS, P])
    ps_tail, ps_head, ps_sel = ph.ps("ps_tail"), ph.ps("ps_head"), ph.ps("ps_sel")
    link, opened, wide_in, turned, ready, exp_in = (
        ph.sem(n) for n in ("link", "opened", "wide_in", "turned", "ready", "exp_in"))

    with nc.Block() as block:
        @block.sync
        def _(sp):
            sp.sem_inc(ph.entered, 1)

            def body(step):
                through = counter(sp, step)
                for u in range(SLOTS):
                    n = edge_places(step, u)
                    sp.wait_ge(take.here[u], take.all_here(step, u, through))
                    sp.dma_start(k.l_msg[:, cols(step, u, n), :], take.rows[u][:, 0:n, :]).then_inc(row_stored[u], 16)
            steps(sp, STEPS, body)
            for u in range(SLOTS):
                sp.wait_ge(row_stored[u], 16 * STEPS)

        @block.gpsimd
        def _(pool):
            def body(step):
                through = counter(pool, step)
                for u in range(SLOTS):
                    take.gather(pool, step, u, through, (row_stored[u], through(16, 1)), (logit_in[u], through(1, 1)))
            steps(pool, STEPS, body)

        @block.scalar
        def _(act):
            take.first_windows(act)

            def body(step):
                through = counter(act, step)
                for u in range(SLOTS):
                    n = edge_places(step, u)
                    wait_apart(act, ph.entered, (take.here[u], take.all_here(step, u, through)))
                    act.activation(e[:, cols(step, u, n), :], take.rows[u][:, 0:n, D:ATT], ACT.Copy)\
                        .then_inc(logit_in[u], 1)
                    take.next_window(act, step, u, through)
            steps(act, STEPS, body)
            act.wait_ge(ready, 1)
            act.activation(e[:, 0:T, :], e[:, 0:T, :], ACT.Exp).then_inc(exp_in, 1)

        @block.tensor
        def _(pe):
            pe.wait_ge(opened, 1)
            pe.matmul(ps_sel[:, 0:HEADS], k.tail_sel[:, :], k.att_dst[:, T, :], start=True, stop=True)\
                .then_inc(turned, 1)
            pe.wait_ge(wide_in, 1)
            for n in range(2 * HEADS):
                ps = (ps_tail, ps_head)[n // HEADS]
                ins = pe.transpose(ps[:, (n % HEADS) * P:(n % HEADS + 1) * P], wide[:, n, :], k.ident[:, :])
            ins.then_inc(turned, 1)

        @block.vector
        def _(dve):
            done = [0]

            def then(ins):
                done[0] += 1
                ins.then_inc(link, 1)
                dve.wait_ge(link, done[0])

            d = k.att_dst
            then(dve.tensor_copy(reset[:, :], k.cont[:, 0:T]))
            dve.tensor_scalar(reset[:, :], reset[:, :], -1.0, HUGE, ALU.add, ALU.mult).then_inc(opened, 1)
            dve.wait_ge(opened, 1)
            dve.wait_ge(turned, 1)
            then(dve.scalar_tensor_tensor(out=d[:, T - 1, :], in0=d[:, T - 1, :], scalar=k.tail_ended[:, :],
                                          in1=ps_sel[:, 0:HEADS], op0=ALU.mult, op1=ALU.add))
            for h in range(HEADS):
                then(dve.tensor_tensor(values[:, :], d[:, 0:T, h], k.seg_end[:, :], ALU.mult))
                then(dve.tensor_tensor_scan(run[:, 0:T, h][:, ::-1], k.not_end[:, ::-1], values[:, ::-1], 0.0,
                                            ALU.mult, ALU.add))
                then(dve.tensor_tensor(run[:, 0:T, h], run[:, 0:T, h], k.not_head_closed[:, :], ALU.mult))
                then(dve.scalar_tensor_tensor(out=run[:, 0:T, h], in0=k.head_closed[:, :], scalar=d[:, T, h:h + 1],
                                              in1=run[:, 0:T, h], op0=ALU.mult, op1=ALU.add))
            for u in range(SLOTS):
                dve.wait_ge(logit_in[u], STEPS)
            then(dve.tensor_tensor(run[:, 0:T, :], run[:, 0:T, :], e[:, 0:T, :], ALU.add))
            then(dve.scalar_tensor_tensor(out=e[:, 0:T, :], in0=run[:, 0:T, :], scalar=0.2, in1=run[:, 0:T, :],
                                          op0=ALU.mult, op1=ALU.max))
            for h in range(HEADS):
                then(dve.tensor_tensor_scan(run[:, 0:T, h], reset[:, :], e[:, 0:T, h], 0.0, ALU.add, ALU.max))
                then(dve.tensor_copy(peak[:, 0, h:h + 1], run[:, T - 1, h:h + 1]))
                then(dve.tensor_scalar(values[:, :], k.in_head[:, :], -1.0, HUGE, ALU.add, ALU.mult))
                then(dve.tensor_tensor(values[:, :], values[:, :], e[:, 0:T, h], ALU.add))
                then(dve.tensor_reduce(peak[:, 1, h:h + 1], values[:, :], AX.X, ALU.max))
            flat = peak[:, :, :].rearrange("p s h -> p (s h)")
            dve.tensor_copy(wide[:, :, :], flat.unsqueeze(2).to_broadcast([P, 2 * HEADS, P])).then_inc(wide_in, 1)
            dve.wait_ge(turned, 2)
            for mine in range(2):
                for part, ps in enumerate((ps_tail, ps_head)):
                    then(dve.tensor_tensor(seen[:, :, :], ps[:, :].rearrange("p (h q) -> p h q", q=P),
                                           k.apart[:, 2 * mine + part, :].unsqueeze(1).to_broadcast([P, HEADS, P]),
                                           ALU.add))
                    out = whole[:, mine, :] if part == 0 else lone[:, :]
                    then(dve.tensor_reduce(out, seen[:, :, :], AX.X, ALU.max))
                then(dve.tensor_tensor(whole[:, mine, :], whole[:, mine, :], lone[:, :], ALU.max))
            then(dve.tensor_copy(run[:, T - 1, :], whole[:, 0, :]))
            for h in range(HEADS):
                then(dve.tensor_tensor(values[:, :], run[:, 0:T, h], k.seg_end[:, :], ALU.mult))
                then(dve.tensor_tensor_scan(run[:, 0:T, h][:, ::-1], k.not_end[:, ::-1], values[:, ::-1], 0.0,
                                            ALU.mult, ALU.add))
                then(dve.tensor_scalar(values[:, :], k.in_head[:, :], -1.0, -1.0, ALU.add, ALU.mult))
                then(dve.tensor_tensor(run[:, 0:T, h], run[:, 0:T, h], values[:, :], ALU.mult))
                then(dve.scalar_tensor_tensor(out=run[:, 0:T, h], in0=k.in_head[:, :], scalar=whole[:, 1, h:h + 1],
                                              in1=run[:, 0:T, h], op0=ALU.mult, op1=ALU.add))
            dve.tensor_tensor(e[:, 0:T, :], e[:, 0:T, :], run[:, 0:T, :], ALU.subtract).then_inc(ready, 1)
    ph.close()


def rows_from_columns(dve, pe, k, columns, rows, wide, ps, wide_in, turned):
    if dve is not None:
        for n, column in enumerate(columns):
            ins = dve.tensor_copy(wide[:, n, :], column.to_broadcast([D, P]))
        ins.then_inc(wide_in, 1)
        dve.wait_ge(turned, 1)
        for n, row in enumerate(rows):
            dve.tensor_copy(row, ps[:, n * P:n * P + D])
    else:
        pe.wait_ge(wide_in, 1)
        for n in range(len(columns)):
            ins = pe.transpose(ps[:, n * P:n * P + D], wide[:, n, :], k.ident[0:D, 0:D])
        ins.then_inc(turned, 1)


class DenseOutput:

    def __init__(self, ph, k, out):
        self.k, self.out = k, out
        self.x, self.y_scaled, self.z, self.c, self.new = (
            four(ph.sb, n, [P, J, D]) for n in ("x", "y_scaled", "z", "c", "new"))
        self.xt = four(ph.sb, "xt", [D + 1, GROUP])
        self.ps_x, self.ps_y = ph.ps("ps_x"), ph.pair(ph.ps, "ps_y")
        self.norm = Norm(ph, "norm", DENSE_SLOTS)
        self.loaded, self.turned, self.copied, self.made, self.scaled_in, self.shifted, self.z_in, self.c_in, \
            self.new_in, self.stored = (
                four(ph.sem, n) for n in ("loaded", "turned", "copied", "made", "scaled_in", "shifted", "z_in",
                                          "c_in", "new_in", "stored"))
        self.ones_set = ph.sem("ones_set")

    def groups(self, step):
        return [(u, dense_parts(step, u)) for u in range(DENSE_SLOTS)]

    def load(self, sp, step, u, n=P):
        at = u % DENSE_SLOTS
        if u == DENSE_SLOTS - 1:
            wait(sp, self.z_in[u], counter(sp, step)(1, 1))
        sp.dma_start(self.x[at][0:n], dense_rows(self.k.t_x3, step, u, n)).then_inc(self.loaded[at], 16)

    def sync_begin(self, sp, step):
        load_ahead(sp, step, lambda step, u, n: self.load(sp, step, u, n))

    def sync_body(self, sp, step):
        through = counter(sp, step)
        if not is_last(step):
            for u in range(DENSE_SLOTS - 1):
                sp.wait_ge(self.z_in[u], through(1))
                self.load(sp, step, u + DENSE_SLOTS)
        for u, n in self.groups(step):
            sp.wait_ge(self.new_in[u], through(1))
            sp.dma_start(dense_rows(self.out, step, u, n), self.new[u][0:n]).then_inc(self.stored[u], 16)

    def sync_end(self, sp):
        for u in range(DENSE_SLOTS):
            sp.wait_ge(self.stored[u], 16 * STEPS)

    def tensor_front(self, pe, step):
        k, through = self.k, counter(pe, step)

        def turn(u, n):
            pe.wait_ge(self.loaded[u], through(16))
            wait(pe, *group_before(self.copied, u, through))
            for j in range(J):
                ins = pe.transpose(self.ps_x[0:D, j * P:j * P + n], self.x[u][0:n, j, :], k.ident[0:n, 0:n])
            ins.then_inc(self.turned[u], 1)

        def product(u, n):
            pe.wait_ge(self.copied[u], through(1))
            bank_free(pe, self.scaled_in, u, through)
            for j in range(J):
                ins = pe.matmul(self.ps_y[u % 2][0:n, j * D:(j + 1) * D], self.xt[u][:, j * P:j * P + n], k.w_node[:, :],
                                start=True, stop=True)
            ins.then_inc(self.made[u], 1)

        groups = self.groups(step)
        turn(*groups[0])
        for u in range(1, DENSE_SLOTS):
            turn(*groups[u])
            product(*groups[u - 1])
        product(*groups[-1])

    def scalar_front(self, act, step):
        through = counter(act, step)
        for u, n in self.groups(step):
            act.wait_ge(self.turned[u], through(1))
            wait(act, self.made[u], through(1, 1))
            if n == P:
                act.activation(self.xt[u][0:D, :], self.ps_x[0:D, :], ACT.Copy).then_inc(self.copied[u], 1)
            else:
                for j in range(J):
                    ins = act.activation(self.xt[u][0:D, j * P:j * P + n], self.ps_x[0:D, j * P:j * P + n], ACT.Copy)
                ins.then_inc(self.copied[u], 1)

    def scalar_back(self, act, step):
        through = counter(act, step)
        for u, n in self.groups(step):
            self.norm.take_root(act, u, through, 1.0, self.k.eps[0:n, :], n)

    def vector_begin(self, dve):
        for u in range(DENSE_SLOTS):
            ins = dve.memset(self.xt[u][D:D + 1, :], 1.0)
        ins.then_inc(self.ones_set, 1)

    def vector_front(self, dve, step):
        k, through = self.k, counter(dve, step)
        for u, n in self.groups(step):
            dve.wait_ge(self.loaded[u], through(16))
            wait(dve, self.c_in[u], through(1, 1))
            dve.tensor_tensor(self.c[u][0:n], self.x[u][0:n], every_place(k.node_shift, n), ALU.add)\
                .then_inc(self.shifted[u], 1)
            dve.wait_ge(self.made[u], through(1))
            dve.scalar_tensor_tensor(
                out=self.y_scaled[u][0:n], in0=self.ps_y[u % 2][0:n, 0:J * D].rearrange("p (j c) -> p j c", c=D), scalar=0.0,
                in1=every_place(k.node_scale, n), op0=ALU.max, op1=ALU.mult).then_inc(self.scaled_in[u], 1)
        for u, n in self.groups(step):
            dve.wait_ge(self.shifted[u], through(1))
            dve.wait_ge(self.scaled_in[u], through(1))
            dve.tensor_tensor(self.z[u][0:n], self.c[u][0:n], self.y_scaled[u][0:n], ALU.add)\
                .then_inc(self.z_in[u], 1)
        for u, n in self.groups(step):
            dve.wait_ge(self.z_in[u], through(1))
            self.norm.spread(dve, u, self.z[u][0:n], through, n)

    def vector_back(self, dve, step):
        norm, through = self.norm, counter(dve, step)
        for u, n in self.groups(step):
            dve.wait_ge(norm.var_in[u], through(1))
            dve.tensor_tensor(self.c[u][0:n], self.z[u][0:n], norm.mean(u, n), ALU.subtract)\
                .then_inc(self.c_in[u], 1)
        for u, n in self.groups(step):
            norm.invert(dve, u, through, n)
            dve.wait_ge(self.c_in[u], through(1))
            wait(dve, self.stored[u], through(16, 1))
            dve.tensor_tensor(self.new[u][0:n], self.c[u][0:n], norm.inverse(u, n), ALU.mult)\
                .then_inc(self.new_in[u], 1)


def message_round(nc, k, out):
    ph = Phase(nc, "msg")
    src = Rows(ph, k.t_x3, k.src_idx)
    ph.name = "msg_dst"
    dst = Rows(ph, k.t_x3, k.own_idx, head_too=True)
    ph.name = "msg"
    ef = EdgeFeatures(ph, k, 1)
    src_t, dst_t = ph.pair(ph.sb, "src_t", [D, GROUP]), ph.pair(ph.sb, "dst_t", [D, GROUP])
    feat_t = ph.pair(ph.sb, "feat_t", [D + 1, GROUP])
    rows = ph.pair(ph.sb, "rows", [P, J, D])
    acc, cont = ph.pair(ph.sb, "acc", [P, J, D]), ph.pair(ph.sb, "cont", [P, J])
    head_part = ph.sb("head_part", [P, D])
    stat, lone = ph.sb("stat", [D, 2 * STEPS + 1, 6]), ph.sb("lone", [D, TH])
    mv, root, both = ph.sb("mv", [D, 2]), ph.sb("root", [D, 1]), ph.sb("both", [D, 2])
    wide = ph.sb("wide", [D, 2, P])
    ps_s, ps_d, ps_m, ps_z = (ph.ps(n) for n in ("ps_s", "ps_d", "ps_m", "ps_z"))
    ps_c = ps_s
    dense = DenseOutput(ph.part("dense_out"), k, out)
    link = [ph.pair(ph.sem, f"summed{j}_") for j in range(J)]
    (src_turned, dst_turned, src_copied, dst_copied, rows_made, rows_in, across_turned, across_read,
     acc_stored, dst_stored, windows) = (
        ph.pair(ph.sem, n) for n in ("src_turned", "dst_turned", "src_copied", "dst_copied", "rows_made",
                                     "rows_in", "across_turned", "across_read", "acc_stored",
                                     "dst_stored", "windows"))
    carried, head_here, ones_set, bias_in, stat_in, var_in, rooted, chain, wide_in, wide_turned = (
        ph.sem(n) for n in ("carried", "head_here", "ones_set", "bias_in", "stat_in", "var_in", "rooted", "chain",
                            "wide_in", "wide_turned"))

    with nc.Block() as block:
        @block.sync
        def _(sp):
            sp.sem_inc(ph.entered, 1)
            sp.dma_start(k.w_feat[D:D + 1, :], k.msg_bias[0:1, :]).then_inc(bias_in, 16)

            def body(step):
                through = counter(sp, step)
                dense.sync_begin(sp, step)
                for u in range(SLOTS):
                    n = edge_places(step, u)
                    sp.wait_ge(dst.here[u], through(16 * J))
                    sp.dma_start(k.l_xd[:, cols(step, u), :], dst.rows[u][:, :, :]).then_inc(dst_stored[u], 16)
                    if u == 0:
                        if not (isinstance(step, int) and step == 0):
                            store(step - 1, 1)
                    else:
                        store(step, 0)
                dense.sync_body(sp, step)

            def store(step, u):
                n = edge_places(step, u)
                sp.wait_ge(link[n - 1][u], counter(sp, step)(1))
                sp.dma_start(k.l_acc[:, cols(step, u, n), :], acc[u][:, 0:n, :]).then_inc(acc_stored[u], 16)
            steps(sp, STEPS, body)
            dense.sync_end(sp)
            store(STEPS - 1, 1)
            sp.wait_ge(link[J - 1][1], STEPS)
            sp.dma_start(k.l_acc[:, T:TH, :], acc[1][:, J - 1:J, :]).then_inc(acc_stored[1], 16)
            sp.wait_ge(acc_stored[0], 16 * STEPS)
            sp.wait_ge(acc_stored[1], 16 * STEPS + 16)
            for u in range(SLOTS):
                sp.wait_ge(dst_stored[u], 16 * STEPS)

        @block.gpsimd
        def _(pool):
            def body(step):
                through = counter(pool, step)
                for u in range(SLOTS):
                    src.gather(pool, step, u, through, (src_turned[u], through(1, 1)))
                    dst.gather(pool, step, u, through, (dst_turned[u], through(1, 1)), (dst_stored[u], through(16, 1)))
            steps(pool, STEPS, body)
            pool.wait_ge(acc_stored[0], 16 * STEPS)
            pool.wait_ge(acc_stored[1], 16 * STEPS)
            pool.indirect_dma_start(
                out=head_part[:, :], out_offset=None, in_=k.l_acc.rearrange("p t c -> (p t) c"),
                in_offset=bass.IndirectOffsetOnAxis(ap=k.head_row[:, 0:1], axis=0)).then_inc(head_here, 16)

        @block.scalar
        def _(act):
            src.first_windows(act)
            dst.first_windows(act)

            def front(step, u):
                through = counter(act, step)
                n = edge_places(step, u) * P
                wait_apart(act, ph.entered, (link[J - 1][u], through(1, 1)))
                act.activation(cont[u][:, :], k.cont[:, cols(step, u)], ACT.Copy).then_inc(windows[u], 1)
                ef.take(act, step, u, through)
                act.wait_ge(src_turned[u], through(1))
                wait(act, rows_made[u], through(1, 1))
                act.activation(src_t[u][:, 0:n], ps_s[0:D, 0:n], ACT.Copy).then_inc(src_copied[u], 1)
                act.wait_ge(ef.turned[u], through(1))
                wait(act, *group_before(ef.made, u, through))
                act.activation(ef.attr_t[0][:, 0:n], ef.ps_attr[0][0:5, 0:n], ACT.Copy).then_inc(ef.copied[u], 1)
                src.next_window(act, step, u, through)
                dst.next_window(act, step, u, through)

            def back(step, u):
                through = counter(act, step)
                n = edge_places(step, u) * P
                act.wait_ge(ef.made[u], through(1))
                act.activation(feat_t[u][0:D, 0:n], ef.ps_feat[0][0:D, 0:n], ACT.Relu).then_inc(ef.kept[u], 1)
                act.wait_ge(rows_made[u], through(1))
                wait(act, link[J - 1][u], through(1, 1))
                wait(act, across_turned[u], through(1, 1))
                act.activation(rows_of(rows[u][:, :, :])[:, 0:n // P * D], ps_m[:, 0:n // P * D],
                               ACT.Relu).then_inc(rows_in[u], 1)
            turns(act, (back, 1), (front, 0), between=(dense.scalar_front, dense.scalar_back))
            column_scale(None, act, None, None, mv, root[:, :], None, None, (var_in, rooted, chain), k, True)

        @block.tensor
        def _(pe):
            pe.wait_ge(ones_set, 1)
            pe.wait_ge(bias_in, 16)
            pe.wait_ge(dense.ones_set, 1)

            def front(step, u):
                through = counter(pe, step)
                n = edge_places(step, u)
                pe.wait_ge(src.here[u], src.all_here(step, u, through))
                wait(pe, *group_before(src_copied, u, through))
                for j in range(n):
                    ins = pe.transpose(ps_s[0:D, j * P:(j + 1) * P], src.rows[u][:, j, :], k.ident[:, :])
                ins.then_inc(src_turned[u], 1)
                pe.wait_ge(dst.here[u], through(16 * J))
                wait(pe, *group_before(dst_copied, u, through))
                for j in range(n):
                    ins = pe.transpose(ps_d[0:D, j * P:(j + 1) * P], dst.rows[u][:, j, :], k.ident[:, :])
                ins.then_inc(dst_turned[u], 1)
                wait(pe, *group_before(ef.kept, u, through))
                ef.turn(pe, step, u, through)

            def back(step, u):
                through = counter(pe, step)
                n = edge_places(step, u)
                pe.wait_ge(ef.copied[u], through(1))
                pe.matmul(ef.ps_feat[0][0:D, 0:n * P], k.w_edge[:, :], ef.attr_t[0][:, 0:n * P],
                          start=True, stop=True).then_inc(ef.made[u], 1)
                pe.wait_ge(src_copied[u], through(1))
                pe.wait_ge(dst_copied[u], through(1))
                pe.wait_ge(ef.kept[u], through(1))
                wait(pe, *group_before(rows_in, u, through))
                for j in range(n):
                    at = slice(j * P, (j + 1) * P)
                    out = ps_m[:, j * D:(j + 1) * D]
                    pe.matmul(out, src_t[u][:, at], k.w_msg[:, 0, :], start=True, stop=False)
                    pe.matmul(out, dst_t[u][:, at], k.w_msg[:, 1, :], start=False, stop=False)
                    ins = pe.matmul(out, feat_t[u][:, at], k.w_feat[:, :], start=False, stop=True)
                ins.then_inc(rows_made[u], 1)
                if is_last(step) and u == SLOTS - 1:
                    pe.wait_ge(link[J - 2][u], STEPS)
                    pe.matmul(ps_c[:, 0:D], k.carry_sel[:, :], acc[u][:, J - 2, :], start=True, stop=True)\
                        .then_inc(carried, 1)

            def tail(step, u):
                through = counter(pe, step)
                n = edge_places(step, u)
                pe.wait_ge(rows_in[u], through(1))
                wait(pe, *group_before(across_read, u, through))
                for j in range(n):
                    ins = pe.transpose(ps_z[0:D, j * P:(j + 1) * P], rows[u][:, j, :], k.ident[:, :])
                ins.then_inc(across_turned[u], 1)
            turns(pe, (tail, 2), (back, 1), (front, 0), between=(dense.tensor_front, None))
            rows_from_columns(None, pe, k, [None] * 2, None, wide, ps_c, wide_in, wide_turned)

        @block.vector
        def _(dve):
            for u in range(SLOTS):
                dve.memset(feat_t[u][D:D + 1, :], 1.0)
            dve.memset(acc[1][:, J - 1, :], 0.0).then_inc(ones_set, 1)
            dve.wait_ge(ones_set, 1)
            dense.vector_begin(dve)

            def front(step, u):
                through = counter(dve, step)
                n = edge_places(step, u) * P
                dve.wait_ge(dst_turned[u], through(1))
                wait(dve, rows_made[u], through(1, 1))
                dve.tensor_copy(dst_t[u][:, 0:n], ps_d[0:D, 0:n]).then_inc(dst_copied[u], 1)

            def back(step, u):
                through = counter(dve, step)
                n = edge_places(step, u)
                dve.wait_ge(rows_in[u], through(1))
                dve.wait_ge(windows[u], through(1))
                wait(dve, acc_stored[u], through(16, 1))
                for j in range(n):
                    if j:
                        dve.wait_ge(link[j - 1][u], through(1))
                        before = acc[u][:, j - 1, :]
                    else:
                        wait(dve, link[J - 1][1 - u], through(1, 1) if u == 0 else through(1))
                        before = acc[1 - u][:, J - 1, :]
                    dve.scalar_tensor_tensor(out=acc[u][:, j, :], in0=before, scalar=cont[u][:, j:j + 1],
                                             in1=rows[u][:, j, :], op0=ALU.mult, op1=ALU.add).then_inc(link[j][u], 1)
                if n < J:
                    dve.wait_ge(carried, 1)
                    dve.wait_ge(head_here, 16)
                    dve.tensor_tensor(acc[u][:, J - 1, :], ps_c[:, 0:D], head_part[:, :],
                                      ALU.add).then_inc(link[J - 1][u], 1)

            def tail(step, u):
                through = counter(dve, step)
                wait_apart(dve, ph.entered, (across_turned[u], through(1)))
                column_stats(dve, ph, stat, lone, ps_z[0:D, :], step, u).then_inc(across_read[u], 1)
            turns(dve, (front, 0), (back, 1), (tail, 2), between=(dense.vector_front, dense.vector_back))
            dve.wait_ge(across_read[0], STEPS)
            dve.wait_ge(across_read[1], STEPS)
            dve.bn_stats(stat[:, 2 * STEPS, :], lone[:, 0:LAST]).then_inc(stat_in, 1)
            dve.wait_ge(stat_in, 1)
            dve.bn_aggr(mv[:, :], stat[:, :, :].rearrange("c a s -> c (a s)")).then_inc(var_in, 1)
            column_scale(dve, None, k.l3_cols[:, 4:5], k.l3_cols[:, 5:6], mv, root[:, :], both[:, 0:1],
                         both[:, 1:2], (var_in, rooted, chain), k, False)
            rows_from_columns(dve, None, k, [both[:, 0:1], both[:, 1:2]], [k.msg_scale[:, :], k.msg_shift[:, :]],
                              wide, ps_c, wide_in, wide_turned)
    ph.close()


def node_stats(nc, k):
    ph = Phase(nc, "stats")
    x, xt, across = four(ph.sb, "x", [P, J, D]), four(ph.sb, "xt", [D + 1, GROUP]), four(ph.sb, "across", [D, GROUP])
    ps_x, ps_z = ph.pair(ph.ps, "ps_x"), four(ph.ps, "ps_z")
    ps_w = ph.ps("ps_w")
    stat = ph.sb("stat", [D, DENSE_FULL + 1, 6])
    mv, root, both, wide = ph.sb("mv", [D, 2]), ph.sb("root", [D, 1]), ph.sb("both", [D, 2]), ph.sb("wide", [D, 2, P])
    loaded, turned, copied, made, kept, read = (
        four(ph.sem, n) for n in ("loaded", "turned", "copied", "made", "kept", "read"))
    ones_set, var_in, rooted, chain, wide_in, wide_turned = (
        ph.sem(n) for n in ("ones_set", "var_in", "rooted", "chain", "wide_in", "wide_turned"))

    with nc.Block() as block:
        @block.sync
        def _(sp):
            sp.sem_inc(ph.entered, 1)

            def body(step):
                through = counter(sp, step)
                for u in range(DENSE_SLOTS):
                    n = dense_parts(step, u)
                    wait(sp, turned[u], through(1, 1))
                    sp.dma_start(x[u][0:n], dense_rows(k.t_x3, step, u, n)).then_inc(loaded[u], 16)
            steps(sp, STEPS, body)

        @block.tensor
        def _(pe):
            pe.wait_ge(ones_set, 1)

            def body(step):
                through = counter(pe, step)
                for u in range(DENSE_SLOTS):
                    n = dense_parts(step, u)
                    pe.wait_ge(loaded[u], through(16))
                    bank_free(pe, copied, u, through)
                    for j in range(J):
                        ins = pe.transpose(ps_x[u % 2][0:D, j * n:(j + 1) * n], x[u][0:n, j, :], k.ident[0:n, 0:n])
                    ins.then_inc(turned[u], 1)
                for u in range(DENSE_SLOTS):
                    n = dense_parts(step, u) * J
                    pe.wait_ge(copied[u], through(1))
                    wait(pe, kept[u], through(1, 1))
                    pe.matmul(ps_z[u][0:D, 0:n], k.w_node[:, :], xt[u][:, 0:n], start=True, stop=True)\
                        .then_inc(made[u], 1)
            steps(pe, STEPS, body)
            rows_from_columns(None, pe, k, [None] * 2, None, wide, ps_w, wide_in, wide_turned)

        @block.scalar
        def _(act):
            def body(step):
                through = counter(act, step)
                for u in range(DENSE_SLOTS):
                    n = dense_parts(step, u) * J
                    act.wait_ge(turned[u], through(1))
                    wait(act, made[u], through(1, 1))
                    act.activation(xt[u][0:D, 0:n], ps_x[u % 2][0:D, 0:n], ACT.Copy).then_inc(copied[u], 1)
                for u in range(DENSE_SLOTS):
                    n = dense_parts(step, u) * J
                    act.wait_ge(made[u], through(1))
                    wait(act, read[u], through(1, 1))
                    act.activation(across[u][:, 0:n], ps_z[u][0:D, 0:n], ACT.Relu).then_inc(kept[u], 1)
            steps(act, STEPS, body)
            column_scale(None, act, None, None, mv, root[:, :], None, None, (var_in, rooted, chain), k, True)

        @block.vector
        def _(dve):
            for u in range(DENSE_SLOTS):
                ins = dve.memset(xt[u][D:D + 1, :], 1.0)
            ins.then_inc(ones_set, 1)
            def body(step):
                through = counter(dve, step)
                for u in range(DENSE_SLOTS):
                    n = dense_parts(step, u) * J
                    wait_apart(dve, ph.entered, (kept[u], through(1)))
                    dve.bn_stats(stat[:, bass.ds(step * DENSE_SLOTS + u, 1), :].rearrange("c a s -> c (a s)"),
                                 across[u][:, 0:n]).then_inc(read[u], 1)
            steps(dve, STEPS, body)
            for u in range(DENSE_SLOTS):
                dve.wait_ge(read[u], STEPS)
            dve.bn_aggr(mv[:, :], stat[:, :, :].rearrange("c a s -> c (a s)")).then_inc(var_in, 1)
            column_scale(dve, None, k.l3_cols[:, 0:1], k.l3_cols[:, 1:2], mv, root[:, :], both[:, 0:1],
                         both[:, 1:2], (var_in, rooted, chain), k, False)
            rows_from_columns(dve, None, k, [both[:, 0:1], both[:, 1:2]], [k.node_scale[:, :], k.node_shift[:, :]],
                              wide, ps_w, wide_in, wide_turned)
    ph.close()


def output_pass(nc, k, out):
    ph = Phase(nc, "out_edges")
    put = Rows(ph, None, None, out, k.out_idx)
    x, y_scaled, z, c, new = (ph.pair(ph.sb, n, [P, J, D]) for n in ("x", "y_scaled", "z", "c", "new"))
    xt = ph.pair(ph.sb, "xt", [D + 1, GROUP])
    ps_x, ps_y = ph.pair(ph.ps, "ps_x"), ph.pair(ph.ps, "ps_y")
    norm = Norm(ph, "norm")
    loaded, turned, copied, made, scaled_in, shifted, z_in, c_in, new_in = (
        ph.pair(ph.sem, n) for n in ("loaded", "turned", "copied", "made", "scaled_in", "shifted", "z_in", "c_in",
                                     "new_in"))
    ones_set = ph.sem("ones_set")
    sums, sums_in = ph.pair(ph.sb, "sums", [P, J, D]), ph.pair(ph.sem, "sums_in")
    parts = ph.pair(ph.sb, "parts", [P, J, D])
    part_a, part_b, part_c, placed = (ph.pair(ph.sem, n) for n in ("part_a", "part_b", "part_c", "placed"))

    with nc.Block() as block:
        @block.sync
        def _(sp):
            sp.sem_inc(ph.entered, 1)

            def body(step):
                through = counter(sp, step)
                for u in range(SLOTS):
                    wait(sp, z_in[u], through(1, 1))
                    sp.dma_start(sums[u][:, :, :], k.l_acc[:, cols(step, u), :]).then_inc(sums_in[u], 16)
                    sp.dma_start(x[u][:, :, :], k.l_xd[:, cols(step, u), :]).then_inc(loaded[u], 16)
            steps(sp, STEPS, body)

        @block.gpsimd
        def _(pool):
            bound = pool.to_reg(N - 1)

            def body(step):
                through = counter(pool, step)
                for u in range(SLOTS):
                    put.scatter(pool, new[u], u, through, new_in[u], bound)
            steps(pool, STEPS, body)
            for u in range(SLOTS):
                pool.wait_ge(put.gone[u], 16 * J * STEPS)

        @block.tensor
        def _(pe):
            pe.wait_ge(ones_set, 1)

            def body(step):
                through = counter(pe, step)
                for u in range(SLOTS):
                    pe.wait_ge(loaded[u], through(16))
                    wait(pe, copied[u], through(1, 1))
                    for j in range(J):
                        ins = pe.transpose(ps_x[u][0:D, j * P:(j + 1) * P], x[u][:, j, :], k.ident[:, :])
                    ins.then_inc(turned[u], 1)
                for u in range(SLOTS):
                    pe.wait_ge(copied[u], through(1))
                    wait(pe, scaled_in[u], through(1, 1))
                    for j in range(J):
                        ins = pe.matmul(ps_y[u][:, j * D:(j + 1) * D], xt[u][:, j * P:(j + 1) * P], k.w_node[:, :],
                                        start=True, stop=True)
                    ins.then_inc(made[u], 1)
            steps(pe, STEPS, body)

        @block.scalar
        def _(act):
            def body(step):
                through = counter(act, step)
                for u in range(SLOTS):
                    act.wait_ge(turned[u], through(1))
                    wait(act, made[u], through(1, 1))
                    act.activation(xt[u][0:D, :], ps_x[u][0:D, :], ACT.Copy).then_inc(copied[u], 1)
                for u in range(SLOTS):
                    put.put_window(act, step, u, through)
                    norm.take_root(act, u, through, 1.0, k.eps[:, :])
            steps(act, STEPS, body)

        @block.vector
        def _(dve):
            for u in range(SLOTS):
                ins = dve.memset(xt[u][D:D + 1, :], 1.0)
            ins.then_inc(ones_set, 1)
            def body(step):
                through = counter(dve, step)
                for u in range(SLOTS):
                    dve.tensor_tensor(parts[u][:, :, :], over_rows(k.cnt[:, cols(step, u)], D),
                                      every_place(k.msg_shift, P), ALU.mult).then_inc(part_a[u], 1)
                    dve.wait_ge(sums_in[u], through(16))
                    dve.tensor_tensor(sums[u][:, :, :], sums[u][:, :, :], every_place(k.msg_scale, P),
                                      ALU.mult).then_inc(part_b[u], 1)
                    dve.wait_ge(part_a[u], through(1))
                    dve.wait_ge(part_b[u], through(1))
                    dve.tensor_tensor(parts[u][:, :, :], parts[u][:, :, :], sums[u][:, :, :],
                                      ALU.add).then_inc(part_c[u], 1)
                    dve.wait_ge(loaded[u], through(16))
                    wait(dve, c_in[u], through(1, 1))
                    dve.tensor_tensor(c[u][:, :, :], x[u][:, :, :], every_place(k.node_shift, P), ALU.add)\
                        .then_inc(placed[u], 1)
                    dve.wait_ge(made[u], through(1))
                    dve.scalar_tensor_tensor(
                        out=y_scaled[u][:, :, :], in0=ps_y[u][:, 0:J * D].rearrange("p (j c) -> p j c", c=D), scalar=0.0,
                        in1=every_place(k.node_scale, P), op0=ALU.max, op1=ALU.mult).then_inc(scaled_in[u], 1)
                    dve.wait_ge(placed[u], through(1))
                    dve.wait_ge(part_c[u], through(1))
                    dve.tensor_tensor(c[u][:, :, :], c[u][:, :, :], parts[u][:, :, :], ALU.add)\
                        .then_inc(shifted[u], 1)
                for u in range(SLOTS):
                    dve.wait_ge(shifted[u], through(1))
                    dve.wait_ge(scaled_in[u], through(1))
                    dve.tensor_tensor(z[u][:, :, :], c[u][:, :, :], y_scaled[u][:, :, :], ALU.add).then_inc(z_in[u], 1)
                for u in range(SLOTS):
                    dve.wait_ge(z_in[u], through(1))
                    norm.spread(dve, u, z[u][:, :, :], through)
                for u in range(SLOTS):
                    dve.wait_ge(norm.var_in[u], through(1))
                    dve.tensor_tensor(c[u][:, :, :], z[u][:, :, :], norm.mean(u), ALU.subtract).then_inc(c_in[u], 1)
                for u in range(SLOTS):
                    norm.invert(dve, u, through)
                    dve.wait_ge(c_in[u], through(1))
                    wait(dve, put.gone[u], through(16 * J, 1))
                    dve.tensor_tensor(new[u][:, :, :], c[u][:, :, :], norm.inverse(u), ALU.mult).then_inc(new_in[u], 1)
            steps(dve, STEPS, body)
    ph.close()


class Kept:

    def __init__(self, nc, stack):
        def sb(name, shape, dt=F32):
            return stack.enter_context(nc.sbuf_tensor(name, shape, dt))

        def dram(name, shape):
            return nc.dram_tensor(name, shape, F32).ap()

        self.src_idx, self.own_idx, self.out_idx = (sb(n, [P, TH], I32) for n in ("src_idx", "own_idx", "out_idx"))
        self.head_row = sb("head_row", [P, 1], I32)
        self.cont, self.cnt, self.dinv = (sb(n, [P, TH]) for n in ("cont", "cnt", "dinv"))
        self.in_head, self.seg_end, self.not_end, self.head_closed, self.not_head_closed = (
            sb(n, [P, T]) for n in ("in_head", "seg_end", "not_end", "head_closed", "not_head_closed"))
        self.tail_ended, self.eps = sb("tail_ended", [P, 1]), sb("eps", [P, 1])
        self.carry_sel, self.tail_sel, self.ident = (sb(n, [P, P]) for n in ("carry_sel", "tail_sel", "ident"))
        self.apart = sb("apart", [P, 4, P])
        self.att_dst, self.att_e = sb("att_dst", [P, TH, HEADS]), sb("att_e", [P, TH, HEADS])
        self.edge_in = sb("edge_in", [P, TH, 5])
        self.w_gcn = [sb(f"w_gcn{i}", [D + 1, D]) for i in range(2)]
        self.w_self = [sb(f"w_self{i}", [D + 1, D]) for i in range(2)]
        self.w_agg = [sb(f"w_agg{i}", [D + 1, D]) for i in range(2)]
        self.w_att = [sb(f"w_att{i}", [D, ATT_ALL]) for i in range(3)]
        self.gat_bias = sb("gat_bias", [D, 3])
        self.gat_bias_row, self.gat_rest_row = sb("gat_bias_row", [P, D]), sb("gat_rest_row", [P, D])
        self.wide_bias = sb("wide_bias", [D, 2, P])
        self.att_rest = [sb(f"att_rest{i}", [P, J, ATT]) for i in range(2)]
        self.w_node, self.w_edge = sb("w_node", [D + 1, D]), sb("w_edge", [5, D])
        self.w_msg, self.w_feat = sb("w_msg", [D, 3, D]), sb("w_feat", [D + 1, D])
        self.l3_cols, self.edge_scale, self.msg_bias = sb("l3_cols", [D, 8]), sb("edge_scale", [D, 1]), sb("msg_bias", [1, D])
        self.msg_scale, self.msg_shift, self.node_scale, self.node_shift = (
            sb(n, [P, D]) for n in ("msg_scale", "msg_shift", "node_scale", "node_shift"))
        self.t_x, self.t_h1, self.t_x1, self.t_y1, self.t_x3 = (
            dram(n, (N, D)) for n in ("t_x", "t_h1", "t_x1", "t_y1", "t_x3"))
        self.t_att = [dram(f"t_att{i}", (N, ATT)) for i in range(3)]
        self.base_copied = nc.alloc_semaphore("base_copied")
        self.l_x, self.l_s, self.l_h1, self.l_x1, self.l_y1, self.l_x2, self.l_xd, self.l_acc = (
            dram(n, (P, TH, D)) for n in ("l_x", "l_s", "l_h1", "l_x1", "l_y1", "l_x2", "l_xd", "l_acc"))
        self.l_msg, self.l_acc100 = dram("l_msg", (P, TH, ATT)), dram("l_acc100", (P, TH, ATT))


def gnn_resnorm(nc, a, out):
    with ExitStack() as stack:
        k = Kept(nc, stack)
        prepare(nc, a, k)
        own_rows(nc, a, k)
        node_round(nc, a, k, GCN1, k.t_x, k.t_h1, own=k.l_s, keep=k.l_h1, layer=0)
        node_round(nc, a, k, GCN2, k.t_h1, k.t_x1, own=k.l_h1, rest=k.l_x, keep=k.l_x1, layer=1)
        node_round(nc, a, k, SAGE1, k.t_x1, k.t_y1, own=k.l_x1, keep=k.l_y1, layer=0)
        node_round(nc, a, k, SAGE2, k.t_y1, k.t_att[0], own=k.l_y1, rest=k.l_x1, keep=k.l_x2, layer=1)
        attention_weights(nc, k, k.t_att[0], 0)
        node_round(nc, a, k, GAT1, out=k.t_att[1], layer=0)
        attention_weights(nc, k, k.t_att[1], 1)
        node_round(nc, a, k, GAT2, out=k.t_att[2], layer=1)
        attention_weights(nc, k, k.t_att[2], 2)
        node_round(nc, a, k, GAT3, out=k.t_x3, rest=k.l_x2, layer=2)
        node_stats(nc, k)
        message_round(nc, k, out)
        output_pass(nc, k, out)


_INS = ["x", "src", "dst", "edge_attr_4", "L0_gnn_W1", "L0_gnn_b1", "L0_gnn_W2", "L0_gnn_b2", "L1_gnn_W0", "L1_gnn_b0",
        "L1_gnn_W1", "L1_gnn_b1", "L1_gnn_W2", "L1_gnn_b2", "L2_gnn_W", "L2_gnn_att_src", "L2_gnn_att_dst",
        "L2_gnn_bias", "L3_gnn_W_node", "L3_gnn_b_node", "L3_gnn_g_node", "L3_gnn_beta_node", "L3_gnn_W_edge",
        "L3_gnn_b_edge", "L3_gnn_g_edge", "L3_gnn_beta_edge", "L3_gnn_W_msg", "L3_gnn_b_msg", "L3_gnn_g_msg",
        "L3_gnn_beta_msg"]


def kernel(**inputs):
    import concourse.bacc as bacc
    from concourse.bass_utils import run_bass_kernel_spmd as run

    nc = bacc.Bacc("TRN2", target_bir_lowering=False, num_devices=1)
    arrays, args = {}, {}
    for name in _INS:
        array = np.ascontiguousarray(inputs[name])
        arrays[f"in_{name}"] = array
        args[name] = nc.dram_tensor(f"in_{name}", array.shape, mybir.dt.from_np(array.dtype), kind="ExternalInput").ap()
    out = nc.dram_tensor("out_rows", (N, D), F32, kind="ExternalOutput").ap()
    gnn_resnorm(nc, args, out)
    return run(nc, [arrays], core_ids=[0]).results[0]["out_rows"]
```
